# Optimizing a Trainium2 kernel written in Bass

```python
import numpy as np
import jax
import jax.numpy as jnp

def _softmax(x, axis=-1):
    return jax.nn.softmax(x, axis=axis)

def _gelu(x):
    return jax.nn.gelu(x, approximate=True)

def _silu(x):
    return jax.nn.silu(x)

def _sigmoid(x):
    return jax.nn.sigmoid(x)

def _layernorm(x, axis=-1, eps=1e-05):
    m = jnp.mean(x, axis=axis, keepdims=True)
    v = jnp.var(x, axis=axis, keepdims=True)
    return (x - m) / jnp.sqrt(v + eps)

def _scatter_add(tgt, idx, src, axis=0):
    return tgt.at[idx].add(src)

def _segment_sum(src, seg, n):
    return jax.ops.segment_sum(src, seg, n)
kernel_name = 'mk_xattn_ffn_d1_seqx_r8_8c7588'

def setup_inputs(seed: int=0):
    np.random.seed(seed)
    _w = jnp.asarray

    def _rec_inputs():
        import jax
        import jax.numpy as jnp
        _rk = jax.random.key(seed)
        x = -0.0002928 + 1 * jax.random.normal(jax.random.fold_in(_rk, 1), (128, 64, 128), jnp.float32)
        _lenS = 64 - jax.random.randint(jax.random.fold_in(_rk, 7), (128,), 0, max(1, 64 // 4) + 1, jnp.int32)
        _lenS2 = 64 - jax.random.randint(jax.random.fold_in(_rk, 8), (128,), 0, max(1, 64 // 4) + 1, jnp.int32)
        _ctx_1024P = jax.random.normal(jax.random.fold_in(_rk, 11), (128, 16, 128), jnp.float32)
        _ctx_1024c = jax.random.dirichlet(jax.random.fold_in(_rk, 511), 0.3 * jnp.ones((16,), jnp.float32), (128, 64))
        _ctx_1024t = jnp.einsum('bsk,bkd->bsd', _ctx_1024c, _ctx_1024P)
        _ctx_1024t = _ctx_1024t * jax.lax.rsqrt(jnp.mean(jnp.square(_ctx_1024t)) + 1e-12) * 0.953939
        ctx_1024 = -1.39393e-06 + 0.999914 * (_ctx_1024t + 0.3 * jax.random.normal(jax.random.fold_in(_rk, 611), (128, 64, 128), jnp.float32))
        return (x, ctx_1024)
    x, ctx_1024 = _rec_inputs()

    def _L0_xattn_setup():
        import jax, jax.numpy as jnp
        import numpy as np
        D_MODEL = 128
        NUM_HEADS = 16
        HEAD_DIM = D_MODEL // NUM_HEADS
        MAX_REL = 64
        NUM_EMB = 2 * MAX_REL + 1
        B, L = (2, 256)

        def _glorot(key, shape):
            fan_in, fan_out = (shape[0], shape[1])
            lim = jnp.sqrt(6.0 / (fan_in + fan_out))
            return jax.random.uniform(key, shape, jnp.float32, -lim, lim)

        def _split_heads(x):
            b, l, _ = x.shape
            return x.reshape(b, l, NUM_HEADS, HEAD_DIM).transpose(0, 2, 1, 3)
        key = jax.random.key(seed)
        ks = jax.random.split(key, 9)
        return {'query': jax.random.normal(ks[0], (B, L, D_MODEL), jnp.float32), 'key': jax.random.normal(ks[1], (B, L, D_MODEL), jnp.float32), 'value': jax.random.normal(ks[2], (B, L, D_MODEL), jnp.float32), 'wq': _glorot(ks[3], (D_MODEL, D_MODEL)), 'bq': jnp.zeros((D_MODEL,), jnp.float32), 'wk': _glorot(ks[4], (D_MODEL, D_MODEL)), 'bk': jnp.zeros((D_MODEL,), jnp.float32), 'wv': _glorot(ks[5], (D_MODEL, D_MODEL)), 'bv': jnp.zeros((D_MODEL,), jnp.float32), 'wo': _glorot(ks[6], (D_MODEL, D_MODEL)), 'bo': jnp.zeros((D_MODEL,), jnp.float32), 'rel_emb': _glorot(ks[7], (NUM_EMB, HEAD_DIM))}
    _L0_xattn_all = _L0_xattn_setup()
    _L0_xattn_in = {k: v for k, v in _L0_xattn_all.items() if k in ('wq', 'bq', 'wk', 'bk', 'wv', 'bv', 'wo', 'bo', 'rel_emb')}
    del _L0_xattn_all

    def _L0_ffn_setup():
        import jax, jax.numpy as jnp
        import numpy as np
        HIDDEN = 128
        INTER = 512
        N_EXPERTS = 8

        def geglu(x, w1, w2, w3):
            return jax.nn.gelu(x @ w1, approximate=False) * (x @ w2) @ w3
        key = jax.random.key(seed)
        ks = jax.random.split(key, 8)
        s = 0.02
        x = jax.random.normal(ks[0], (2, 256, HIDDEN), dtype=jnp.float32)
        w1s = jax.random.normal(ks[1], (HIDDEN, INTER), dtype=jnp.float32) * s
        w2s = jax.random.normal(ks[2], (HIDDEN, INTER), dtype=jnp.float32) * s
        w3s = jax.random.normal(ks[3], (INTER, HIDDEN), dtype=jnp.float32) * s
        W1 = jax.random.normal(ks[4], (N_EXPERTS, HIDDEN, INTER), dtype=jnp.float32) * s
        W2 = jax.random.normal(ks[5], (N_EXPERTS, HIDDEN, INTER), dtype=jnp.float32) * s
        W3 = jax.random.normal(ks[6], (N_EXPERTS, INTER, HIDDEN), dtype=jnp.float32) * s
        Wg = jax.random.normal(ks[7], (HIDDEN, N_EXPERTS), dtype=jnp.float32) * s
        return {'x': x, 'w1s': w1s, 'w2s': w2s, 'w3s': w3s, 'W1': W1, 'W2': W2, 'W3': W3, 'Wg': Wg}
    _L0_ffn_all = _L0_ffn_setup()
    _L0_ffn_in = {k: v for k, v in _L0_ffn_all.items() if k in ('w1s', 'w2s', 'w3s', 'W1', 'W2', 'W3', 'Wg')}
    del _L0_ffn_all
    return {'x': x, 'ctx_1024': ctx_1024, 'L0_xattn_wq': _L0_xattn_in['wq'], 'L0_xattn_bq': _L0_xattn_in['bq'], 'L0_xattn_wk': _L0_xattn_in['wk'], 'L0_xattn_bk': _L0_xattn_in['bk'], 'L0_xattn_wv': _L0_xattn_in['wv'], 'L0_xattn_bv': _L0_xattn_in['bv'], 'L0_xattn_wo': _L0_xattn_in['wo'], 'L0_xattn_bo': _L0_xattn_in['bo'], 'L0_xattn_rel_emb': _L0_xattn_in['rel_emb'], 'L0_ffn_w1s': _L0_ffn_in['w1s'], 'L0_ffn_w2s': _L0_ffn_in['w2s'], 'L0_ffn_w3s': _L0_ffn_in['w3s'], 'L0_ffn_W1': _L0_ffn_in['W1'], 'L0_ffn_W2': _L0_ffn_in['W2'], 'L0_ffn_W3': _L0_ffn_in['W3'], 'L0_ffn_Wg': _L0_ffn_in['Wg']}

def reference(x, ctx_1024, L0_xattn_wq, L0_xattn_bq, L0_xattn_wk, L0_xattn_bk, L0_xattn_wv, L0_xattn_bv, L0_xattn_wo, L0_xattn_bo, L0_xattn_rel_emb, L0_ffn_w1s, L0_ffn_w2s, L0_ffn_w3s, L0_ffn_W1, L0_ffn_W2, L0_ffn_W3, L0_ffn_Wg):
    import jax
    import jax.numpy as jnp

    def _L0_xattn_ref(query, key, value, wq, bq, wk, bk, wv, bv, wo, bo, rel_emb):
        import jax, jax.numpy as jnp
        import numpy as np
        D_MODEL = 128
        NUM_HEADS = 16
        HEAD_DIM = D_MODEL // NUM_HEADS
        MAX_REL = 64
        NUM_EMB = 2 * MAX_REL + 1
        B, L = (2, 256)

        def _glorot(key, shape):
            fan_in, fan_out = (shape[0], shape[1])
            lim = jnp.sqrt(6.0 / (fan_in + fan_out))
            return jax.random.uniform(key, shape, jnp.float32, -lim, lim)

        def _split_heads(x):
            b, l, _ = x.shape
            return x.reshape(b, l, NUM_HEADS, HEAD_DIM).transpose(0, 2, 1, 3)
        q = _split_heads(query @ wq + bq)
        k = _split_heads(key @ wk + bk)
        v = _split_heads(value @ wv + bv)
        content = jnp.einsum('bhid,bhjd->bhij', q, k)
        idx = jnp.arange(q.shape[2])
        final_mat = jnp.clip(idx[None, :] - idx[:, None], -MAX_REL, MAX_REL) + MAX_REL
        q_rel = jnp.einsum('bhid,rd->bhir', q, rel_emb)
        position = jnp.take_along_axis(q_rel, final_mat[None, None, :, :], axis=-1)
        scores = (content + position) / jnp.sqrt(jnp.float32(HEAD_DIM))
        weights = jax.nn.softmax(scores, axis=-1)
        out = jnp.einsum('bhij,bhjd->bhid', weights, v)
        out = out.transpose(0, 2, 1, 3).reshape(query.shape[0], -1, D_MODEL)
        return out @ wo + bo

    def _L0_ffn_ref(x, w1s, w2s, w3s, W1, W2, W3, Wg):
        import jax, jax.numpy as jnp
        import numpy as np
        HIDDEN = 128
        INTER = 512
        N_EXPERTS = 8

        def geglu(x, w1, w2, w3):
            return jax.nn.gelu(x @ w1, approximate=False) * (x @ w2) @ w3
        B, T, C = x.shape
        xf = x.reshape(-1, C)
        shared = geglu(xf, w1s, w2s, w3s)
        logits = xf @ Wg
        idx = jnp.argmax(logits, axis=-1)
        final = jnp.zeros_like(xf)
        for e in range(N_EXPERTS):
            y = geglu(xf, W1[e], W2[e], W3[e])
            final = final + jnp.where((idx == e)[:, None], y, 0.0)
        return (shared + final).reshape(B, T, C)
    x = x + _L0_xattn_ref(_layernorm(x, axis=-1), ctx_1024, ctx_1024, L0_xattn_wq, L0_xattn_bq, L0_xattn_wk, L0_xattn_bk, L0_xattn_wv, L0_xattn_bv, L0_xattn_wo, L0_xattn_bo, L0_xattn_rel_emb)
    x = x + _L0_ffn_ref(_layernorm(x, axis=-1), L0_ffn_w1s, L0_ffn_w2s, L0_ffn_w3s, L0_ffn_W1, L0_ffn_W2, L0_ffn_W3, L0_ffn_Wg)
    return x

_drawn_inputs = setup_inputs


def setup_inputs(seed=0):
    import zlib

    import numpy as np

    out = dict(_drawn_inputs(seed))
    spreads = {'L0_xattn_bq': (0.0, 0.326),
     'L0_xattn_bk': (0.0, 0.8),
     'L0_xattn_bv': (0.0, 0.1),
     'L0_xattn_bo': (0.0, 0.1)}
    factors = {'L0_xattn_rel_emb': 3.233,
     'L0_ffn_w1s': 5.507,
     'L0_ffn_w2s': 5.4,
     'L0_ffn_w3s': 5.4,
     'L0_ffn_W1': 5.505,
     'L0_ffn_W2': 5.436,
     'L0_ffn_W3': 5.427,
     'L0_ffn_Wg': 5.775}
    for name, (base, spread) in spreads.items():
        noise = np.random.default_rng([zlib.crc32(name.encode()), seed]).standard_normal(out[name].shape)
        drawn = base * np.exp(spread * noise) if base else spread * noise
        out[name] = jnp.asarray(drawn.astype(out[name].dtype))
    for name, factor in factors.items():
        out[name] = (out[name] * factor).astype(out[name].dtype)
    return out
```

```python
from contextlib import ExitStack

import concourse.bass as bass
from concourse import mybir

P = 128
F32 = mybir.dt.float32
I32 = mybir.dt.int32
ALU = mybir.AluOpType
ACT = mybir.ActivationFunctionType
AX = mybir.AxisListType.X

BATCHES, SEQ, DIM = 128, 64, 128
HEADS, HEAD = 16, 8
TOKENS = BATCHES * SEQ
TILES = TOKENS // P
GROUP_TILES = 4
GTOK = GROUP_TILES * P
GB = GTOK // SEQ
GROUPS = TOKENS // GTOK
QUADS, QH = HEADS // 4, 4
MAX_REL = 64
NREL = 2 * MAX_REL
INTER = 512
IC = INTER // P
EXPERTS = 8
RTILE = 256
ROUTED_TILES = TOKENS // RTILE + EXPERTS - 1
EPS = 1e-5
SCALE = float(HEAD) ** -0.5
POS_BANKS = 2 * SEQ // 4


def xattn_moe(nc, x, ctx_1024, wq, bq, wk, bk, wv, bv, wo, bo, rel_emb, w1s, w2s, w3s, W1, W2, W3, Wg, out):
    x_rows = x.rearrange("b s d -> (b s) d").rearrange("(n t p) d -> n p t d", t=GROUP_TILES, p=P)
    ctx_rows = ctx_1024.rearrange("b s d -> (b s) d").rearrange("(n t p) d -> n p t d", t=GROUP_TILES, p=P)
    out_rows = out.rearrange("b s d -> (b s) d").rearrange("(n t p) d -> n p t d", t=GROUP_TILES, p=P)
    q_d = nc.dram_tensor("q_scratch", [DIM, TOKENS], F32).ap()
    k_d = nc.dram_tensor("k_scratch", [DIM, TOKENS], F32).ap()
    v_d = nc.dram_tensor("v_scratch", [TOKENS, DIM], F32).ap()
    attn_d = nc.dram_tensor("attn_scratch", [DIM, TOKENS], F32).ap()
    sorted_x = nc.dram_tensor("sorted_x", [ROUTED_TILES * RTILE, DIM], F32).ap()
    sorted_y = nc.dram_tensor("sorted_y", [ROUTED_TILES * RTILE, DIM], F32).ap()
    v_groups = v_d.rearrange("(n t p) d -> n p t d", t=GROUP_TILES, p=P)
    v_keys = v_d.rearrange("(n b j) c -> n j b c", b=GB, j=SEQ)
    attn_store = attn_d.rearrange("(q c) (n h b i) -> q n b c h i", q=QUADS, h=2, b=4, i=SEQ)
    sorted_x_tiles = sorted_x.rearrange("(k t p) d -> k p t d", t=2, p=P)
    sorted_y_tiles = sorted_y.rearrange("(k t p) d -> k p t d", t=2, p=P)

    with ExitStack() as ctx:
        def sb(name, shape, dt=F32):
            return ctx.enter_context(nc.sbuf_tensor(name, shape, dt))

        def sem(name):
            return ctx.enter_context(nc.semaphore(name))

        ident = sb("ident", [P, P])
        ones = sb("ones", [P, 512])
        lower = sb("lower", [P, P])
        zero_row = sb("zero_row", [P, P])
        head_mask = sb("head_mask", [P, HEADS])
        quad_mask = sb("quad_mask", [P, QH])
        sum_heads = sb("sum_heads", [P, 2, 32])
        rel_rows = sb("rel_rows", [P, HEADS, HEAD])
        rel_t = sb("rel_t", [P, NREL])
        wq_s, wk_s, wv_s, wo_s = (sb(n, [DIM, DIM]) for n in ("wq_s", "wk_s", "wv_s", "wo_s"))
        wg_s = sb("wg_s", [DIM, P])
        bq_s, bk_s = sb("bq_s", [DIM, 1]), sb("bk_s", [DIM, 1])
        bv_s, bo_s = sb("bv_s", [P, DIM]), sb("bo_s", [P, DIM])
        w1s_s, w2s_s = sb("w1s_s", [DIM, INTER]), sb("w2s_s", [DIM, INTER])
        w3s_s = sb("w3s_s", [P, IC, DIM])
        expert_down = sb("expert_down", [P, EXPERTS])
        tile_starts = sb("tile_starts", [P, TOKENS // RTILE])
        tile_numbers = sb("tile_numbers", [P, ROUTED_TILES])

        big = sb("big", [P, 3 * TOKENS])
        pos_t = big[:, 0:2 * TOKENS].rearrange("p (r t) -> p r t", r=2)
        q_pos = big[:, 2 * TOKENS:3 * TOKENS].rearrange("p (i b) -> p i b", i=SEQ)
        acc = big[:, 0:TOKENS]
        xn2 = big[:, TOKENS:2 * TOKENS]
        xn2_t = big[:, 2 * TOKENS:3 * TOKENS]

        work = sb("work", [P, 10240])

        def ring(at, n, size):
            return work[:, at:at + n * size].rearrange("p (s f) -> p s f", s=n)

        x_in, ctx_in, xn = ring(0, 2, GTOK), ring(1024, 2, GTOK), ring(2048, 2, GTOK)
        xn_t, ctx_t = ring(3072, 2, GTOK), ring(4096, 2, GTOK)
        q_out, k_out, v_out = ring(5120, 2, GTOK), ring(6144, 2, GTOK), ring(7168, 2, GTOK)
        k_exp = ring(0, 2, 4 * GTOK)
        prob = ring(4096, 2, 2 * GTOK)
        prob_t = ring(6144, 2, 2 * GTOK)
        ln_stats = sb("ln_stats", [P, GROUP_TILES, 6])
        ln_mv = sb("ln_mv", [P, GROUP_TILES, 2])
        ln_std = sb("ln_std", [P, GROUP_TILES])
        ln_rstd = sb("ln_rstd", [P, GROUP_TILES])

        eps_s = sb("eps_s", [P, 1])
        wait_word = sb("wait_word", [P, 1])
        parity = sb("parity", [P, 2])

        rel_win = sb("rel_win", [P, 2, NREL, 2])
        pos_g = sb("pos_g", [P, 2, 2, GTOK])
        q_g = sb("q_g", [P, 2, GTOK])
        k_g = sb("k_g", [P, 2, GTOK])
        v_g = sb("v_g", [P, 2, GB, 32])
        v_exp = sb("v_exp", [P, 2, GB, 2, 32])
        row_max = sb("row_max", [P, 2, GROUP_TILES * 2, 2])
        den_r = sb("den_r", [P, 2, 2 * SEQ])
        attn_o = sb("attn_o", [P, 2, 2 * SEQ])

        x_in3, xb, xn3 = ring(0, 2, GTOK), ring(1024, 2, GTOK), ring(2048, 2, GTOK)
        attn_in = ring(3072, 2, GTOK)
        xn3_t = ring(4096, 2, GTOK)
        logits = work[:, 5120:5120 + 512].rearrange("p (t e) -> p t e", e=EXPERTS)
        hit = work[:, 5632:6144].rearrange("p (t e) -> p t e", e=EXPERTS)
        chosen = work[:, 6144:6656].rearrange("p (e t) -> p e t", e=EXPERTS)
        seen = work[:, 6656:7168].rearrange("p (e t) -> p e t", e=EXPERTS)
        place = work[:, 7168:7680].rearrange("p (e t) -> p e t", e=EXPERTS)
        starts_hit = work[:, 7680:7936].rearrange("p (e k) -> p e k", e=EXPERTS)
        tiles_hit = work[:, 7936:7936 + ROUTED_TILES * EXPERTS].rearrange("p (k e) -> p k e", e=EXPERTS)
        best = sb("best", [P, TILES])
        rank = sb("rank", [P, TILES])
        count = sb("count", [P, EXPERTS])
        total = sb("total", [P, EXPERTS])
        n_tiles = sb("n_tiles", [P, EXPERTS])
        tiles_end = sb("tiles_end", [P, EXPERTS])
        base = sb("base", [P, EXPERTS])
        row_f = sb("row_f", [P, TILES])
        row_i = sb("row_i", [P, TILES], I32)
        expert_f = sb("expert_f", [P, ROUTED_TILES])
        expert_i = sb("expert_i", [P, ROUTED_TILES], I32)
        gate = ring(0, 2, GTOK)
        hidden_t = ring(1024, 2, IC * GTOK)
        rhidden_t = ring(5120, 3, IC * RTILE)
        rx_t = ring(8192, 3, RTILE)
        rx = sb("rx", [P, 3, RTILE])
        ry = sb("ry", [P, 3, RTILE])
        rw1, rw2, rw3 = (sb(n, [P, 3, INTER]) for n in ("rw1", "rw2", "rw3"))
        y_in = ring(0, 2, GTOK)

        ps = ctx.enter_context(nc.psum_tensor("ps", [P, 8, 512], F32))

        eps_made, sums_made = sem("eps_made"), sem("sums_made")
        consts_made, idents_made = sem("consts_made"), sem("idents_made")
        weights_loaded, zeros_stored = sem("weights_loaded"), sem("zeros_stored")
        rel_transposed, rel_copied = sem("rel_transposed"), sem("rel_copied")
        qkv_weights_loaded = sem("qkv_weights_loaded")
        ctx_loaded = [sem(f"ctx_loaded{s}") for s in range(2)]
        in_loaded = [sem(f"in_loaded{s}") for s in range(2)]
        stats_done, mv_done, std_done, rstd_done, ln_done = (sem(n) for n in (
            "stats_done", "mv_done", "std_done", "rstd_done", "ln_done"))
        in_transposed, xn_t_copied, ctx_t_copied = sem("in_transposed"), sem("xn_t_copied"), sem("ctx_t_copied")
        q_projected, k_projected, v_projected = sem("q_projected"), sem("k_projected"), sem("v_projected")
        q_copied, k_copied, v_copied, q_turned = sem("q_copied"), sem("k_copied"), sem("v_copied"), sem("q_turned")
        qkv_stored = [sem(f"qkv_stored{s}") for s in range(2)]

        window_made, pos_made = sem("window_made"), sem("pos_made")
        pos_copied_act, pos_copied_dve = sem("pos_copied_act"), sem("pos_copied_dve")
        posq_loaded = [sem(f"posq_loaded{s}") for s in range(2)]
        k_loaded = [sem(f"k_loaded{s}") for s in range(2)]
        v_loaded = [sem(f"v_loaded{s}") for s in range(2)]
        k_expanded, k_expanded_act, v_expanded = sem("k_expanded"), sem("k_expanded_act"), sem("v_expanded")
        scored, maxed, shifted, exped = sem("scored"), sem("maxed"), sem("shifted"), sem("exped")
        prob_turned, prob_t_copied = sem("prob_turned"), sem("prob_t_copied")
        attended, den_inverted, normed = sem("attended"), sem("den_inverted"), sem("normed")
        quads_stored = sem("quads_stored")
        attn_stored = [sem(f"attn_stored{s}") for s in range(2)]

        res_loaded = [sem(f"res_loaded{s}") for s in range(2)]
        biased, o_projected, x2_done = sem("biased"), sem("o_projected"), sem("x2_done")
        stats2, mv2, std2, rstd2, ln2 = (sem(n) for n in ("stats2", "mv2", "std2", "rstd2", "ln2"))
        xn3_kept, xn3_turned, xn3_t_copied = sem("xn3_kept"), sem("xn3_turned"), sem("xn3_t_copied")
        logit_made, logit_copied = sem("logit_made"), sem("logit_copied")
        route_step, ranked, routed, scattered = sem("route_step"), sem("ranked"), sem("routed"), sem("scattered")

        up_made, gated, hidden_made = sem("up_made"), sem("gated"), sem("hidden_made")
        down_made, added = sem("down_made"), sem("added")
        tile_loaded = [sem(f"tile_loaded{s}") for s in range(3)]
        rx_turned, rx_t_copied = sem("rx_turned"), sem("rx_t_copied")
        r_up_made, r_gated, r_hidden_made = sem("r_up_made"), sem("r_gated"), sem("r_hidden_made")
        r_down_made, ry_copied = sem("r_down_made"), sem("ry_copied")
        ry_stored = [sem(f"ry_stored{s}") for s in range(3)]
        y_gathered = [sem(f"y_gathered{s}") for s in range(2)]
        summed, out_stored = sem("summed"), sem("out_stored")

        N_QKV_WEIGHTS, N_WEIGHTS = 6, 9
        block = ctx.enter_context(nc.Block())

        def pairs(eng, step, first, last):
            with eng.Fori(0, (last - first) // 2) as m:
                for par in range(2):
                    step(m * 2 + (first + par), (first + par) % 2)

        def triples(eng, step, first, last):
            with eng.Fori(0, (last - first) // 3) as m:
                for par in range(3):
                    step(m * 3 + (first + par), (first + par) % 3)

        def early(n, depth=2):
            return isinstance(n, int) and n < depth

        def round_of(n, slot, depth=2):
            return (n - slot) // depth + 1

        @block.sync
        def _(sp):
            def load_in(n, s):
                if not early(n):
                    sp.wait_ge(ln_done, n - 1)
                sp.dma_start(x_in[:, s, :].rearrange("p (t d) -> p t d", d=DIM), x_rows[n]).then_inc(in_loaded[s], 16)
                if not early(n):
                    sp.wait_ge(in_transposed, n - 1)
                sp.dma_start(ctx_in[:, s, :].rearrange("p (t d) -> p t d", d=DIM), ctx_rows[n]).then_inc(ctx_loaded[s], 16)

            load_in(0, 0)
            for dst, src in ((wq_s[:, :], wq), (wk_s[:, :], wk), (wv_s[:, :], wv),
                             (bq_s[:, :], bq.rearrange("(c a) -> c a", a=1)),
                             (bk_s[:, :], bk.rearrange("(c a) -> c a", a=1)),
                             (bv_s[:, :], bv.rearrange("(a c) -> a c", a=1).to_broadcast([P, DIM])),
                             ):
                sp.dma_start(dst, src).then_inc(qkv_weights_loaded, 16)
            load_in(1, 1)
            for dst, src in ((wo_s[:, :], wo),
                             (bo_s[:, :], bo.rearrange("(a c) -> a c", a=1).to_broadcast([P, DIM])),
                             (w1s_s[:, :], w1s), (w2s_s[:, :], w2s),
                             (w3s_s[:, :, :], w3s.rearrange("(c p) d -> p c d", p=P)),
                             ):
                sp.dma_start(dst, src).then_inc(weights_loaded, 16)
            for h in range(0, HEADS, 4):
                sp.dma_start(rel_rows[:, h:h + 4, :],
                             rel_emb[1:NREL + 1, :].rearrange("r (a d) -> r a d", a=1).to_broadcast([NREL, 4, HEAD]),
                             ).then_inc(weights_loaded, 16)
            pairs(sp, load_in, 2, GROUPS)
            sp.wait_ge(consts_made, 1)
            sp.dma_start(wg_s[:, 0:EXPERTS], Wg).then_inc(zeros_stored, 16)
            sp.dma_start(sorted_x.rearrange("(t p) d -> p t d", p=P),
                         zero_row[:, :].rearrange("p (a d) -> p a d", a=1).to_broadcast([P, 2 * ROUTED_TILES, P]),
                         ).then_inc(zeros_stored, 16)
            for s in range(2):
                sp.wait_ge(qkv_stored[s], 48 * GROUPS // 2)

            with sp.Fori(0, QUADS) as quad:
                def load_k(n, s):
                    if not early(n):
                        sp.wait_ge(k_expanded, quad * GROUPS + n - 1)
                        sp.wait_ge(k_expanded_act, quad * GROUPS + n - 1)
                    sp.dma_start(k_g[:, s, :], k_d[:, bass.ds(n * GTOK, GTOK)]).then_inc(k_loaded[s], 16)

                def load_q(n, s):
                    if not early(n):
                        sp.wait_ge(scored, quad * GROUPS + n - 1)
                    sp.dma_start(q_g[:, s, :], q_d[:, bass.ds(n * GTOK, GTOK)]).then_inc(posq_loaded[s], 16)

                def load_pos(n, s):
                    sp.dma_start(pos_g[:, s, :, :], pos_t[:, :, bass.ds(n * GTOK, GTOK)]).then_inc(posq_loaded[s], 16)

                def load_v(n, s):
                    if not early(n):
                        sp.wait_ge(v_expanded, quad * GROUPS + n - 1)
                    for hp in range(2):
                        sp.dma_start(v_g[hp:P:2, s, :, :],
                                     v_keys[n][:, :, bass.ds(quad * 32, 32)]).then_inc(v_loaded[s], 16)

                def store_attn(n, s):
                    sp.wait_ge(normed, quad * GROUPS + n + 1)
                    for b in range(4):
                        sp.dma_start(attn_store[quad, n, b], attn_o[32 * b:32 * b + 32, s, :].rearrange(
                            "p (h i) -> p h i", h=2)).then_inc(attn_stored[s], 16)

                for n in range(2):
                    load_k(n, n)
                    load_q(n, n)
                    load_v(n, n)
                sp.wait_ge(pos_copied_act, quad * (POS_BANKS // 2) + POS_BANKS // 2)
                sp.wait_ge(pos_copied_dve, quad * (POS_BANKS // 2) + POS_BANKS // 2)
                for n in range(2):
                    load_pos(n, n)

                def load(n, s):
                    load_k(n, s)
                    load_q(n, s)
                    load_pos(n, s)
                    load_v(n, s)
                load(2, 0)
                load(3, 1)

                def step(n, s):
                    load(n, s)
                    store_attn(n - 4, s)
                pairs(sp, step, 4, GROUPS)
                for n in range(GROUPS - 4, GROUPS):
                    store_attn(n, n % 2)
                for s in range(2):
                    sp.wait_ge(attn_stored[s], quad * (32 * GROUPS) + 32 * GROUPS)
                sp.sem_inc(quads_stored, 1)
            sp.wait_ge(quads_stored, QUADS)

            def load_res(n, s):
                if not early(n):
                    sp.wait_ge(x2_done, n - 1)
                sp.dma_start(x_in3[:, s, :].rearrange("p (t d) -> p t d", d=DIM), x_rows[n]).then_inc(res_loaded[s], 16)
                sp.dma_start(attn_in[:, s, :], attn_d[:, bass.ds(n * GTOK, GTOK)]).then_inc(res_loaded[s], 16)
            load_res(0, 0)
            load_res(1, 1)
            pairs(sp, load_res, 2, GROUPS)

            sp.wait_ge(routed, 1)
            sp.wait_ge(scattered, 16 * TILES)

            def load_tile(k, s):
                if not early(k, 3):
                    sp.wait_ge(r_down_made, k - 2)
                sp.dma_start(rx[:, s, :].rearrange("p (t d) -> p t d", d=DIM), sorted_x_tiles[k]).then_inc(tile_loaded[s], 16)
                e = sp.value_load(expert_i[0:1, bass.ds(k, 1)], min_val=0, max_val=EXPERTS - 1)
                sp.dma_start(rw1[:, s, :], W1[e]).then_inc(tile_loaded[s], 16)
                sp.dma_start(rw2[:, s, :], W2[e]).then_inc(tile_loaded[s], 16)
                sp.dma_start(rw3[:, s, :].rearrange("p (c d) -> p c d", d=DIM),
                             W3[e].rearrange("(c p) d -> p c d", p=P)).then_inc(tile_loaded[s], 16)

            def store_tile(k, s):
                sp.wait_ge(ry_copied, k + 1)
                sp.dma_start(sorted_y_tiles[k], ry[:, s, :].rearrange("p (t d) -> p t d", d=DIM)).then_inc(ry_stored[s], 16)

            for k in range(3):
                load_tile(k, k)

            def step(k, s):
                load_tile(k, s)
                store_tile(k - 3, s)
            triples(sp, step, 3, ROUTED_TILES)
            for k in range(ROUTED_TILES - 3, ROUTED_TILES):
                store_tile(k, k % 3)

            with sp.Fori(0, GROUPS) as n:
                sp.wait_ge(summed, n + 1)
                sp.dma_start(out_rows[n], acc[:, bass.ds(n * GTOK, GTOK)].rearrange("p (t d) -> p t d", d=DIM),
                             ).then_inc(out_stored, 16)
            sp.wait_ge(out_stored, 16 * GROUPS)

        @block.gpsimd
        def _(pool):
            pool.memset(wg_s[:, :], 0.0)
            pool.memset(zero_row[:, :], 0.0).then_inc(consts_made, 1)
            pool.memset(ident[:, :], 0.0).then_inc(idents_made, 1)
            pool.memset(ones[:, :], 1.0).then_inc(idents_made, 1)
            pool.memset(sum_heads[:, :, :], 0.0).then_inc(idents_made, 1)
            pool.wait_ge(idents_made, 3)
            pool.affine_select(out=ident[:, :], in_=ident[:, :], compare_op=ALU.not_equal, fill=1.0,
                               base=0, pattern=[[-1, P]], channel_multiplier=1).then_inc(idents_made, 1)
            pool.affine_select(out=lower[:, :], in_=ones[:, 0:P], compare_op=ALU.is_gt, fill=0.0,
                               base=0, pattern=[[1, P]], channel_multiplier=-1).then_inc(idents_made, 1)
            pool.affine_select(out=head_mask[:, :], in_=ones[:, 0:HEADS], compare_op=ALU.is_ge, fill=0.0,
                               base=0, pattern=[[-HEAD, HEADS]], channel_multiplier=1).then_inc(idents_made, 1)
            pool.wait_ge(idents_made, 6)
            pool.affine_select(out=head_mask[:, :], in_=head_mask[:, :], compare_op=ALU.is_ge, fill=0.0,
                               base=HEAD - 1, pattern=[[HEAD, HEADS]], channel_multiplier=-1).then_inc(idents_made, 1)
            pool.iota(expert_down[:, :], pattern=[[-1, EXPERTS]], base=EXPERTS, channel_multiplier=0,
                      allow_small_or_imprecise_dtypes=True).then_inc(idents_made, 1)
            pool.iota(tile_starts[:, :], pattern=[[RTILE, TOKENS // RTILE]], base=0, channel_multiplier=0,
                      allow_small_or_imprecise_dtypes=True).then_inc(idents_made, 1)
            pool.iota(tile_numbers[:, :], pattern=[[1, ROUTED_TILES]], base=0, channel_multiplier=0,
                      allow_small_or_imprecise_dtypes=True).then_inc(idents_made, 1)

            def turn_q(n, s):
                pool.wait_ge(q_copied, n + 1)
                pool.tensor_copy(q_pos[:, :, bass.ds(n * GB, GB)].rearrange("p i b -> p b i"),
                                 q_out[:, s, :].rearrange("p (b i) -> p b i", i=SEQ)).then_inc(q_turned, 1)
            pairs(pool, turn_q, 0, GROUPS)

            pool.wait_ge(sums_made, 5)
            with pool.Fori(0, QUADS) as quad:
                def expand_v(n, s):
                    pool.wait_ge(v_loaded[s], (quad * (GROUPS // 2) + round_of(n, s)) * 32)
                    if not early(n):
                        pool.wait_ge(attended, quad * GROUPS + n - 1)
                    for pair in range(2):
                        last = pool.tensor_tensor(v_exp[:, s, :, pair, :], v_g[:, s, :, :],
                                                  sum_heads[:, pair:pair + 1, :].to_broadcast([P, GB, 32]), ALU.mult)
                    last.then_inc(v_expanded, 1)
                expand_v(0, 0)
                expand_v(1, 1)
                pairs(pool, expand_v, 2, GROUPS)

            def stage3(n, s):
                pool.wait_ge(res_loaded[s], round_of(n, s) * 32)
                if not early(n):
                    pool.wait_ge(x2_done, n - 1)
                for t in range(GROUP_TILES):
                    last = pool.tensor_tensor(xb[:, s, t * DIM:(t + 1) * DIM], x_in3[:, s, t * DIM:(t + 1) * DIM],
                                              bo_s[:, :], ALU.add)
                last.then_inc(biased, 1)

            def keep_xn(n, s):
                pool.wait_ge(ln2, n + 1)
                pool.tensor_copy(xn2[:, bass.ds(n * GTOK, GTOK)], xn3[:, s, :]).then_inc(xn3_kept, 1)
            stage3(0, 0)
            stage3(1, 1)

            def step(n, s):
                keep_xn(n - 2, s)
                stage3(n, s)
            pairs(pool, step, 2, GROUPS)
            keep_xn(GROUPS - 2, 0)
            keep_xn(GROUPS - 1, 1)

            pool.wait_ge(routed, 1)
            pool.wait_ge(zeros_stored, 32)
            pool.wait_ge(xn3_kept, GROUPS)
            for t in range(TILES):
                pool.indirect_dma_start(
                    out=sorted_x, out_offset=bass.IndirectOffsetOnAxis(ap=row_i[:, t:t + 1], axis=0),
                    in_=xn2[:, t * P:(t + 1) * P], in_offset=None).then_inc(scattered, 16)

            for s in range(3):
                pool.wait_ge(ry_stored[s], 16 * (ROUTED_TILES // 3))
            pool.wait_ge(added, GROUPS)
            for n in range(GROUPS):
                s = n % 2
                if n >= 2:
                    pool.wait_ge(summed, n - 1)
                for t in range(GROUP_TILES):
                    tt = n * GROUP_TILES + t
                    pool.indirect_dma_start(
                        out=y_in[:, s, t * DIM:(t + 1) * DIM], out_offset=None, in_=sorted_y,
                        in_offset=bass.IndirectOffsetOnAxis(ap=row_i[:, tt:tt + 1], axis=0)).then_inc(y_gathered[s], 16)

        @block.scalar
        def _(act):
            act.wait_ge(qkv_weights_loaded, 16 * N_QKV_WEIGHTS)

            def deviation(n, var_done, done):
                act.wait_ge(var_done, n + 1)
                act.activation(ln_std[:, :], ln_mv[:, :, 1], ACT.Sqrt, bias=eps_s[:, 0:1]).then_inc(done, 1)

            def copy_in(n, s):
                act.wait_ge(in_transposed, n + 1)
                if not early(n):
                    act.wait_ge(v_projected, n - 1)
                act.activation(xn_t[:, s, :], ps[:, 0, :], ACT.Identity).then_inc(xn_t_copied, 1)
                act.activation(ctx_t[:, s, :], ps[:, 1, :], ACT.Identity).then_inc(ctx_t_copied, 1)

            def project(n, s):
                if not early(n):
                    act.wait_ge(qkv_stored[s], round_of(n, s) * 48 - 48)
                    act.wait_ge(q_turned, n - 1)
                act.wait_ge(q_projected, n + 1)
                act.activation(q_out[:, s, :], ps[:, 2, :], ACT.Identity, bias=bq_s[:, 0:1]).then_inc(q_copied, 1)
                act.wait_ge(k_projected, n + 1)
                act.activation(k_out[:, s, :], ps[:, 3, :], ACT.Identity, bias=bk_s[:, 0:1]).then_inc(k_copied, 1)

            def store_qkv(n, s):
                act.wait_ge(q_copied, n + 1)
                act.dma_start(q_d[:, bass.ds(n * GTOK, GTOK)], q_out[:, s, :]).then_inc(qkv_stored[s], 16)
                act.wait_ge(k_copied, n + 1)
                act.dma_start(k_d[:, bass.ds(n * GTOK, GTOK)], k_out[:, s, :]).then_inc(qkv_stored[s], 16)
                act.wait_ge(v_copied, n + 1)
                act.dma_start(v_groups[n], v_out[:, s, :].rearrange("p (t d) -> p t d", d=DIM)).then_inc(qkv_stored[s], 16)
            act.wait_ge(eps_made, 1)
            deviation(0, mv_done, std_done)
            copy_in(0, 0)
            deviation(1, mv_done, std_done)
            copy_in(1, 1)
            project(0, 0)

            def step(n, s):
                deviation(n, mv_done, std_done)
                store_qkv(n - 2, s)
                copy_in(n, s)
                project(n - 1, 1 - s)
            pairs(act, step, 2, GROUPS)
            store_qkv(GROUPS - 2, 0)
            project(GROUPS - 1, 1)
            store_qkv(GROUPS - 1, 1)

            with act.Fori(0, QUADS) as quad:
                act.wait_ge(window_made, quad + 1)
                for k in range(0, POS_BANKS, 2):
                    act.wait_ge(pos_made, quad * POS_BANKS + (k + 1))
                    i = 4 * (k % (SEQ // 4))
                    act.activation(
                        pos_t[:, k // (SEQ // 4), :].rearrange("p (b i) -> p i b", i=SEQ)[:, i:i + 4, :],
                        ps[:, k % 4, :].rearrange("p (i b) -> p i b", i=4), ACT.Identity).then_inc(pos_copied_act, 1)

                def exp(n, s):
                    act.wait_ge(shifted, quad * GROUPS + n + 1)
                    act.activation(prob[:, s, :], prob[:, s, :], ACT.Exp, scale=SCALE).then_inc(exped, 1)

                def copy_prob_t(n, s):
                    act.wait_ge(prob_turned, quad * GROUPS + n + 1)
                    if not early(n):
                        act.wait_ge(attended, quad * GROUPS + n - 1)
                    act.activation(prob_t[:, s, :].rearrange("p (r t) -> p r t", r=2), ps[:, 4:6, :],
                                   ACT.Identity).then_inc(prob_t_copied, 1)

                def expand_k(n, s):
                    act.wait_ge(k_loaded[s], (quad * (GROUPS // 2) + round_of(n, s)) * 16)
                    if not early(n):
                        act.wait_ge(scored, quad * GROUPS + n - 1)
                    out = k_exp[:, s, :].rearrange("p (b r j h) -> p b r j h", r=2, j=SEQ, h=2)
                    for h in range(2, QH):
                        last = act.activation(out[:, :, h // 2, :, h % 2],
                                              k_g[:, s, :].rearrange("p (b j) -> p b j", j=SEQ), ACT.Identity,
                                              scale=quad_mask[:, h:h + 1])
                    last.then_inc(k_expanded_act, 1)
                expand_k(0, 0)
                expand_k(1, 1)
                exp(0, 0)
                expand_k(2, 0)

                def step(n, s):
                    copy_prob_t(n - 2, s)
                    exp(n - 1, 1 - s)
                    expand_k(n + 1, 1 - s)
                step(2, 0)
                step(3, 1)
                pairs(act, step, 4, GROUPS - 2)
                step(GROUPS - 2, 0)
                for n in (GROUPS - 1, GROUPS):
                    copy_prob_t(n - 2, n % 2)
                    exp(n - 1, (n - 1) % 2)
                copy_prob_t(GROUPS - 1, 1)

            def stage3(n, s):
                act.wait_ge(xn3_turned, n + 1)
                act.activation(xn2_t[:, bass.ds(n * GTOK, GTOK)], ps[:, 2 + s, :], ACT.Identity)
                if not early(n):
                    act.wait_ge(logit_made, n - 1)
                act.activation(xn3_t[:, s, :], ps[:, 2 + s, :], ACT.Identity).then_inc(xn3_t_copied, 1)
            deviation(0, mv2, std2)

            def step(n, s):
                deviation(n + 1, mv2, std2)
                stage3(n, s)
            step(0, 0)
            step(1, 1)
            pairs(act, step, 2, GROUPS - 2)
            step(GROUPS - 2, 0)
            stage3(GROUPS - 1, 1)

            def gelu(n, s):
                for c in range(IC):
                    act.wait_ge(up_made, n * IC + (c + 1))
                    if not (isinstance(n, int) and n == 0 and c < 2):
                        act.wait_ge(hidden_made, n * IC + (c - 1))
                    act.activation(gate[:, c % 2, :], ps[:, c % 2, :], ACT.Gelu).then_inc(gated, 1)
            gelu(0, 0)
            gelu(1, 1)
            pairs(act, gelu, 2, GROUPS)

            def expert(k, s):
                act.wait_ge(rx_turned, k + 1)
                if not early(k, 3):
                    act.wait_ge(r_up_made, (k - 2) * IC)
                act.activation(rx_t[:, s, :], ps[:, 6, 0:RTILE], ACT.Identity).then_inc(rx_t_copied, 1)
                for c in range(IC):
                    act.wait_ge(r_up_made, k * IC + (c + 1))
                    if not (isinstance(k, int) and k == 0 and c < 2):
                        act.wait_ge(r_hidden_made, k * IC + (c - 1))
                    act.activation(gate[:, c % 2, 0:RTILE], ps[:, c % 2, 0:RTILE], ACT.Gelu).then_inc(r_gated, 1)
            for k in range(3):
                expert(k, k)
            triples(act, expert, 3, ROUTED_TILES)

        @block.tensor
        def _(pe):
            pe.wait_ge(qkv_weights_loaded, 16 * N_QKV_WEIGHTS)
            pe.wait_ge(idents_made, 7)

            def turn_in(n, s):
                pe.wait_ge(ln_done, n + 1)
                pe.wait_ge(ctx_loaded[s], round_of(n, s) * 16)
                if not early(n, 1):
                    pe.wait_ge(xn_t_copied, n)
                    pe.wait_ge(ctx_t_copied, n)
                for t in range(GROUP_TILES):
                    pe.transpose(ps[:, 0, t * P:(t + 1) * P], xn[:, s, t * DIM:(t + 1) * DIM], ident[:, :])
                    last = pe.transpose(ps[:, 1, t * P:(t + 1) * P], ctx_in[:, s, t * DIM:(t + 1) * DIM], ident[:, :])
                last.then_inc(in_transposed, 1)

            def project(n, s):
                pe.wait_ge(xn_t_copied, n + 1)
                pe.wait_ge(ctx_t_copied, n + 1)
                if not early(n, 1):
                    pe.wait_ge(q_copied, n)
                    pe.wait_ge(k_copied, n)
                    pe.wait_ge(v_copied, n)
                pe.matmul(ps[:, 2, :], wq_s[:, :], xn_t[:, s, :], start=True, stop=True).then_inc(q_projected, 1)
                pe.matmul(ps[:, 3, :], wk_s[:, :], ctx_t[:, s, :], start=True, stop=True).then_inc(k_projected, 1)
                for t in range(GROUP_TILES):
                    last = pe.matmul(ps[:, 4, t * P:(t + 1) * P], ctx_t[:, s, t * P:(t + 1) * P], wv_s[:, :],
                                     start=True, stop=True)
                last.then_inc(v_projected, 1)

            turn_in(0, 0)

            def step(n, s):
                turn_in(n + 1, 1 - s)
                project(n, s)
            step(0, 0)
            step(1, 1)
            pairs(pe, step, 2, GROUPS - 2)
            step(GROUPS - 2, 0)
            project(GROUPS - 1, 1)
            pe.wait_ge(weights_loaded, 16 * N_WEIGHTS)
            pe.transpose(ps[:, 7, 0:P], rel_rows[:, :, :].rearrange("p h d -> p (h d)"), ident[:, :]).then_inc(rel_transposed, 1)
            pe.wait_ge(q_turned, GROUPS)
            pe.wait_ge(sums_made, 5)
            pe.wait_ge(v_copied, GROUPS)
            pe.wait_ge(k_copied, GROUPS)

            with pe.Fori(0, QUADS) as quad:
                pe.wait_ge(window_made, quad + 1)
                for k in range(POS_BANKS):
                    if k >= 4:
                        copied = pos_copied_act if k % 2 == 0 else pos_copied_dve
                        pe.wait_ge(copied, quad * (POS_BANKS // 2) + ((k - 4) // 2 + 1))
                    pair, i0 = k // (SEQ // 4), 4 * (k % (SEQ // 4))
                    for i in range(i0, i0 + 4):
                        lo = MAX_REL - 1 - i
                        last = pe.matmul(ps[:, k % 4, (i - i0) * P:(i - i0 + 1) * P],
                                         rel_win[:, pair, lo:lo + SEQ, :].rearrange("p j h -> p (j h)"), q_pos[:, i, :],
                                         start=True, stop=True)
                    last.then_inc(pos_made, 1)
                pe.wait_ge(pos_copied_act, quad * (POS_BANKS // 2) + POS_BANKS // 2)
                pe.wait_ge(pos_copied_dve, quad * (POS_BANKS // 2) + POS_BANKS // 2)

                def score(n, s):
                    g = quad * GROUPS + n
                    pe.wait_ge(posq_loaded[s], (quad * (GROUPS // 2) + round_of(n, s)) * 32)
                    pe.wait_ge(k_expanded, g + 1)
                    pe.wait_ge(k_expanded_act, g + 1)
                    if not early(n):
                        pe.wait_ge(shifted, g - 1)
                    for t in range(GROUP_TILES):
                        bank, c = 2 * s + t // 2, 256 * (t % 2)
                        for pair in range(2):
                            pe.matmul(ps[:, bank, c + P * pair:c + P * pair + P], pos_g[:, s, pair, t * P:(t + 1) * P],
                                      ident[:, :], start=(t % 2 == 0 and pair == 0), stop=False, is_transpose=True,
                                      skip_group_check=True)
                        for b in range(2):
                            last = pe.matmul(ps[64 * b:64 * b + 64, bank, c:c + 256],
                                             q_g[:, s, t * P + 64 * b:t * P + 64 * b + 64],
                                             k_exp[:, s, (2 * t + b) * 256:(2 * t + b + 1) * 256],
                                             start=False, stop=True, skip_group_check=True)
                    last.then_inc(scored, 1)

                def turn_prob(n, s):
                    g = quad * GROUPS + n
                    pe.wait_ge(exped, g + 1)
                    if not early(n, 1):
                        pe.wait_ge(prob_t_copied, g)
                    for pair in range(2):
                        for t in range(GROUP_TILES):
                            last = pe.transpose(ps[:, 4 + pair, t * P:(t + 1) * P],
                                                prob[:, s, t * 256 + pair * P:t * 256 + pair * P + P], ident[:, :])
                    last.then_inc(prob_turned, 1)

                def attend(n, s):
                    g = quad * GROUPS + n
                    pe.wait_ge(prob_t_copied, g + 1)
                    pe.wait_ge(v_expanded, g + 1)
                    if not early(n):
                        pe.wait_ge(normed, g - 1)
                    for half in range(2):
                        for pair in range(2):
                            for b4 in range(4):
                                b = 4 * half + b4
                                pe.matmul(ps[32 * b4:32 * b4 + 32, 6 + s, 64 * half:64 * half + 64],
                                          v_exp[:, s, b, pair, :],
                                          prob_t[:, s, pair * GTOK + b * SEQ:pair * GTOK + (b + 1) * SEQ],
                                          start=(pair == 0), stop=(pair == 1), tile_position=(0, 32 * b4))
                    pt = prob_t[:, s, :].rearrange("p (r h b i) -> p r b h i", r=2, h=2, b=4)
                    for pair in range(2):
                        for b4 in range(4):
                            last = pe.matmul(ps[32 * b4:32 * b4 + 32, 6 + s, P:2 * P], sum_heads[:, pair, :],
                                             pt[:, pair, b4], start=(pair == 0), stop=(pair == 1),
                                             tile_position=(0, 32 * b4))
                    last.then_inc(attended, 1)

                score(0, 0)
                score(1, 1)
                turn_prob(0, 0)

                def step(n, s):
                    score(n, s)
                    turn_prob(n - 1, 1 - s)
                    attend(n - 2, s)
                step(2, 0)
                step(3, 1)
                pairs(pe, step, 4, GROUPS)
                turn_prob(GROUPS - 1, 1)
                attend(GROUPS - 2, 0)
                attend(GROUPS - 1, 1)

            pe.wait_ge(normed, QUADS * GROUPS)
            pe.wait_ge(zeros_stored, 32)

            def project_out(n, s):
                pe.wait_ge(res_loaded[s], round_of(n, s) * 32)
                if not early(n):
                    pe.wait_ge(x2_done, n - 1)
                for t in range(GROUP_TILES):
                    last = pe.matmul(ps[:, s, t * DIM:(t + 1) * DIM], attn_in[:, s, t * P:(t + 1) * P], wo_s[:, :],
                                     start=True, stop=True)
                last.then_inc(o_projected, 1)

            def turn_xn(n, s):
                pe.wait_ge(ln2, n + 1)
                if not early(n):
                    pe.wait_ge(xn3_t_copied, n - 1)
                for t in range(GROUP_TILES):
                    last = pe.transpose(ps[:, 2 + s, t * P:(t + 1) * P], xn3[:, s, t * DIM:(t + 1) * DIM], ident[:, :])
                last.then_inc(xn3_turned, 1)

            def make_logits(n, s):
                pe.wait_ge(xn3_t_copied, n + 1)
                if not early(n):
                    pe.wait_ge(logit_copied, n - 1)
                for t in range(GROUP_TILES):
                    last = pe.matmul(ps[:, 4 + s, t * P:(t + 1) * P], xn3_t[:, s, t * P:(t + 1) * P], wg_s[:, :],
                                     start=True, stop=True)
                last.then_inc(logit_made, 1)
            project_out(0, 0)
            project_out(1, 1)
            turn_xn(0, 0)

            def step(n, s):
                project_out(n, s)
                turn_xn(n - 1, 1 - s)
                make_logits(n - 2, s)
            step(2, 0)
            step(3, 1)
            pairs(pe, step, 4, GROUPS)
            turn_xn(GROUPS - 1, 1)
            make_logits(GROUPS - 2, 0)
            make_logits(GROUPS - 1, 1)

            pe.wait_ge(ranked, 1)
            pe.matmul(ps[:, 6, 0:EXPERTS], lower[:, :], count[:, :], start=True, stop=True)
            pe.matmul(ps[:, 7, 0:EXPERTS], ones[:, 0:P], count[:, :], start=True, stop=True).then_inc(ranked, 1)

            pe.wait_ge(logit_copied, GROUPS)

            def up(n):
                for c in range(IC):
                    if not (isinstance(n, int) and n == 0 and c < 2):
                        pe.wait_ge(hidden_made, n * IC + (c - 1))
                    xs = xn2_t[:, bass.ds(n * GTOK, GTOK)]
                    pe.matmul(ps[:, c % 2, :], w1s_s[:, c * P:(c + 1) * P], xs, start=True, stop=True)
                    pe.matmul(ps[:, 2 + c % 2, :], w2s_s[:, c * P:(c + 1) * P], xs, start=True, stop=True).then_inc(up_made, 1)

            def down(n, s):
                pe.wait_ge(hidden_made, n * IC + IC)
                if not early(n):
                    pe.wait_ge(added, n - 1)
                for t in range(GROUP_TILES):
                    for c in range(IC):
                        last = pe.matmul(ps[:, 4 + s, t * DIM:(t + 1) * DIM],
                                         hidden_t[:, s, c * GTOK + t * P:c * GTOK + (t + 1) * P], w3s_s[:, c, :],
                                         start=(c == 0), stop=(c == IC - 1))
                last.then_inc(down_made, 1)
            up(0)

            def step(n, s):
                up(n)
                down(n - 1, 1 - s)
            step(1, 1)
            pairs(pe, step, 2, GROUPS)
            down(GROUPS - 1, 1)

            def turn_tile(k, s):
                pe.wait_ge(tile_loaded[s], round_of(k, s, 3) * 64)
                if not early(k, 1):
                    pe.wait_ge(rx_t_copied, k)
                for t in range(2):
                    last = pe.transpose(ps[:, 6, t * P:(t + 1) * P], rx[:, s, t * DIM:(t + 1) * DIM], ident[:, :])
                last.then_inc(rx_turned, 1)

            def r_up(k, s, cs):
                for c in cs:
                    if c == 0:
                        pe.wait_ge(rx_t_copied, k + 1)
                    if not (isinstance(k, int) and k == 0 and c < 2):
                        pe.wait_ge(r_hidden_made, k * IC + (c - 1))
                    pe.matmul(ps[:, c % 2, 0:RTILE], rw1[:, s, c * P:(c + 1) * P], rx_t[:, s, :], start=True, stop=True)
                    pe.matmul(ps[:, 2 + c % 2, 0:RTILE], rw2[:, s, c * P:(c + 1) * P], rx_t[:, s, :],
                              start=True, stop=True).then_inc(r_up_made, 1)

            def r_down(k, s):
                pe.wait_ge(r_hidden_made, k * IC + IC)
                if not early(k, 1):
                    pe.wait_ge(ry_copied, k)
                for t in range(2):
                    for c in range(IC):
                        last = pe.matmul(ps[:, 4, t * DIM:(t + 1) * DIM],
                                         rhidden_t[:, s, c * RTILE + t * P:c * RTILE + (t + 1) * P],
                                         rw3[:, s, c * DIM:(c + 1) * DIM], start=(c == 0), stop=(c == IC - 1))
                last.then_inc(r_down_made, 1)

            pe.wait_ge(added, GROUPS)
            turn_tile(0, 0)
            r_up(0, 0, range(IC))
            turn_tile(1, 1)

            def step(k, s, last=False):
                r_up(k, s, (0, 1))
                r_down(k - 1, (s - 1) % 3)
                r_up(k, s, (2, 3))
                if not last:
                    turn_tile(k + 1, (s + 1) % 3)
            triples(pe, step, 1, ROUTED_TILES - 2)
            step(ROUTED_TILES - 2, 1)
            step(ROUTED_TILES - 1, 2, last=True)
            r_down(ROUTED_TILES - 1, 2)

        @block.vector
        def _(dve):
            dve.memset(eps_s[:, :], EPS).then_inc(eps_made, 1)
            dve.wait_ge(idents_made, 4)
            for hp in range(2):
                last = dve.tensor_reduce(parity[:, hp:hp + 1], ident[:, hp:P:2], AX, ALU.add)
            last.then_inc(sums_made, 1)
            dve.wait_ge(sums_made, 1)
            for h in range(QH):
                dve.tensor_scalar(sum_heads[:, h // 2, HEAD * h:HEAD * h + HEAD], ones[:, 0:HEAD], parity[:, h % 2:h % 2 + 1],
                                  None, ALU.mult).then_inc(sums_made, 1)
            def layer_norm(n, x_of, out_of, sems, before_write, between=lambda: None):
                stats, mv, std, rstd, done = sems
                dve.memset(wait_word[:, :], 0.0)
                for t in range(GROUP_TILES):
                    last = dve.bn_stats(ln_stats[:, t, :], x_of(t))
                last.then_inc(stats, 1)
                dve.wait_ge(stats, n + 1)
                dve.memset(wait_word[:, :], 0.0)
                for t in range(GROUP_TILES):
                    last = dve.bn_aggr(ln_mv[:, t, :], ln_stats[:, t, :])
                last.then_inc(mv, 1)
                between()
                dve.wait_ge(std, n + 1)
                dve.reciprocal(ln_rstd[:, :], ln_std[:, :]).then_inc(rstd, 1)
                dve.wait_ge(rstd, n + 1)
                before_write()
                for t in range(GROUP_TILES):
                    last = dve.tensor_scalar(out_of(t), x_of(t), ln_mv[:, t, 0:1], ln_rstd[:, t:t + 1],
                                             ALU.subtract, ALU.mult)
                last.then_inc(done, 1)

            def norm_in(n, s, between=lambda: None):
                dve.wait_ge(in_loaded[s], round_of(n, s) * 16)

                def free():
                    if not early(n):
                        dve.wait_ge(in_transposed, n - 1)
                layer_norm(n, lambda t: x_in[:, s, t * DIM:(t + 1) * DIM], lambda t: xn[:, s, t * DIM:(t + 1) * DIM],
                           (stats_done, mv_done, std_done, rstd_done, ln_done), free, between)

            def copy_v(n, s):
                dve.wait_ge(v_projected, n + 1)
                if not early(n):
                    dve.wait_ge(qkv_stored[s], round_of(n, s) * 48 - 48)
                dve.tensor_tensor(v_out[:, s, :].rearrange("p (t d) -> p t d", d=DIM),
                                  ps[:, 4, :].rearrange("p (t d) -> p t d", d=DIM),
                                  bv_s[:, :].rearrange("p (a d) -> p a d", a=1).to_broadcast([P, GROUP_TILES, DIM]),
                                  ALU.add).then_inc(v_copied, 1)
            dve.wait_ge(qkv_weights_loaded, 16 * N_QKV_WEIGHTS)
            norm_in(0, 0)
            norm_in(1, 1)

            def step(n, s):
                norm_in(n, s, between=lambda: copy_v(n - 2, s))
            step(2, 0)
            step(3, 1)
            pairs(dve, step, 4, GROUPS)
            copy_v(GROUPS - 2, 0)
            copy_v(GROUPS - 1, 1)

            dve.wait_ge(rel_transposed, 1)
            dve.tensor_copy(rel_t[:, :], ps[:, 7, 0:NREL]).then_inc(rel_copied, 1)
            dve.wait_ge(rel_copied, 1)

            with dve.Fori(0, QUADS) as quad:
                dve.tensor_copy(quad_mask[:, :], head_mask[:, bass.ds(quad * QH, QH)])
                for h in range(QH):
                    last = dve.tensor_scalar(rel_win[:, h // 2, :, h % 2], rel_t[:, :], head_mask[:, bass.ds(quad * QH + h, 1)],
                                             None, ALU.mult)
                last.then_inc(window_made, 1)
                for k in range(1, POS_BANKS, 2):
                    dve.wait_ge(pos_made, quad * POS_BANKS + (k + 1))
                    i = 4 * (k % (SEQ // 4))
                    dve.tensor_copy(
                        pos_t[:, k // (SEQ // 4), :].rearrange("p (b i) -> p i b", i=SEQ)[:, i:i + 4, :],
                        ps[:, k % 4, :].rearrange("p (i b) -> p i b", i=4)).then_inc(pos_copied_dve, 1)

                def expand_k(n, s):
                    dve.wait_ge(k_loaded[s], (quad * (GROUPS // 2) + round_of(n, s)) * 16)
                    if not early(n):
                        dve.wait_ge(scored, quad * GROUPS + n - 1)
                    out = k_exp[:, s, :].rearrange("p (b r j h) -> p b r j h", r=2, j=SEQ, h=2)
                    for h in range(2):
                        last = dve.tensor_scalar(out[:, :, h // 2, :, h % 2], k_g[:, s, :].rearrange("p (b j) -> p b j", j=SEQ),
                                                 quad_mask[:, h:h + 1], None, ALU.mult)
                    last.then_inc(k_expanded, 1)

                def shift(n, s):
                    g = quad * GROUPS + n
                    scores = ps[:, 2 * s:2 * s + 2, :].rearrange("p k (r j h) -> p (k r) j h", j=SEQ, h=2)
                    dve.wait_ge(scored, g + 1)
                    dve.tensor_reduce(row_max[:, s, :, :], scores.rearrange("p r j h -> p r h j"), AX, ALU.max).then_inc(maxed, 1)
                    dve.wait_ge(maxed, g + 1)
                    if not early(n):
                        dve.wait_ge(prob_turned, g - 1)
                    dve.tensor_tensor(prob[:, s, :].rearrange("p (r j h) -> p r j h", j=SEQ, h=2), scores,
                                      row_max[:, s, :, :].rearrange("p r (a h) -> p r a h", a=1).to_broadcast(
                                          [P, GROUP_TILES * 2, SEQ, 2]), ALU.subtract).then_inc(shifted, 1)

                def norm(n, s):
                    g = quad * GROUPS + n
                    dve.wait_ge(attended, g + 1)
                    dve.reciprocal(den_r[:, s, :], ps[:, 6 + s, P:2 * P]).then_inc(den_inverted, 1)
                    dve.wait_ge(den_inverted, g + 1)
                    if not early(n):
                        dve.wait_ge(attn_stored[s], (quad * (GROUPS // 2) + round_of(n, s)) * 64 - 64)
                    dve.tensor_tensor(attn_o[:, s, :], ps[:, 6 + s, 0:P], den_r[:, s, :], ALU.mult).then_inc(normed, 1)
                expand_k(0, 0)
                expand_k(1, 1)
                shift(0, 0)
                expand_k(2, 0)
                shift(1, 1)

                def step(n, s):
                    expand_k(n, s)
                    shift(n - 1, 1 - s)
                    norm(n - 3, 1 - s)
                step(3, 1)
                pairs(dve, step, 4, GROUPS)
                shift(GROUPS - 1, 1)
                for n in range(GROUPS - 3, GROUPS):
                    norm(n, n % 2)

            def residual(n, s):
                dve.wait_ge(biased, n + 1)
                dve.wait_ge(o_projected, n + 1)
                dve.tensor_tensor(acc[:, bass.ds(n * GTOK, GTOK)], ps[:, s, :], xb[:, s, :], ALU.add).then_inc(x2_done, 1)
                dve.wait_ge(x2_done, n + 1)

                def free():
                    if not early(n):
                        dve.wait_ge(xn3_turned, n - 1)
                        dve.wait_ge(xn3_kept, n - 1)
                layer_norm(n, lambda t: acc[:, bass.ds(n * GTOK + t * DIM, DIM)],
                           lambda t: xn3[:, s, t * DIM:(t + 1) * DIM], (stats2, mv2, std2, rstd2, ln2), free)

            def keep_logits(n, s):
                dve.wait_ge(logit_made, n + 1)
                dve.tensor_copy(logits[:, bass.ds(n * GROUP_TILES, GROUP_TILES), :],
                                ps[:, 4 + s, :].rearrange("p (t e) -> p t e", t=GROUP_TILES)[:, :, 0:EXPERTS],
                                ).then_inc(logit_copied, 1)
            residual(0, 0)
            residual(1, 1)
            residual(2, 0)

            def step(n, s):
                residual(n, s)
                keep_logits(n - 3, 1 - s)
            step(3, 1)
            pairs(dve, step, 4, GROUPS)
            for n in range(GROUPS - 3, GROUPS):
                keep_logits(n, n % 2)

            steps = [0]

            def then(ins):
                steps[0] += 1
                ins.then_inc(route_step, 1)
                dve.wait_ge(route_step, steps[0])

            def over_experts(a):
                return a.rearrange("p (t e) -> p t e", e=1).to_broadcast([P, TILES, EXPERTS])

            dve.wait_ge(logit_copied, GROUPS)
            dve.wait_ge(idents_made, 10)
            then(dve.tensor_reduce(best[:, :], logits, AX, ALU.max))
            then(dve.tensor_tensor(hit, logits, over_experts(best[:, :]), ALU.is_equal))
            down_b = expert_down[:, :].rearrange("p (t e) -> p t e", t=1).to_broadcast([P, TILES, EXPERTS])
            then(dve.tensor_tensor(hit, hit, down_b, ALU.mult))
            then(dve.tensor_reduce(rank[:, :], hit, AX, ALU.max))
            then(dve.tensor_tensor(chosen.rearrange("p e t -> p t e"), down_b, over_experts(rank[:, :]), ALU.is_equal))
            then(dve.tensor_reduce(count[:, :], chosen, AX, ALU.add))
            dve.sem_inc(ranked, 1)
            then(dve.tensor_tensor_scan(seen.rearrange("p e t -> p (e t)"), ones[:, :],
                                        chosen.rearrange("p e t -> p (e t)"), 0.0, ALU.mult, ALU.add))
            dve.wait_ge(ranked, 2)
            then(dve.tensor_copy(total[:, :], ps[:, 7, 0:EXPERTS]))
            then(dve.tensor_tensor(starts_hit, total[:, :].rearrange("p (e k) -> p e k", k=1).to_broadcast(
                [P, EXPERTS, TOKENS // RTILE]), tile_starts[:, :].rearrange("p (e k) -> p e k", e=1).to_broadcast(
                [P, EXPERTS, TOKENS // RTILE]), ALU.is_gt))
            then(dve.tensor_reduce(n_tiles[:, :], starts_hit, AX, ALU.add))
            then(dve.tensor_tensor_scan(tiles_end[:, :], ones[:, 0:EXPERTS], n_tiles[:, :], 0.0, ALU.mult, ALU.add))
            then(dve.tensor_tensor(base[:, :], tiles_end[:, :], n_tiles[:, :], ALU.subtract))
            then(dve.tensor_scalar(base[:, :], base[:, :], float(RTILE), None, ALU.mult))
            then(dve.tensor_tensor(base[:, :], ps[:, 6, 0:EXPERTS], base[:, :], ALU.add))
            then(dve.tensor_tensor(base[:, 1:EXPERTS], base[:, 1:EXPERTS], seen[:, 0:EXPERTS - 1, TILES - 1], ALU.subtract))
            then(dve.scalar_tensor_tensor(out=place, in0=seen, scalar=-1.0,
                                          in1=base[:, :].rearrange("p (e t) -> p e t", t=1).to_broadcast([P, EXPERTS, TILES]),
                                          op0=ALU.add, op1=ALU.add))
            then(dve.tensor_tensor(place, place, chosen, ALU.mult))
            then(dve.tensor_reduce(row_f[:, :], place.rearrange("p e t -> p t e"), AX, ALU.add))
            then(dve.tensor_copy(row_i[:, :], row_f[:, :]))
            then(dve.tensor_tensor(tiles_hit, tiles_end[:, :].rearrange("p (k e) -> p k e", k=1).to_broadcast(
                [P, ROUTED_TILES, EXPERTS]), tile_numbers[:, :].rearrange("p (k e) -> p k e", e=1).to_broadcast(
                [P, ROUTED_TILES, EXPERTS]), ALU.is_le))
            then(dve.tensor_reduce(expert_f[:, :], tiles_hit, AX, ALU.add))
            then(dve.tensor_scalar(expert_f[:, :], expert_f[:, :], float(EXPERTS - 1), None, ALU.min))
            dve.tensor_copy(expert_i[:, :], expert_f[:, :]).then_inc(routed, 1)

            dve.wait_ge(xn3_kept, GROUPS)

            def hidden(n, s):
                for c in range(IC):
                    dve.wait_ge(gated, n * IC + (c + 1))
                    if c == 0 and not early(n):
                        dve.wait_ge(down_made, n - 1)
                    dve.tensor_tensor(hidden_t[:, s, c * GTOK:(c + 1) * GTOK], ps[:, 2 + c % 2, :], gate[:, c % 2, :],
                                      ALU.mult).then_inc(hidden_made, 1)

            def add_shared(n, s):
                dve.wait_ge(down_made, n + 1)
                rows = acc[:, bass.ds(n * GTOK, GTOK)]
                dve.tensor_tensor(rows, ps[:, 4 + s, :], rows, ALU.add).then_inc(added, 1)
            hidden(0, 0)
            hidden(1, 1)
            add_shared(0, 0)

            def step(n, s):
                hidden(n, s)
                add_shared(n - 1, 1 - s)
            pairs(dve, step, 2, GROUPS)
            add_shared(GROUPS - 1, 1)

            def r_hidden(k, s):
                for c in range(IC):
                    dve.wait_ge(r_gated, k * IC + (c + 1))
                    if c == 0 and not early(k, 3):
                        dve.wait_ge(r_down_made, k - 2)
                    dve.tensor_tensor(rhidden_t[:, s, c * RTILE:(c + 1) * RTILE], ps[:, 2 + c % 2, 0:RTILE],
                                      gate[:, c % 2, 0:RTILE], ALU.mult).then_inc(r_hidden_made, 1)

            def copy_y(k, s):
                dve.wait_ge(r_down_made, k + 1)
                if not early(k, 3):
                    dve.wait_ge(ry_stored[s], round_of(k, s, 3) * 16 - 16)
                dve.tensor_copy(ry[:, s, :], ps[:, 4, 0:RTILE]).then_inc(ry_copied, 1)
            r_hidden(0, 0)

            def step(k, s):
                r_hidden(k, s)
                copy_y(k - 1, (s - 1) % 3)
            step(1, 1)
            step(2, 2)
            step(3, 0)
            triples(dve, step, 4, ROUTED_TILES - 2)
            step(ROUTED_TILES - 2, 1)
            step(ROUTED_TILES - 1, 2)
            copy_y(ROUTED_TILES - 1, 2)

            def add_routed(n, s):
                dve.wait_ge(y_gathered[s], round_of(n, s) * (16 * GROUP_TILES))
                rows = acc[:, bass.ds(n * GTOK, GTOK)]
                dve.tensor_tensor(rows, rows, y_in[:, s, :], ALU.add).then_inc(summed, 1)
            pairs(dve, add_routed, 0, GROUPS)


_INS = ['x', 'ctx_1024', 'L0_xattn_wq', 'L0_xattn_bq', 'L0_xattn_wk', 'L0_xattn_bk', 'L0_xattn_wv', 'L0_xattn_bv',
        'L0_xattn_wo', 'L0_xattn_bo', 'L0_xattn_rel_emb', 'L0_ffn_w1s', 'L0_ffn_w2s', 'L0_ffn_w3s', 'L0_ffn_W1',
        'L0_ffn_W2', 'L0_ffn_W3', 'L0_ffn_Wg']
_OUTS = [((BATCHES, SEQ, DIM), 'float32')]


def kernel(**inputs):
    import numpy as _np
    import concourse.bacc as _bacc
    from concourse import mybir as _mybir
    from concourse.bass_utils import run_bass_kernel_spmd as _run

    nc = _bacc.Bacc("TRN2", target_bir_lowering=False, num_devices=1)
    arrays, args = {}, []
    for name in _INS:
        a = _np.ascontiguousarray(inputs[name])
        arrays[f"in_{name}_dram"] = a
        args.append(nc.dram_tensor(f"in_{name}_dram", a.shape, _mybir.dt.from_np(a.dtype), kind="ExternalInput").ap())
    for i, (shape, dtype) in enumerate(_OUTS):
        dt = _mybir.dt.from_np(_np.dtype(dtype))
        args.append(nc.dram_tensor(f"out_{i}_dram", shape, dt, kind="ExternalOutput").ap())
    xattn_moe(nc, *args)
    r = _run(nc, [arrays], core_ids=[0])
    got = tuple(r.results[0][f"out_{i}_dram"] for i in range(len(_OUTS)))
    return got[0]
```

```python
from contextlib import ExitStack

import concourse.bass as bass
from concourse import mybir

P = 128
F32 = mybir.dt.float32
I32 = mybir.dt.int32
ALU = mybir.AluOpType
ACT = mybir.ActivationFunctionType
AX = mybir.AxisListType.X

BATCHES, SEQ, DIM = 128, 64, 128
HEADS, HEAD = 16, 8
TOKENS = BATCHES * SEQ
TILES = TOKENS // P
GROUP_TILES = 4
GTOK = GROUP_TILES * P
GB = GTOK // SEQ
GROUPS = TOKENS // GTOK
QUADS, QH = HEADS // 4, 4
MAX_REL = 64
NREL = 2 * MAX_REL
INTER = 512
IC = INTER // P
EXPERTS = 8
RTILE = 256
ROUTED_TILES = TOKENS // RTILE + EXPERTS - 1
EPS = 1e-5
SCALE = float(HEAD) ** -0.5
POS_BANKS = 2 * SEQ // 4
FRONT = GROUPS // 2


def xattn_moe(nc, x, ctx_1024, wq, bq, wk, bk, wv, bv, wo, bo, rel_emb, w1s, w2s, w3s, W1, W2, W3, Wg, out):
    x_rows = x.rearrange("b s d -> (b s) d").rearrange("(n t p) d -> n p t d", t=GROUP_TILES, p=P)
    ctx_rows = ctx_1024.rearrange("b s d -> (b s) d").rearrange("(n t p) d -> n p t d", t=GROUP_TILES, p=P)
    out_rows = out.rearrange("b s d -> (b s) d").rearrange("(n t p) d -> n p t d", t=GROUP_TILES, p=P)
    k_d = nc.dram_tensor("k_scratch", [DIM, TOKENS], F32).ap()
    v_d = nc.dram_tensor("v_scratch", [TOKENS, DIM], F32).ap()
    attn_d = nc.dram_tensor("attn_scratch", [QUADS, GROUPS, P, 2 * SEQ], F32).ap()
    sorted_x = nc.dram_tensor("sorted_x", [ROUTED_TILES * RTILE, DIM], F32).ap()
    sorted_y = nc.dram_tensor("sorted_y", [ROUTED_TILES * RTILE, DIM], F32).ap()
    v_groups = v_d.rearrange("(n t p) d -> n p t d", t=GROUP_TILES, p=P)
    v_keys = v_d.rearrange("(n b j) c -> n j b c", b=GB, j=SEQ)
    sorted_x_tiles = sorted_x.rearrange("(k t p) d -> k p t d", t=2, p=P)
    sorted_y_tiles = sorted_y.rearrange("(k t p) d -> k p t d", t=2, p=P)

    with ExitStack() as ctx:
        def sb(name, shape, dt=F32):
            return ctx.enter_context(nc.sbuf_tensor(name, shape, dt))

        def sem(name):
            return ctx.enter_context(nc.semaphore(name))

        ident = sb("ident", [P, P])
        ones = sb("ones", [P, 512])
        lower = sb("lower", [P, P])
        zero_row = sb("zero_row", [P, P])
        head_mask = sb("head_mask", [P, HEADS])
        quad_mask = sb("quad_mask", [P, QH])
        sum_heads = sb("sum_heads", [P, 2, 32])
        rel_rows = sb("rel_rows", [P, HEADS, HEAD])
        rel_t = sb("rel_t", [P, NREL])
        wq_s, wk_s, wv_s, wo_s = (sb(n, [DIM, DIM]) for n in ("wq_s", "wk_s", "wv_s", "wo_s"))
        wg_s = sb("wg_s", [DIM, P])
        bq_s, bk_s = sb("bq_s", [DIM, 1]), sb("bk_s", [DIM, 1])
        bv_s, bo_s = sb("bv_s", [P, DIM]), sb("bo_s", [P, DIM])
        w1s_s, w2s_s = sb("w1s_s", [DIM, INTER]), sb("w2s_s", [DIM, INTER])
        w3s_s = sb("w3s_s", [P, IC, DIM])
        expert_down = sb("expert_down", [P, EXPERTS])
        tile_starts = sb("tile_starts", [P, TOKENS // RTILE])
        tile_numbers = sb("tile_numbers", [P, ROUTED_TILES])

        big = sb("big", [P, 3 * TOKENS])
        pos_t = big[:, 0:2 * TOKENS].rearrange("p (r t) -> p r t", r=2)
        q_pos = big[:, 2 * TOKENS:3 * TOKENS].rearrange("p (i b) -> p i b", i=SEQ)
        acc = big[:, 0:TOKENS]
        xn2 = big[:, TOKENS:2 * TOKENS]
        xn2_t = big[:, 2 * TOKENS:3 * TOKENS]

        work = sb("work", [P, 10240])

        def ring(at, n, size):
            return work[:, at:at + n * size].rearrange("p (s f) -> p s f", s=n)

        x_in, ctx_in, xn = ring(0, 4, GTOK), ring(2048, 4, GTOK), ring(4096, 2, GTOK)
        xn_t, ctx_t = ring(5120, 2, GTOK), ring(6144, 2, GTOK)
        q_out, k_out, v_out = ring(7168, 2, GTOK), ring(8192, 2, GTOK), ring(9216, 2, GTOK)
        k_exp = ring(0, 2, 4 * GTOK)
        prob = ring(4096, 2, 2 * GTOK)
        prob_t = ring(6144, 2, 2 * GTOK)
        ln_stats = sb("ln_stats", [P, 4, GROUP_TILES, 6])
        ln_mv = sb("ln_mv", [P, 4, GROUP_TILES, 2])
        ln_std = sb("ln_std", [P, 4, GROUP_TILES])
        ln_rstd = sb("ln_rstd", [P, 4, GROUP_TILES])

        eps_s = sb("eps_s", [P, 1])
        wait_word = sb("wait_word", [P, 2])
        parity = sb("parity", [P, 2])

        rel_win = sb("rel_win", [P, 2, NREL, 2])
        pos_g = sb("pos_g", [P, 2, 2, GTOK])
        q_g = sb("q_g", [P, 2, GTOK])
        k_g = sb("k_g", [P, 2, GTOK])
        v_g = sb("v_g", [P, 2, GB, 32])
        v_exp = sb("v_exp", [P, 2, GB, 2, 32])
        row_max = sb("row_max", [P, 2, GROUP_TILES * 2, 2])
        den_r = sb("den_r", [P, 2, 2 * SEQ])
        attn_o = sb("attn_o", [P, 2, 2 * SEQ])

        x_in3, attn_in = ring(0, 4, GTOK), ring(2048, 4, GTOK)
        xn3_t = ring(4096, 2, GTOK)
        logits = work[:, 5120:5120 + 512].rearrange("p (t e) -> p t e", e=EXPERTS)
        hit = work[:, 5632:6144].rearrange("p (t e) -> p t e", e=EXPERTS)
        chosen = work[:, 6144:6656].rearrange("p (e t) -> p e t", e=EXPERTS)
        seen = work[:, 6656:7168].rearrange("p (e t) -> p e t", e=EXPERTS)
        place = work[:, 7168:7680].rearrange("p (e t) -> p e t", e=EXPERTS)
        starts_hit = work[:, 7680:7936].rearrange("p (e k) -> p e k", e=EXPERTS)
        tiles_hit = work[:, 7936:7936 + ROUTED_TILES * EXPERTS].rearrange("p (k e) -> p k e", e=EXPERTS)
        best = sb("best", [P, TILES])
        rank = sb("rank", [P, TILES])
        count = sb("count", [P, EXPERTS])
        total = sb("total", [P, EXPERTS])
        n_tiles = sb("n_tiles", [P, EXPERTS])
        tiles_end = sb("tiles_end", [P, EXPERTS])
        base = sb("base", [P, EXPERTS])
        row_f = sb("row_f", [P, TILES])
        row_i = sb("row_i", [P, TILES], I32)
        expert_f = sb("expert_f", [P, ROUTED_TILES])
        expert_i = sb("expert_i", [P, ROUTED_TILES], I32)
        gate = ring(0, 2, GTOK)
        hidden_t = ring(1024, 2, IC * GTOK)
        rhidden_t = ring(5120, 3, IC * RTILE)
        rx_t = ring(8192, 3, RTILE)
        rx = sb("rx", [P, 3, RTILE])
        ry = sb("ry", [P, 3, RTILE])
        rw1, rw2, rw3 = (sb(n, [P, 3, INTER]) for n in ("rw1", "rw2", "rw3"))
        xb, xn3 = rw2[:, 0:2, :], rw1[:, 0:2, :]
        y_in = ring(8960, 2, GTOK)

        ps = ctx.enter_context(nc.psum_tensor("ps", [P, 8, 512], F32))

        eps_made, sums_made = sem("eps_made"), sem("sums_made")
        consts_made, idents_made = sem("consts_made"), sem("idents_made")
        weights_loaded, zeros_stored = sem("weights_loaded"), sem("zeros_stored")
        rel_transposed, rel_copied = sem("rel_transposed"), sem("rel_copied")
        qkv_weights_loaded = sem("qkv_weights_loaded")
        ctx_loaded = [sem(f"ctx_loaded{s}") for s in range(4)]
        in_loaded = [sem(f"in_loaded{s}") for s in range(4)]
        stats_done, mv_done, std_done, rstd_done, ln_done = (sem(n) for n in (
            "stats_done", "mv_done", "std_done", "rstd_done", "ln_done"))
        in_transposed, xn_t_copied, ctx_t_copied = sem("in_transposed"), sem("xn_t_copied"), sem("ctx_t_copied")
        q_projected, k_projected, v_projected = sem("q_projected"), sem("k_projected"), sem("v_projected")
        q_copied, k_copied, v_copied, q_turned = sem("q_copied"), sem("k_copied"), sem("v_copied"), sem("q_turned")
        kv_stored = [sem(f"kv_stored{s}") for s in range(2)]

        window_made, pos_made = sem("window_made"), sem("pos_made")
        pos_copied_act, pos_copied_dve = sem("pos_copied_act"), sem("pos_copied_dve")
        pos_loaded = [sem(f"pos_loaded{s}") for s in range(2)]
        q_picked = sem("q_picked")
        k_loaded = [sem(f"k_loaded{s}") for s in range(2)]
        v_loaded = [sem(f"v_loaded{s}") for s in range(2)]
        k_expanded, k_expanded_act, v_expanded = sem("k_expanded"), sem("k_expanded_act"), sem("v_expanded")
        scored, maxed, shifted, exped = sem("scored"), sem("maxed"), sem("shifted"), sem("exped")
        prob_turned, prob_t_copied = sem("prob_turned"), sem("prob_t_copied")
        attended, den_inverted, normed = sem("attended"), sem("den_inverted"), sem("normed")
        attn_stored = [sem(f"attn_stored{s}") for s in range(2)]

        res_loaded = [sem(f"res_loaded{s}") for s in range(4)]
        biased, o_projected, x2_done = sem("biased"), sem("o_projected"), sem("x2_done")
        stats2, mv2, std2, rstd2, ln2 = (sem(n) for n in ("stats2", "mv2", "std2", "rstd2", "ln2"))
        xn3_kept, xn3_turned, xn3_t_copied = sem("xn3_kept"), sem("xn3_turned"), sem("xn3_t_copied")
        logit_made, logit_copied = sem("logit_made"), sem("logit_copied")
        route_step, ranked, routed, scattered = sem("route_step"), sem("ranked"), sem("routed"), sem("scattered")

        up_made, gated, hidden_made = sem("up_made"), sem("gated"), sem("hidden_made")
        down_made, added = sem("down_made"), sem("added")
        rx_loaded, up_loaded, down_loaded = ([sem(f"{n}{s}") for s in range(3)] for n in (
            "rx_loaded", "up_loaded", "down_loaded"))
        rx_turned, rx_t_copied = sem("rx_turned"), sem("rx_t_copied")
        r_up_made, r_gated, r_hidden_made = sem("r_up_made"), sem("r_gated"), sem("r_hidden_made")
        r_down_made, ry_copied = sem("r_down_made"), sem("ry_copied")
        ry_stored = [sem(f"ry_stored{s}") for s in range(3)]
        y_gathered = [sem(f"y_gathered{s}") for s in range(2)]
        summed, out_stored = sem("summed"), sem("out_stored")

        N_QKV_WEIGHTS, N_WEIGHTS = 6, 9
        block = ctx.enter_context(nc.Block())

        def pairs(eng, step, first, last):
            with eng.Fori(0, (last - first) // 2) as m:
                for par in range(2):
                    step(m * 2 + (first + par), (first + par) % 2)

        def triples(eng, step, first, last):
            with eng.Fori(0, (last - first) // 3) as m:
                for par in range(3):
                    step(m * 3 + (first + par), (first + par) % 3)

        def fours(eng, step, first, last):
            with eng.Fori(0, (last - first) // 4) as m:
                for par in range(4):
                    step(m * 4 + (first + par), (first + par) % 4)

        def early(n, depth=2):
            return isinstance(n, int) and n < depth

        def first_use(quad, n):
            return isinstance(quad, int) and early(n)

        def quads(eng, body):
            body(0)
            with eng.Fori(0, QUADS - 1) as m:
                body(m + 1)

        def round_of(n, slot, depth=2):
            return (n - slot) // depth + 1

        @block.sync
        def _(sp):
            def load_in(n, s):
                if not early(n, 4):
                    sp.wait_ge(ln_done, n - 3)
                sp.dma_start(x_in[:, s, :].rearrange("p (t d) -> p t d", d=DIM), x_rows[n]).then_inc(in_loaded[s], 16)
                if not early(n, 4):
                    sp.wait_ge(in_transposed, n - 3)
                sp.dma_start(ctx_in[:, s, :].rearrange("p (t d) -> p t d", d=DIM), ctx_rows[n]).then_inc(ctx_loaded[s], 16)

            load_in(0, 0)
            for dst, src in ((wq_s[:, :], wq), (wk_s[:, :], wk), (wv_s[:, :], wv),
                             (bq_s[:, :], bq.rearrange("(c a) -> c a", a=1)),
                             (bk_s[:, :], bk.rearrange("(c a) -> c a", a=1)),
                             (bv_s[:, :], bv.rearrange("(a c) -> a c", a=1).to_broadcast([P, DIM])),
                             ):
                sp.dma_start(dst, src).then_inc(qkv_weights_loaded, 16)
            for n in range(1, 4):
                load_in(n, n)
            for dst, src in ((wo_s[:, :], wo),
                             (bo_s[:, :], bo.rearrange("(a c) -> a c", a=1).to_broadcast([P, DIM])),
                             (w1s_s[:, :], w1s), (w2s_s[:, :], w2s),
                             (w3s_s[:, :, :], w3s.rearrange("(c p) d -> p c d", p=P)),
                             ):
                sp.dma_start(dst, src).then_inc(weights_loaded, 16)
            for h in range(0, HEADS, 4):
                sp.dma_start(rel_rows[:, h:h + 4, :],
                             rel_emb[1:NREL + 1, :].rearrange("r (a d) -> r a d", a=1).to_broadcast([NREL, 4, HEAD]),
                             ).then_inc(weights_loaded, 16)
            fours(sp, load_in, 4, GROUPS)
            sp.wait_ge(consts_made, 1)
            sp.dma_start(wg_s[:, 0:EXPERTS], Wg).then_inc(zeros_stored, 16)
            sp.dma_start(sorted_x.rearrange("(t p) d -> p t d", p=P),
                         zero_row[:, :].rearrange("p (a d) -> p a d", a=1).to_broadcast([P, 2 * ROUTED_TILES, P]),
                         ).then_inc(zeros_stored, 16)
            for s in range(2):
                sp.wait_ge(kv_stored[s], 32 * GROUPS // 2)

            def load_k(quad, n, s):
                if not first_use(quad, n):
                    sp.wait_ge(k_expanded, quad * GROUPS + n - 1)
                    sp.wait_ge(k_expanded_act, quad * GROUPS + n - 1)
                sp.dma_start(k_g[:, s, :], k_d[:, bass.ds(n * GTOK, GTOK)]).then_inc(k_loaded[s], 16)

            def load_pos(n, s):
                sp.dma_start(pos_g[:, s, :, :], pos_t[:, :, bass.ds(n * GTOK, GTOK)]).then_inc(pos_loaded[s], 16)

            def load_v(quad, n, s):
                if not first_use(quad, n):
                    sp.wait_ge(v_expanded, quad * GROUPS + n - 1)
                for hp in range(2):
                    sp.dma_start(v_g[hp:P:2, s, :, :],
                                 v_keys[n][:, :, bass.ds(quad * 32, 32)]).then_inc(v_loaded[s], 16)

            def store_attn(quad, n, s):
                sp.wait_ge(normed, quad * GROUPS + n + 1)
                sp.dma_start(attn_d[quad, n], attn_o[:, s, :]).then_inc(attn_stored[s], 16)

            def attend_quad(quad):
                follows = not isinstance(quad, int)
                for n in range(2):
                    load_k(quad, n, n)
                    load_v(quad, n, n)
                    if follows:
                        store_attn(quad - 1, GROUPS - 4 + n, n)
                sp.wait_ge(pos_copied_act, quad * (POS_BANKS // 2) + POS_BANKS // 2)
                sp.wait_ge(pos_copied_dve, quad * (POS_BANKS // 2) + POS_BANKS // 2)
                for n in range(2):
                    load_pos(n, n)
                for n in (2, 3):
                    sp.wait_ge(scored, quad * GROUPS + n - 1)
                    load_k(quad, n, n - 2)
                    if follows:
                        store_attn(quad - 1, GROUPS - 4 + n, n - 2)
                    load_pos(n, n - 2)
                    load_v(quad, n, n - 2)

                def step(n, s):
                    sp.wait_ge(scored, quad * GROUPS + n - 1)
                    load_k(quad, n, s)
                    load_pos(n, s)
                    load_v(quad, n, s)
                    store_attn(quad, n - 4, s)
                pairs(sp, step, 4, GROUPS)
            quads(sp, attend_quad)
            for n in range(GROUPS - 4, GROUPS):
                store_attn(QUADS - 1, n, n % 2)
            for s in range(2):
                sp.wait_ge(attn_stored[s], QUADS * (16 * GROUPS // 2))

            def load_res(n, s):
                if not early(n, 4):
                    sp.wait_ge(x2_done, n - 3)
                sp.dma_start(x_in3[:, s, :].rearrange("p (t d) -> p t d", d=DIM), x_rows[n]).then_inc(res_loaded[s], 16)
                for quad in range(QUADS):
                    sp.dma_start(attn_in[32 * quad:32 * quad + 32, s, :].rearrange("c (b t) -> c b t", b=4),
                                 attn_d[quad, n].rearrange("(b c) t -> c b t", b=4)).then_inc(res_loaded[s], 16)
            for n in range(4):
                load_res(n, n)
            fours(sp, load_res, 4, GROUPS)

            sp.wait_ge(routed, 1)
            sp.wait_ge(scattered, 16 * TILES)

            def load_tile(k, s):
                if not early(k, 3):
                    sp.wait_ge(r_up_made, (k - 2) * IC)
                sp.dma_start(rx[:, s, :].rearrange("p (t d) -> p t d", d=DIM), sorted_x_tiles[k]).then_inc(rx_loaded[s], 16)
                e = sp.value_load(expert_i[0:1, bass.ds(k, 1)], min_val=0, max_val=EXPERTS - 1)
                sp.dma_start(rw1[:, s, :], W1[e]).then_inc(up_loaded[s], 16)
                sp.dma_start(rw2[:, s, :], W2[e]).then_inc(up_loaded[s], 16)
                if not early(k, 3):
                    sp.wait_ge(r_down_made, k - 2)
                sp.dma_start(rw3[:, s, :].rearrange("p (c d) -> p c d", d=DIM),
                             W3[e].rearrange("(c p) d -> p c d", p=P)).then_inc(down_loaded[s], 16)

            def store_tile(k, s):
                sp.wait_ge(ry_copied, k + 1)
                sp.dma_start(sorted_y_tiles[k], ry[:, s, :].rearrange("p (t d) -> p t d", d=DIM)).then_inc(ry_stored[s], 16)

            for k in range(3):
                load_tile(k, k)

            def step(k, s):
                load_tile(k, s)
                store_tile(k - 3, s)
            triples(sp, step, 3, ROUTED_TILES)
            for k in range(ROUTED_TILES - 3, ROUTED_TILES):
                store_tile(k, k % 3)

            with sp.Fori(0, GROUPS) as n:
                sp.wait_ge(summed, n + 1)
                sp.dma_start(out_rows[n], acc[:, bass.ds(n * GTOK, GTOK)].rearrange("p (t d) -> p t d", d=DIM),
                             ).then_inc(out_stored, 16)
            sp.wait_ge(out_stored, 16 * GROUPS)

        @block.gpsimd
        def _(pool):
            pool.memset(wg_s[:, :], 0.0)
            pool.memset(zero_row[:, :], 0.0).then_inc(consts_made, 1)
            pool.memset(ident[:, :], 0.0).then_inc(idents_made, 1)
            pool.memset(ones[:, :], 1.0).then_inc(idents_made, 1)
            pool.memset(sum_heads[:, :, :], 0.0).then_inc(idents_made, 1)
            pool.wait_ge(idents_made, 3)
            pool.affine_select(out=ident[:, :], in_=ident[:, :], compare_op=ALU.not_equal, fill=1.0,
                               base=0, pattern=[[-1, P]], channel_multiplier=1).then_inc(idents_made, 1)
            pool.affine_select(out=lower[:, :], in_=ones[:, 0:P], compare_op=ALU.is_gt, fill=0.0,
                               base=0, pattern=[[1, P]], channel_multiplier=-1).then_inc(idents_made, 1)
            pool.affine_select(out=head_mask[:, :], in_=ones[:, 0:HEADS], compare_op=ALU.is_ge, fill=0.0,
                               base=0, pattern=[[-HEAD, HEADS]], channel_multiplier=1).then_inc(idents_made, 1)
            pool.wait_ge(idents_made, 6)
            pool.affine_select(out=head_mask[:, :], in_=head_mask[:, :], compare_op=ALU.is_ge, fill=0.0,
                               base=HEAD - 1, pattern=[[HEAD, HEADS]], channel_multiplier=-1).then_inc(idents_made, 1)
            pool.iota(expert_down[:, :], pattern=[[-1, EXPERTS]], base=EXPERTS, channel_multiplier=0,
                      allow_small_or_imprecise_dtypes=True).then_inc(idents_made, 1)
            pool.iota(tile_starts[:, :], pattern=[[RTILE, TOKENS // RTILE]], base=0, channel_multiplier=0,
                      allow_small_or_imprecise_dtypes=True).then_inc(idents_made, 1)
            pool.iota(tile_numbers[:, :], pattern=[[1, ROUTED_TILES]], base=0, channel_multiplier=0,
                      allow_small_or_imprecise_dtypes=True).then_inc(idents_made, 1)

            def turn_q(n, s):
                pool.wait_ge(q_copied, n + 1)
                pool.tensor_copy(q_pos[:, :, bass.ds(n * GB, GB)].rearrange("p i b -> p b i"),
                                 q_out[:, s, :].rearrange("p (b i) -> p b i", i=SEQ)).then_inc(q_turned, 1)
            pairs(pool, turn_q, 0, GROUPS)

            def pick_q(g, n, s):
                if not early(g):
                    pool.wait_ge(scored, g - 1)
                q = q_pos[:, :, bass.ds(n * GB, GB)].rearrange("p i b -> p b i")
                pool.tensor_tensor(q_g[:, s, :].rearrange("p (b i) -> p b i", i=SEQ), q,
                                   ones[:, 0:GTOK].rearrange("p (b i) -> p b i", i=SEQ), ALU.mult).then_inc(q_picked, 1)

            pool.wait_ge(sums_made, 5)
            def expand_v(g, s):
                pool.wait_ge(v_loaded[s], (g - s) * 16 + 32)
                if not early(g):
                    pool.wait_ge(attended, g - 1)
                for pair in range(2):
                    last = pool.tensor_tensor(v_exp[:, s, :, pair, :], v_g[:, s, :, :],
                                              sum_heads[:, pair:pair + 1, :].to_broadcast([P, GB, 32]), ALU.mult)
                last.then_inc(v_expanded, 1)
            def attend_quad(quad):
                def step(n, s):
                    pick_q(quad * GROUPS + n + 1, n + 1, 1 - s)
                    expand_v(quad * GROUPS + n, s)
                pick_q(quad * GROUPS, 0, 0)
                step(0, 0)
                step(1, 1)
                pairs(pool, step, 2, GROUPS - 2)
                step(GROUPS - 2, 0)
                expand_v(quad * GROUPS + GROUPS - 1, 1)
            quads(pool, attend_quad)

            def stage3(n, j):
                s = j % 2
                pool.wait_ge(res_loaded[j], round_of(n, j, 4) * (16 + 16 * QUADS))
                if not early(n):
                    pool.wait_ge(x2_done, n - 1)
                for t in range(GROUP_TILES):
                    last = pool.tensor_tensor(xb[:, s, t * DIM:(t + 1) * DIM], x_in3[:, j, t * DIM:(t + 1) * DIM],
                                              bo_s[:, :], ALU.add)
                last.then_inc(biased, 1)
            for n in range(4):
                stage3(n, n)
            fours(pool, stage3, 4, GROUPS)

            pool.wait_ge(routed, 1)
            pool.wait_ge(zeros_stored, 32)
            pool.wait_ge(xn3_kept, GROUPS)
            for t in range(TILES):
                pool.indirect_dma_start(
                    out=sorted_x, out_offset=bass.IndirectOffsetOnAxis(ap=row_i[:, t:t + 1], axis=0),
                    in_=xn2[:, t * P:(t + 1) * P], in_offset=None).then_inc(scattered, 16)

            for s in range(3):
                pool.wait_ge(ry_stored[s], 16 * (ROUTED_TILES // 3))
            for n in range(GROUPS):
                s = n % 2
                if n >= 2:
                    pool.wait_ge(summed, n - 1)
                for t in range(GROUP_TILES):
                    tt = n * GROUP_TILES + t
                    pool.indirect_dma_start(
                        out=y_in[:, s, t * DIM:(t + 1) * DIM], out_offset=None, in_=sorted_y,
                        in_offset=bass.IndirectOffsetOnAxis(ap=row_i[:, tt:tt + 1], axis=0)).then_inc(y_gathered[s], 16)

        @block.scalar
        def _(act):
            act.wait_ge(qkv_weights_loaded, 16 * N_QKV_WEIGHTS)

            def deviation(n, j, var_done, done):
                act.wait_ge(var_done, n + 1)
                act.activation(ln_std[:, j, :], ln_mv[:, j, :, 1], ACT.Sqrt, bias=eps_s[:, 0:1]).then_inc(done, 1)

            def copy_in(n, s):
                act.wait_ge(in_transposed, n + 1)
                if not early(n):
                    act.wait_ge(v_projected, n - 1)
                act.activation(xn_t[:, s, :], ps[:, 0, :], ACT.Identity).then_inc(xn_t_copied, 1)
                act.activation(ctx_t[:, s, :], ps[:, 1, :], ACT.Identity).then_inc(ctx_t_copied, 1)

            def project(n, s):
                if not early(n):
                    act.wait_ge(kv_stored[s], round_of(n, s) * 32 - 32)
                    act.wait_ge(q_turned, n - 1)
                act.wait_ge(q_projected, n + 1)
                act.activation(q_out[:, s, :], ps[:, 2, :], ACT.Identity, bias=bq_s[:, 0:1]).then_inc(q_copied, 1)
                act.wait_ge(k_projected, n + 1)
                act.activation(k_out[:, s, :], ps[:, 3, :], ACT.Identity, bias=bk_s[:, 0:1]).then_inc(k_copied, 1)

            def store_kv(n, s):
                act.wait_ge(k_copied, n + 1)
                act.dma_start(k_d[:, bass.ds(n * GTOK, GTOK)], k_out[:, s, :]).then_inc(kv_stored[s], 16)
                act.wait_ge(v_copied, n + 1)
                act.dma_start(v_groups[n], v_out[:, s, :].rearrange("p (t d) -> p t d", d=DIM)).then_inc(kv_stored[s], 16)

            def step(n, j, last=False):
                if not last:
                    deviation(n + 1, (j + 1) % 4, mv_done, std_done)
                copy_in(n, j % 2)
                if not early(n, 1):
                    project(n - 1, (j + 1) % 2)
                if not early(n, 2):
                    store_kv(n - 2, j % 2)
            act.wait_ge(eps_made, 1)
            deviation(0, 0, mv_done, std_done)
            for n in range(4):
                step(n, n)
            fours(act, step, 4, GROUPS - 4)
            for n in range(GROUPS - 4, GROUPS):
                step(n, n % 4, last=n == GROUPS - 1)
            project(GROUPS - 1, 1)
            store_kv(GROUPS - 2, 0)
            store_kv(GROUPS - 1, 1)

            def exp(quad, n, s):
                act.wait_ge(shifted, quad * GROUPS + n + 1)
                act.activation(prob[:, s, :], prob[:, s, :], ACT.Exp, scale=SCALE).then_inc(exped, 1)

            def copy_prob_t(quad, n, s):
                act.wait_ge(prob_turned, quad * GROUPS + n + 1)
                if not first_use(quad, n):
                    act.wait_ge(attended, quad * GROUPS + n - 1)
                act.activation(prob_t[:, s, :].rearrange("p (r t) -> p r t", r=2), ps[:, 4:6, :],
                               ACT.Identity).then_inc(prob_t_copied, 1)

            def expand_k(quad, n, s):
                act.wait_ge(k_loaded[s], (quad * (GROUPS // 2) + round_of(n, s)) * 16)
                if not first_use(quad, n):
                    act.wait_ge(scored, quad * GROUPS + n - 1)
                out = k_exp[:, s, :].rearrange("p (b r j h) -> p b r j h", r=2, j=SEQ, h=2)
                for h in range(2, QH):
                    last = act.activation(out[:, :, h // 2, :, h % 2],
                                          k_g[:, s, :].rearrange("p (b j) -> p b j", j=SEQ), ACT.Identity,
                                          scale=quad_mask[:, h:h + 1])
                last.then_inc(k_expanded_act, 1)

            def attend_quad(quad):
                follows = not isinstance(quad, int)
                if follows:
                    copy_prob_t(quad - 1, GROUPS - 2, 0)
                act.wait_ge(window_made, quad + 1)
                for k in range(0, POS_BANKS, 2):
                    act.wait_ge(pos_made, quad * POS_BANKS + (k + 1))
                    i = 4 * (k % (SEQ // 4))
                    act.activation(
                        pos_t[:, k // (SEQ // 4), :].rearrange("p (b i) -> p i b", i=SEQ)[:, i:i + 4, :],
                        ps[:, k % 4, :].rearrange("p (i b) -> p i b", i=4), ACT.Identity).then_inc(pos_copied_act, 1)
                    if k == 0 and follows:
                        exp(quad - 1, GROUPS - 1, 1)
                    if k == 10 and follows:
                        copy_prob_t(quad - 1, GROUPS - 1, 1)
                    if k == 16:
                        expand_k(quad, 0, 0)
                    if k == 22:
                        expand_k(quad, 1, 1)
                exp(quad, 0, 0)
                expand_k(quad, 2, 0)

                def step(n, s):
                    copy_prob_t(quad, n - 2, s)
                    exp(quad, n - 1, 1 - s)
                    expand_k(quad, n + 1, 1 - s)
                step(2, 0)
                step(3, 1)
                pairs(act, step, 4, GROUPS - 2)
                step(GROUPS - 2, 0)
                copy_prob_t(quad, GROUPS - 3, 1)
                exp(quad, GROUPS - 2, 0)
            quads(act, attend_quad)
            copy_prob_t(QUADS - 1, GROUPS - 2, 0)
            exp(QUADS - 1, GROUPS - 1, 1)
            copy_prob_t(QUADS - 1, GROUPS - 1, 1)

            def turned(n, s):
                act.wait_ge(xn3_turned, n + 1)
                act.activation(xn2_t[:, bass.ds(n * GTOK, GTOK)], ps[:, 2 + s, :], ACT.Identity)
                if not early(n):
                    act.wait_ge(logit_made, n - 1)
                act.activation(xn3_t[:, s, :], ps[:, 2 + s, :], ACT.Identity).then_inc(xn3_t_copied, 1)

            def keep_xn(n, s):
                act.wait_ge(ln2, n + 1)
                act.activation(xn2[:, bass.ds(n * GTOK, GTOK)], xn3[:, s, :], ACT.Identity).then_inc(xn3_kept, 1)

            def step(n, j, last=False):
                if not last:
                    deviation(n + 1, (j + 1) % 4, mv2, std2)
                keep_xn(n, j % 2)
                turned(n, j % 2)
            deviation(0, 0, mv2, std2)
            for n in range(4):
                step(n, n)
            fours(act, step, 4, GROUPS - 4)
            for n in range(GROUPS - 4, GROUPS):
                step(n, n % 4, last=n == GROUPS - 1)

            def gelu(n, s):
                for c in range(IC):
                    act.wait_ge(up_made, n * IC + (c + 1))
                    if not (isinstance(n, int) and n == 0 and c < 2):
                        act.wait_ge(hidden_made, n * IC + (c - 1))
                    act.activation(gate[:, c % 2, :], ps[:, c % 2, :], ACT.Gelu).then_inc(gated, 1)
            gelu(0, 0)
            gelu(1, 1)
            pairs(act, gelu, 2, FRONT)

            def copy_rx(k, s):
                act.wait_ge(rx_turned, k + 1)
                if not early(k, 3):
                    act.wait_ge(r_up_made, (k - 2) * IC)
                act.activation(rx_t[:, s, :], ps[:, 6, 0:RTILE], ACT.Identity).then_inc(rx_t_copied, 1)

            def expert(k, s, last=False):
                for c in range(IC):
                    if c == 2 and not last:
                        copy_rx(k + 1, (s + 1) % 3)
                    act.wait_ge(r_up_made, k * IC + (c + 1))
                    if not (isinstance(k, int) and k == 0 and c < 2):
                        act.wait_ge(r_hidden_made, k * IC + (c - 1))
                    act.activation(gate[:, c % 2, 0:RTILE], ps[:, c % 2, 0:RTILE], ACT.Gelu).then_inc(r_gated, 1)
            copy_rx(0, 0)
            for k in range(3):
                expert(k, k)
            triples(act, expert, 3, ROUTED_TILES - 3)
            for k in range(3):
                expert(ROUTED_TILES - 3 + k, k, last=k == 2)
            pairs(act, gelu, FRONT, GROUPS)

        @block.tensor
        def _(pe):
            pe.wait_ge(qkv_weights_loaded, 16 * N_QKV_WEIGHTS)
            pe.wait_ge(idents_made, 7)

            def turn_in(n, j):
                s = j % 2
                pe.wait_ge(ctx_loaded[j], round_of(n, j, 4) * 16)
                pe.wait_ge(ln_done, n + 1)
                if not early(n, 1):
                    pe.wait_ge(xn_t_copied, n)
                    pe.wait_ge(ctx_t_copied, n)
                for t in range(GROUP_TILES):
                    pe.transpose(ps[:, 0, t * P:(t + 1) * P], xn[:, s, t * DIM:(t + 1) * DIM], ident[:, :])
                    last = pe.transpose(ps[:, 1, t * P:(t + 1) * P], ctx_in[:, j, t * DIM:(t + 1) * DIM], ident[:, :])
                last.then_inc(in_transposed, 1)

            def project(n, s):
                pe.wait_ge(xn_t_copied, n + 1)
                pe.wait_ge(ctx_t_copied, n + 1)
                if not early(n, 1):
                    pe.wait_ge(q_copied, n)
                    pe.wait_ge(k_copied, n)
                    pe.wait_ge(v_copied, n)
                pe.matmul(ps[:, 2, :], wq_s[:, :], xn_t[:, s, :], start=True, stop=True).then_inc(q_projected, 1)
                pe.matmul(ps[:, 3, :], wk_s[:, :], ctx_t[:, s, :], start=True, stop=True).then_inc(k_projected, 1)
                for t in range(GROUP_TILES):
                    last = pe.matmul(ps[:, 4, t * P:(t + 1) * P], ctx_t[:, s, t * P:(t + 1) * P], wv_s[:, :],
                                     start=True, stop=True)
                last.then_inc(v_projected, 1)

            turn_in(0, 0)

            def step(n, j):
                turn_in(n + 1, (j + 1) % 4)
                project(n, j % 2)
            for n in range(4):
                step(n, n)
            fours(pe, step, 4, GROUPS - 4)
            for n in range(GROUPS - 4, GROUPS - 1):
                step(n, n % 4)
            project(GROUPS - 1, 1)
            pe.wait_ge(weights_loaded, 16 * N_WEIGHTS)
            pe.transpose(ps[:, 7, 0:P], rel_rows[:, :, :].rearrange("p h d -> p (h d)"), ident[:, :]).then_inc(rel_transposed, 1)
            pe.wait_ge(q_turned, GROUPS)
            pe.wait_ge(sums_made, 5)
            pe.wait_ge(v_copied, GROUPS)
            pe.wait_ge(k_copied, GROUPS)

            def score(quad, n, s):
                g = quad * GROUPS + n
                pe.wait_ge(pos_loaded[s], (quad * (GROUPS // 2) + round_of(n, s)) * 16)
                pe.wait_ge(q_picked, g + 1)
                pe.wait_ge(k_expanded, g + 1)
                pe.wait_ge(k_expanded_act, g + 1)
                if not early(n):
                    pe.wait_ge(shifted, g - 1)
                for t in range(GROUP_TILES):
                    bank, c = 2 * s + t // 2, 256 * (t % 2)
                    for pair in range(2):
                        pe.matmul(ps[:, bank, c + P * pair:c + P * pair + P], pos_g[:, s, pair, t * P:(t + 1) * P],
                                  ident[:, :], start=(t % 2 == 0 and pair == 0), stop=False, is_transpose=True,
                                  skip_group_check=True)
                    for b in range(2):
                        last = pe.matmul(ps[64 * b:64 * b + 64, bank, c:c + 256],
                                         q_g[:, s, t * P + 64 * b:t * P + 64 * b + 64],
                                         k_exp[:, s, (2 * t + b) * 256:(2 * t + b + 1) * 256],
                                         start=False, stop=True, skip_group_check=True)
                last.then_inc(scored, 1)

            def turn_prob(quad, n, s):
                g = quad * GROUPS + n
                pe.wait_ge(exped, g + 1)
                if not (first_use(quad, n) and n == 0):
                    pe.wait_ge(prob_t_copied, g)
                for pair in range(2):
                    for t in range(GROUP_TILES):
                        last = pe.transpose(ps[:, 4 + pair, t * P:(t + 1) * P],
                                            prob[:, s, t * 256 + pair * P:t * 256 + pair * P + P], ident[:, :])
                last.then_inc(prob_turned, 1)

            def attend(quad, n, s):
                g = quad * GROUPS + n
                pe.wait_ge(prob_t_copied, g + 1)
                pe.wait_ge(v_expanded, g + 1)
                if not first_use(quad, n):
                    pe.wait_ge(normed, g - 1)
                for b2 in range(2):
                    for pair in range(2):
                        for b4 in range(4):
                            b = 2 * b4 + b2
                            pe.matmul(ps[32 * b4:32 * b4 + 32, 6 + s, 64 * b2:64 * b2 + 64], v_exp[:, s, b, pair, :],
                                      prob_t[:, s, pair * GTOK + b * SEQ:pair * GTOK + (b + 1) * SEQ],
                                      start=(pair == 0), stop=(pair == 1), tile_position=(0, 32 * b4))
                for pair in range(2):
                    for b4 in range(4):
                        at = pair * GTOK + b4 * 2 * SEQ
                        last = pe.matmul(ps[32 * b4:32 * b4 + 32, 6 + s, P:2 * P], sum_heads[:, pair, :],
                                         prob_t[:, s, at:at + 2 * SEQ], start=(pair == 0), stop=(pair == 1),
                                         tile_position=(0, 32 * b4))
                last.then_inc(attended, 1)

            def attend_quad(quad):
                follows = not isinstance(quad, int)
                pe.wait_ge(window_made, quad + 1)
                for k in range(POS_BANKS):
                    if k >= 4:
                        copied = pos_copied_act if k % 2 == 0 else pos_copied_dve
                        pe.wait_ge(copied, quad * (POS_BANKS // 2) + ((k - 4) // 2 + 1))
                    elif follows and k % 2 == 0:
                        pe.wait_ge(shifted, quad * GROUPS - 1 + k // 2)
                    pair, i0 = k // (SEQ // 4), 4 * (k % (SEQ // 4))
                    for i in range(i0, i0 + 4):
                        lo = MAX_REL - 1 - i
                        last = pe.matmul(ps[:, k % 4, (i - i0) * P:(i - i0 + 1) * P],
                                         rel_win[:, pair, lo:lo + SEQ, :].rearrange("p j h -> p (j h)"), q_pos[:, i, :],
                                         start=True, stop=True)
                    last.then_inc(pos_made, 1)
                    if k == 7 and follows:
                        turn_prob(quad - 1, GROUPS - 1, 1)
                if follows:
                    attend(quad - 1, GROUPS - 2, 0)
                    attend(quad - 1, GROUPS - 1, 1)
                pe.wait_ge(pos_copied_act, quad * (POS_BANKS // 2) + POS_BANKS // 2)
                pe.wait_ge(pos_copied_dve, quad * (POS_BANKS // 2) + POS_BANKS // 2)
                score(quad, 0, 0)
                score(quad, 1, 1)
                turn_prob(quad, 0, 0)

                def step(n, s):
                    score(quad, n, s)
                    turn_prob(quad, n - 1, 1 - s)
                    attend(quad, n - 2, s)
                step(2, 0)
                step(3, 1)
                pairs(pe, step, 4, GROUPS)
            quads(pe, attend_quad)
            turn_prob(QUADS - 1, GROUPS - 1, 1)
            attend(QUADS - 1, GROUPS - 2, 0)
            attend(QUADS - 1, GROUPS - 1, 1)

            pe.wait_ge(normed, QUADS * GROUPS)
            pe.wait_ge(zeros_stored, 32)

            def project_out(n, j):
                s = j % 2
                pe.wait_ge(res_loaded[j], round_of(n, j, 4) * (16 + 16 * QUADS))
                if not early(n):
                    pe.wait_ge(x2_done, n - 1)
                for t in range(GROUP_TILES):
                    last = pe.matmul(ps[:, s, t * DIM:(t + 1) * DIM], attn_in[:, j, t * P:(t + 1) * P], wo_s[:, :],
                                     start=True, stop=True)
                last.then_inc(o_projected, 1)

            def turn_xn(n, s):
                pe.wait_ge(ln2, n + 1)
                if not early(n):
                    pe.wait_ge(xn3_t_copied, n - 1)
                for t in range(GROUP_TILES):
                    last = pe.transpose(ps[:, 2 + s, t * P:(t + 1) * P], xn3[:, s, t * DIM:(t + 1) * DIM], ident[:, :])
                last.then_inc(xn3_turned, 1)

            def make_logits(n, s):
                pe.wait_ge(xn3_t_copied, n + 1)
                if not early(n):
                    pe.wait_ge(logit_copied, n - 1)
                for t in range(GROUP_TILES):
                    last = pe.matmul(ps[:, 4 + s, t * P:(t + 1) * P], xn3_t[:, s, t * P:(t + 1) * P], wg_s[:, :],
                                     start=True, stop=True)
                last.then_inc(logit_made, 1)
            def step(n, j):
                project_out(n, j)
                if not early(n, 2):
                    turn_xn(n - 2, j % 2)
                if not early(n, 3):
                    make_logits(n - 3, (j + 1) % 2)
            for n in range(4):
                step(n, n)
            fours(pe, step, 4, GROUPS)
            turn_xn(GROUPS - 2, 0)
            make_logits(GROUPS - 3, 1)
            turn_xn(GROUPS - 1, 1)
            make_logits(GROUPS - 2, 0)
            make_logits(GROUPS - 1, 1)

            pe.wait_ge(ranked, 1)
            pe.matmul(ps[:, 6, 0:EXPERTS], lower[:, :], count[:, :], start=True, stop=True)
            pe.matmul(ps[:, 7, 0:EXPERTS], ones[:, 0:P], count[:, :], start=True, stop=True).then_inc(ranked, 1)

            pe.wait_ge(logit_copied, GROUPS)

            def up(n):
                for c in range(IC):
                    if not (isinstance(n, int) and n == 0 and c < 2):
                        pe.wait_ge(hidden_made, n * IC + (c - 1))
                    xs = xn2_t[:, bass.ds(n * GTOK, GTOK)]
                    pe.matmul(ps[:, c % 2, :], w1s_s[:, c * P:(c + 1) * P], xs, start=True, stop=True)
                    pe.matmul(ps[:, 2 + c % 2, :], w2s_s[:, c * P:(c + 1) * P], xs, start=True, stop=True).then_inc(up_made, 1)

            def down(n, s):
                pe.wait_ge(hidden_made, n * IC + IC)
                if not early(n):
                    pe.wait_ge(added, n - 1)
                for t in range(GROUP_TILES):
                    for c in range(IC):
                        last = pe.matmul(ps[:, 4 + s, t * DIM:(t + 1) * DIM],
                                         hidden_t[:, s, c * GTOK + t * P:c * GTOK + (t + 1) * P], w3s_s[:, c, :],
                                         start=(c == 0), stop=(c == IC - 1))
                last.then_inc(down_made, 1)
            up(0)

            def shared(n, s):
                up(n)
                down(n - 1, 1 - s)
            shared(1, 1)
            pairs(pe, shared, 2, FRONT)
            down(FRONT - 1, 1)

            def turn_tile(k, s):
                pe.wait_ge(rx_loaded[s], round_of(k, s, 3) * 16)
                if not early(k, 1):
                    pe.wait_ge(rx_t_copied, k)
                for t in range(2):
                    last = pe.transpose(ps[:, 6, t * P:(t + 1) * P], rx[:, s, t * DIM:(t + 1) * DIM], ident[:, :])
                last.then_inc(rx_turned, 1)

            def r_up(k, s, cs):
                for c in cs:
                    if c == 0:
                        pe.wait_ge(rx_t_copied, k + 1)
                        pe.wait_ge(up_loaded[s], round_of(k, s, 3) * 32)
                    if not (isinstance(k, int) and k == 0 and c < 2):
                        pe.wait_ge(r_hidden_made, k * IC + (c - 1))
                    pe.matmul(ps[:, c % 2, 0:RTILE], rw1[:, s, c * P:(c + 1) * P], rx_t[:, s, :], start=True, stop=True)
                    pe.matmul(ps[:, 2 + c % 2, 0:RTILE], rw2[:, s, c * P:(c + 1) * P], rx_t[:, s, :],
                              start=True, stop=True).then_inc(r_up_made, 1)

            def r_down(k, s, ts=(0, 1)):
                if ts[0] == 0:
                    pe.wait_ge(down_loaded[s], round_of(k, s, 3) * 16)
                    pe.wait_ge(r_hidden_made, k * IC + IC)
                    if not early(k, 1):
                        pe.wait_ge(ry_copied, k)
                for t in ts:
                    for c in range(IC):
                        last = pe.matmul(ps[:, 4, t * DIM:(t + 1) * DIM],
                                         rhidden_t[:, s, c * RTILE + t * P:c * RTILE + (t + 1) * P],
                                         rw3[:, s, c * DIM:(c + 1) * DIM], start=(c == 0), stop=(c == IC - 1))
                if ts[-1] == 1:
                    last.then_inc(r_down_made, 1)

            pe.wait_ge(added, FRONT)
            turn_tile(0, 0)
            r_up(0, 0, range(IC))
            turn_tile(1, 1)

            def step(k, s, last=False):
                r_up(k, s, (0, 1))
                r_down(k - 1, (s - 1) % 3, (0,))
                if not last:
                    turn_tile(k + 1, (s + 1) % 3)
                r_up(k, s, (2, 3))
                r_down(k - 1, (s - 1) % 3, (1,))
            triples(pe, step, 1, ROUTED_TILES - 2)
            step(ROUTED_TILES - 2, 1)
            step(ROUTED_TILES - 1, 2, last=True)
            r_down(ROUTED_TILES - 1, 2)

            pe.wait_ge(ry_copied, ROUTED_TILES)
            up(FRONT)
            shared(FRONT + 1, 1)
            pairs(pe, shared, FRONT + 2, GROUPS)
            down(GROUPS - 1, 1)

        @block.vector
        def _(dve):
            dve.memset(eps_s[:, :], EPS).then_inc(eps_made, 1)
            dve.wait_ge(idents_made, 4)
            for hp in range(2):
                last = dve.tensor_reduce(parity[:, hp:hp + 1], ident[:, hp:P:2], AX, ALU.add)
            last.then_inc(sums_made, 1)
            dve.wait_ge(sums_made, 1)
            for h in range(QH):
                dve.tensor_scalar(sum_heads[:, h // 2, HEAD * h:HEAD * h + HEAD], ones[:, 0:HEAD], parity[:, h % 2:h % 2 + 1],
                                  None, ALU.mult).then_inc(sums_made, 1)

            def statistics(n, j, x_of, stats, mv):
                dve.memset(wait_word[:, 0:1], 0.0)
                for t in range(GROUP_TILES):
                    last = dve.bn_stats(ln_stats[:, j, t, :], x_of(t))
                last.then_inc(stats, 1)
                dve.wait_ge(stats, n + 1)
                dve.memset(wait_word[:, 1:2], 0.0)
                for t in range(GROUP_TILES):
                    last = dve.bn_aggr(ln_mv[:, j, t, :], ln_stats[:, j, t, :])
                last.then_inc(mv, 1)

            def inverse(n, j, std, rstd):
                dve.wait_ge(std, n + 1)
                dve.reciprocal(ln_rstd[:, j, :], ln_std[:, j, :]).then_inc(rstd, 1)

            def normalize(n, j, x_of, out_of, rstd, done):
                dve.wait_ge(rstd, n + 1)
                for t in range(GROUP_TILES):
                    last = dve.tensor_scalar(out_of(t), x_of(t), ln_mv[:, j, t, 0:1], ln_rstd[:, j, t:t + 1],
                                             ALU.subtract, ALU.mult)
                last.then_inc(done, 1)

            def stats_in(n, j):
                dve.wait_ge(in_loaded[j], round_of(n, j, 4) * 16)
                statistics(n, j, lambda t: x_in[:, j, t * DIM:(t + 1) * DIM], stats_done, mv_done)

            def norm_in(n, j):
                if not early(n):
                    dve.wait_ge(in_transposed, n - 1)
                normalize(n, j, lambda t: x_in[:, j, t * DIM:(t + 1) * DIM],
                          lambda t: xn[:, j % 2, t * DIM:(t + 1) * DIM], rstd_done, ln_done)

            def copy_v(n, s):
                dve.wait_ge(v_projected, n + 1)
                if not early(n):
                    dve.wait_ge(kv_stored[s], round_of(n, s) * 32 - 32)
                dve.tensor_tensor(v_out[:, s, :].rearrange("p (t d) -> p t d", d=DIM),
                                  ps[:, 4, :].rearrange("p (t d) -> p t d", d=DIM),
                                  bv_s[:, :].rearrange("p (a d) -> p a d", a=1).to_broadcast([P, GROUP_TILES, DIM]),
                                  ALU.add).then_inc(v_copied, 1)

            def step(n, j, ahead=True):
                inverse(n, j, std_done, rstd_done)
                norm_in(n, j)
                if not early(n):
                    copy_v(n - 2, j % 2)
                if ahead:
                    stats_in(n + 2, (j + 2) % 4)
            stats_in(0, 0)
            stats_in(1, 1)
            dve.wait_ge(qkv_weights_loaded, 16 * N_QKV_WEIGHTS)
            for n in range(4):
                step(n, n)
            fours(dve, step, 4, GROUPS - 4)
            for n in range(GROUPS - 4, GROUPS):
                step(n, n % 4, ahead=n < GROUPS - 2)
            copy_v(GROUPS - 2, 0)
            copy_v(GROUPS - 1, 1)

            dve.wait_ge(rel_transposed, 1)
            dve.tensor_copy(rel_t[:, :], ps[:, 7, 0:NREL]).then_inc(rel_copied, 1)
            dve.wait_ge(rel_copied, 1)

            def expand_k(quad, n, s):
                dve.wait_ge(k_loaded[s], (quad * (GROUPS // 2) + round_of(n, s)) * 16)
                if not first_use(quad, n):
                    dve.wait_ge(scored, quad * GROUPS + n - 1)
                out = k_exp[:, s, :].rearrange("p (b r j h) -> p b r j h", r=2, j=SEQ, h=2)
                for h in range(2):
                    last = dve.tensor_scalar(out[:, :, h // 2, :, h % 2], k_g[:, s, :].rearrange("p (b j) -> p b j", j=SEQ),
                                             quad_mask[:, h:h + 1], None, ALU.mult)
                last.then_inc(k_expanded, 1)

            def shift(quad, n, s):
                g = quad * GROUPS + n
                scores = ps[:, 2 * s:2 * s + 2, :].rearrange("p k (r j h) -> p (k r) j h", j=SEQ, h=2)
                dve.wait_ge(scored, g + 1)
                dve.tensor_reduce(row_max[:, s, :, :], scores.rearrange("p r j h -> p r h j"), AX, ALU.max).then_inc(maxed, 1)
                dve.wait_ge(maxed, g + 1)
                if not first_use(quad, n):
                    dve.wait_ge(prob_turned, g - 1)
                dve.tensor_tensor(prob[:, s, :].rearrange("p (r j h) -> p r j h", j=SEQ, h=2), scores,
                                  row_max[:, s, :, :].rearrange("p r (a h) -> p r a h", a=1).to_broadcast(
                                      [P, GROUP_TILES * 2, SEQ, 2]), ALU.subtract).then_inc(shifted, 1)

            def norm(quad, n, s):
                g = quad * GROUPS + n
                dve.wait_ge(attended, g + 1)
                dve.reciprocal(den_r[:, s, :], ps[:, 6 + s, P:2 * P]).then_inc(den_inverted, 1)
                dve.wait_ge(den_inverted, g + 1)
                if not first_use(quad, n):
                    dve.wait_ge(attn_stored[s], (quad * (GROUPS // 2) + round_of(n, s)) * 16 - 16)
                dve.tensor_tensor(attn_o[:, s, :], ps[:, 6 + s, 0:P], den_r[:, s, :], ALU.mult).then_inc(normed, 1)

            def attend_quad(quad):
                follows = not isinstance(quad, int)
                if follows:
                    dve.wait_ge(k_expanded_act, quad * GROUPS)
                    dve.wait_ge(pos_made, quad * POS_BANKS)
                dve.tensor_copy(quad_mask[:, :], head_mask[:, bass.ds(quad * QH, QH)])
                for h in range(QH):
                    last = dve.tensor_scalar(rel_win[:, h // 2, :, h % 2], rel_t[:, :], head_mask[:, bass.ds(quad * QH + h, 1)],
                                             None, ALU.mult)
                last.then_inc(window_made, 1)
                if follows:
                    shift(quad - 1, GROUPS - 1, 1)
                for k in range(1, POS_BANKS, 2):
                    dve.wait_ge(pos_made, quad * POS_BANKS + (k + 1))
                    i = 4 * (k % (SEQ // 4))
                    dve.tensor_copy(
                        pos_t[:, k // (SEQ // 4), :].rearrange("p (b i) -> p i b", i=SEQ)[:, i:i + 4, :],
                        ps[:, k % 4, :].rearrange("p (i b) -> p i b", i=4)).then_inc(pos_copied_dve, 1)
                    if k == 3 and follows:
                        norm(quad - 1, GROUPS - 3, 1)
                    if k == 15:
                        expand_k(quad, 0, 0)
                    if k == 21:
                        expand_k(quad, 1, 1)
                if follows:
                    norm(quad - 1, GROUPS - 2, 0)
                    norm(quad - 1, GROUPS - 1, 1)
                shift(quad, 0, 0)
                expand_k(quad, 2, 0)
                shift(quad, 1, 1)

                def step(n, s):
                    expand_k(quad, n, s)
                    shift(quad, n - 1, 1 - s)
                    norm(quad, n - 3, 1 - s)
                step(3, 1)
                pairs(dve, step, 4, GROUPS)
            quads(dve, attend_quad)
            shift(QUADS - 1, GROUPS - 1, 1)
            for n in range(GROUPS - 3, GROUPS):
                norm(QUADS - 1, n, n % 2)

            def residual(n, j):
                s = j % 2
                dve.wait_ge(biased, n + 1)
                dve.wait_ge(o_projected, n + 1)
                dve.tensor_tensor(acc[:, bass.ds(n * GTOK, GTOK)], ps[:, s, :], xb[:, s, :], ALU.add).then_inc(x2_done, 1)
                dve.wait_ge(x2_done, n + 1)
                statistics(n, j, lambda t: acc[:, bass.ds(n * GTOK + t * DIM, DIM)], stats2, mv2)

            def norm2(n, j):
                if not early(n):
                    dve.wait_ge(xn3_turned, n - 1)
                    dve.wait_ge(xn3_kept, n - 1)
                normalize(n, j, lambda t: acc[:, bass.ds(n * GTOK + t * DIM, DIM)],
                          lambda t: xn3[:, j % 2, t * DIM:(t + 1) * DIM], rstd2, ln2)

            def keep_logits(n, s):
                dve.wait_ge(logit_made, n + 1)
                dve.tensor_copy(logits[:, bass.ds(n * GROUP_TILES, GROUP_TILES), :],
                                ps[:, 4 + s, :].rearrange("p (t e) -> p t e", t=GROUP_TILES)[:, :, 0:EXPERTS],
                                ).then_inc(logit_copied, 1)

            def step(n, j, ahead=True):
                inverse(n, j, std2, rstd2)
                norm2(n, j)
                if not early(n, 3):
                    keep_logits(n - 3, (j + 1) % 2)
                if ahead:
                    residual(n + 2, (j + 2) % 4)
            residual(0, 0)
            residual(1, 1)
            for n in range(4):
                step(n, n)
            fours(dve, step, 4, GROUPS - 4)
            for n in range(GROUPS - 4, GROUPS):
                step(n, n % 4, ahead=n < GROUPS - 2)
            for n in range(GROUPS - 3, GROUPS):
                keep_logits(n, n % 2)

            steps = [0]

            def then(ins):
                steps[0] += 1
                ins.then_inc(route_step, 1)
                dve.wait_ge(route_step, steps[0])

            def over_experts(a):
                return a.rearrange("p (t e) -> p t e", e=1).to_broadcast([P, TILES, EXPERTS])

            dve.wait_ge(logit_copied, GROUPS)
            dve.wait_ge(idents_made, 10)
            then(dve.tensor_reduce(best[:, :], logits, AX, ALU.max))
            then(dve.tensor_tensor(hit, logits, over_experts(best[:, :]), ALU.is_equal))
            down_b = expert_down[:, :].rearrange("p (t e) -> p t e", t=1).to_broadcast([P, TILES, EXPERTS])
            then(dve.tensor_tensor(hit, hit, down_b, ALU.mult))
            then(dve.tensor_reduce(rank[:, :], hit, AX, ALU.max))
            then(dve.tensor_tensor(chosen.rearrange("p e t -> p t e"), down_b, over_experts(rank[:, :]), ALU.is_equal))
            then(dve.tensor_reduce(count[:, :], chosen, AX, ALU.add))
            dve.sem_inc(ranked, 1)
            then(dve.tensor_tensor_scan(seen.rearrange("p e t -> p (e t)"), ones[:, :],
                                        chosen.rearrange("p e t -> p (e t)"), 0.0, ALU.mult, ALU.add))
            dve.wait_ge(ranked, 2)
            then(dve.tensor_copy(total[:, :], ps[:, 7, 0:EXPERTS]))
            then(dve.tensor_tensor(starts_hit, total[:, :].rearrange("p (e k) -> p e k", k=1).to_broadcast(
                [P, EXPERTS, TOKENS // RTILE]), tile_starts[:, :].rearrange("p (e k) -> p e k", e=1).to_broadcast(
                [P, EXPERTS, TOKENS // RTILE]), ALU.is_gt))
            then(dve.tensor_reduce(n_tiles[:, :], starts_hit, AX, ALU.add))
            then(dve.tensor_tensor_scan(tiles_end[:, :], ones[:, 0:EXPERTS], n_tiles[:, :], 0.0, ALU.mult, ALU.add))
            then(dve.tensor_tensor(base[:, :], tiles_end[:, :], n_tiles[:, :], ALU.subtract))
            then(dve.tensor_scalar(base[:, :], base[:, :], float(RTILE), None, ALU.mult))
            then(dve.tensor_tensor(base[:, :], ps[:, 6, 0:EXPERTS], base[:, :], ALU.add))
            then(dve.tensor_tensor(base[:, 1:EXPERTS], base[:, 1:EXPERTS], seen[:, 0:EXPERTS - 1, TILES - 1], ALU.subtract))
            then(dve.scalar_tensor_tensor(out=place, in0=seen, scalar=-1.0,
                                          in1=base[:, :].rearrange("p (e t) -> p e t", t=1).to_broadcast([P, EXPERTS, TILES]),
                                          op0=ALU.add, op1=ALU.add))
            then(dve.tensor_tensor(place, place, chosen, ALU.mult))
            then(dve.tensor_reduce(row_f[:, :], place.rearrange("p e t -> p t e"), AX, ALU.add))
            then(dve.tensor_copy(row_i[:, :], row_f[:, :]))
            then(dve.tensor_tensor(tiles_hit, tiles_end[:, :].rearrange("p (k e) -> p k e", k=1).to_broadcast(
                [P, ROUTED_TILES, EXPERTS]), tile_numbers[:, :].rearrange("p (k e) -> p k e", e=1).to_broadcast(
                [P, ROUTED_TILES, EXPERTS]), ALU.is_le))
            then(dve.tensor_reduce(expert_f[:, :], tiles_hit, AX, ALU.add))
            then(dve.tensor_scalar(expert_f[:, :], expert_f[:, :], float(EXPERTS - 1), None, ALU.min))
            dve.tensor_copy(expert_i[:, :], expert_f[:, :]).then_inc(routed, 1)

            dve.wait_ge(xn3_kept, GROUPS)

            def hidden(n, s):
                for c in range(IC):
                    dve.wait_ge(gated, n * IC + (c + 1))
                    if c == 0 and not early(n):
                        dve.wait_ge(down_made, n - 1)
                    dve.tensor_tensor(hidden_t[:, s, c * GTOK:(c + 1) * GTOK], ps[:, 2 + c % 2, :], gate[:, c % 2, :],
                                      ALU.mult).then_inc(hidden_made, 1)

            def add_shared(n, s):
                dve.wait_ge(down_made, n + 1)
                rows = acc[:, bass.ds(n * GTOK, GTOK)]
                dve.tensor_tensor(rows, ps[:, 4 + s, :], rows, ALU.add).then_inc(added, 1)
            hidden(0, 0)
            hidden(1, 1)
            add_shared(0, 0)

            def step(n, s):
                hidden(n, s)
                add_shared(n - 1, 1 - s)
            pairs(dve, step, 2, FRONT)
            add_shared(FRONT - 1, 1)

            def r_hidden(k, s):
                for c in range(IC):
                    dve.wait_ge(r_gated, k * IC + (c + 1))
                    if c == 0 and not early(k, 3):
                        dve.wait_ge(r_down_made, k - 2)
                    dve.tensor_tensor(rhidden_t[:, s, c * RTILE:(c + 1) * RTILE], ps[:, 2 + c % 2, 0:RTILE],
                                      gate[:, c % 2, 0:RTILE], ALU.mult).then_inc(r_hidden_made, 1)

            def copy_y(k, s):
                dve.wait_ge(r_down_made, k + 1)
                if not early(k, 3):
                    dve.wait_ge(ry_stored[s], round_of(k, s, 3) * 16 - 16)
                dve.tensor_copy(ry[:, s, :], ps[:, 4, 0:RTILE]).then_inc(ry_copied, 1)
            r_hidden(0, 0)

            def step(k, s):
                r_hidden(k, s)
                copy_y(k - 1, (s - 1) % 3)
            step(1, 1)
            step(2, 2)
            step(3, 0)
            triples(dve, step, 4, ROUTED_TILES - 2)
            step(ROUTED_TILES - 2, 1)
            step(ROUTED_TILES - 1, 2)
            copy_y(ROUTED_TILES - 1, 2)

            def add_routed(n, s):
                dve.wait_ge(added, n + 1)
                dve.wait_ge(y_gathered[s], round_of(n, s) * (16 * GROUP_TILES))
                rows = acc[:, bass.ds(n * GTOK, GTOK)]
                dve.tensor_tensor(rows, rows, y_in[:, s, :], ALU.add).then_inc(summed, 1)

            def step(n, s):
                hidden(n, s)
                add_shared(n - 1, 1 - s)
                for k in range(2):
                    add_routed(n * 2 - (2 * FRONT + 2 - k), k)
            hidden(FRONT, 0)
            step(FRONT + 1, 1)
            pairs(dve, step, FRONT + 2, GROUPS)
            add_routed(GROUPS - 2, 0)
            add_shared(GROUPS - 1, 1)
            add_routed(GROUPS - 1, 1)


_INS = ['x', 'ctx_1024', 'L0_xattn_wq', 'L0_xattn_bq', 'L0_xattn_wk', 'L0_xattn_bk', 'L0_xattn_wv', 'L0_xattn_bv',
        'L0_xattn_wo', 'L0_xattn_bo', 'L0_xattn_rel_emb', 'L0_ffn_w1s', 'L0_ffn_w2s', 'L0_ffn_w3s', 'L0_ffn_W1',
        'L0_ffn_W2', 'L0_ffn_W3', 'L0_ffn_Wg']
_OUTS = [((BATCHES, SEQ, DIM), 'float32')]


def kernel(**inputs):
    import numpy as _np
    import concourse.bacc as _bacc
    from concourse import mybir as _mybir
    from concourse.bass_utils import run_bass_kernel_spmd as _run

    nc = _bacc.Bacc("TRN2", target_bir_lowering=False, num_devices=1)
    arrays, args = {}, []
    for name in _INS:
        a = _np.ascontiguousarray(inputs[name])
        arrays[f"in_{name}_dram"] = a
        args.append(nc.dram_tensor(f"in_{name}_dram", a.shape, _mybir.dt.from_np(a.dtype), kind="ExternalInput").ap())
    for i, (shape, dtype) in enumerate(_OUTS):
        dt = _mybir.dt.from_np(_np.dtype(dtype))
        args.append(nc.dram_tensor(f"out_{i}_dram", shape, dt, kind="ExternalOutput").ap())
    xattn_moe(nc, *args)
    r = _run(nc, [arrays], core_ids=[0])
    got = tuple(r.results[0][f"out_{i}_dram"] for i in range(len(_OUTS)))
    return got[0]
```

```python
from contextlib import ExitStack

import concourse.bass as bass
from concourse import mybir

P = 128
F32 = mybir.dt.float32
BF16 = mybir.dt.bfloat16
F32R = mybir.dt.float32r
I32 = mybir.dt.int32
ALU = mybir.AluOpType
ACT = mybir.ActivationFunctionType
AX = mybir.AxisListType.X

BATCHES, SEQ, DIM = 128, 64, 128
HEADS, HEAD = 16, 8
TOKENS = BATCHES * SEQ
TILES = TOKENS // P
GROUP_TILES = 4
GTOK = GROUP_TILES * P
GB = GTOK // SEQ
GROUPS = TOKENS // GTOK
QUADS, QH = HEADS // 4, 4
MAX_REL = 64
NREL = 2 * MAX_REL
INTER = 512
IC = INTER // P
EXPERTS = 8
RTILE = 256
ROUTED_TILES = TOKENS // RTILE + EXPERTS - 1
EPS = 1e-5
SCALE = float(HEAD) ** -0.5
POS_BANKS = 2 * SEQ // 4
REL_PARTS = ((1, 0, 2, 1), (0, 1, 0, 2))
Q_PARTS = ((1, 2, 1, 2), (0, 0, 1, 0))
QF = QH * HEAD
CHUNKS = GROUPS // 4
FRONT = GROUPS // 2


def xattn_moe(nc, x, ctx_1024, wq, bq, wk, bk, wv, bv, wo, bo, rel_emb, w1s, w2s, w3s, W1, W2, W3, Wg, out):
    x_rows = x.rearrange("b s d -> (b s) d").rearrange("(n t p) d -> n p t d", t=GROUP_TILES, p=P)
    ctx_rows = ctx_1024.rearrange("b s d -> (b s) d").rearrange("(n t p) d -> n p t d", t=GROUP_TILES, p=P)
    out_rows = out.rearrange("b s d -> (b s) d").rearrange("(n t p) d -> n p t d", t=GROUP_TILES, p=P)
    q_parts_d = nc.dram_tensor("q_parts_scratch", [DIM, 3, TOKENS], BF16).ap()
    k_d = nc.dram_tensor("k_scratch", [DIM, TOKENS], F32).ap()
    v_d = nc.dram_tensor("v_scratch", [TOKENS, DIM], F32).ap()
    attn_d = nc.dram_tensor("attn_scratch", [QUADS, GROUPS, P, 2 * SEQ], F32).ap()
    sorted_x = nc.dram_tensor("sorted_x", [ROUTED_TILES * RTILE, DIM], F32).ap()
    sorted_y = nc.dram_tensor("sorted_y", [ROUTED_TILES * RTILE, DIM], F32).ap()
    v_groups = v_d.rearrange("(n t p) d -> n p t d", t=GROUP_TILES, p=P)
    v_keys = v_d.rearrange("(n b j) c -> n j b c", b=GB, j=SEQ)
    x_pairs = x.rearrange("b s d -> (b s) d").rearrange("(n t p) d -> n p t d", t=2 * GROUP_TILES, p=P)
    attn_pairs = attn_d.rearrange("q (m g) (b c) t -> q m c (g b) t", g=2, b=4)
    sorted_x_tiles = sorted_x.rearrange("(k t p) d -> k p t d", t=2, p=P)
    sorted_y_tiles = sorted_y.rearrange("(k t p) d -> k p t d", t=2, p=P)

    assert (QUADS - 1) * (GROUPS - 3) == ROUTED_TILES

    with ExitStack() as ctx:
        def sb(name, shape, dt=F32):
            return ctx.enter_context(nc.sbuf_tensor(name, shape, dt))

        def sem(name):
            return ctx.enter_context(nc.semaphore(name))

        ident = sb("ident", [P, P])
        ones = sb("ones", [P, 512])
        lower = sb("lower", [P, P])
        zero_row = sb("zero_row", [P, P])
        head_mask = sb("head_mask", [P, HEADS])
        quad_mask = sb("quad_mask", [P, QH])
        sum_heads = sb("sum_heads", [P, 2, 32])
        rel_rows = sb("rel_rows", [P, HEADS, HEAD])
        rel_t = sb("rel_t", [P, NREL])
        rel_rest = sb("rel_rest", [P, NREL])
        rel_parts = sb("rel_parts", [P, 3, NREL], BF16)
        rel_stacks = sb("rel_stacks", [P, 2, NREL], BF16)
        head_of_quad = sb("head_of_quad", [P, QH])
        wq_s, wk_s, wv_s, wo_s = (sb(n, [DIM, DIM]) for n in ("wq_s", "wk_s", "wv_s", "wo_s"))
        wg_s = sb("wg_s", [DIM, P])
        bq_s, bk_s = sb("bq_s", [DIM, 1]), sb("bk_s", [DIM, 1])
        bv_s, bo_s = sb("bv_s", [P, DIM]), sb("bo_s", [P, DIM])
        w1s_s, w2s_s = sb("w1s_s", [DIM, INTER]), sb("w2s_s", [DIM, INTER])
        w3s_s = sb("w3s_s", [P, IC, DIM])
        expert_down = sb("expert_down", [P, EXPERTS])
        tile_starts = sb("tile_starts", [P, TOKENS // RTILE])
        tile_numbers = sb("tile_numbers", [P, ROUTED_TILES])

        big = sb("big", [P, 3 * TOKENS])
        pos_t = big[:, 0:2 * TOKENS].rearrange("p (r t) -> p r t", r=2)
        q_all = big[:, 2 * TOKENS:3 * TOKENS]
        acc = big[:, 0:TOKENS]
        xn2 = big[:, TOKENS:2 * TOKENS]
        xn2_t = big[:, 2 * TOKENS:3 * TOKENS]

        work = sb("work", [P, 10240])

        def ring(at, n, size):
            return work[:, at:at + n * size].rearrange("p (s f) -> p s f", s=n)

        x_in, ctx_in, xn = ring(0, 4, GTOK), ring(2048, 4, GTOK), ring(4096, 2, GTOK)
        xn_t, ctx_t = ring(5120, 2, GTOK), ring(6144, 2, GTOK)
        q_out, k_out, v_out = ring(7168, 2, GTOK), ring(8192, 2, GTOK), ring(9216, 2, GTOK)
        k_exp = ring(0, 2, 4 * GTOK)
        prob = ring(4096, 2, 2 * GTOK)
        prob_t = ring(6144, 2, 2 * GTOK)
        v_exp = work[:, 8192:9216].rearrange("p (s b r c) -> p s b r c", s=2, b=GB, r=2)
        v_g = work[:, 9216:9728].rearrange("p (s b c) -> p s b c", s=2, b=GB)
        den_r, attn_o = ring(9728, 2, 2 * SEQ), ring(9984, 2, 2 * SEQ)
        ln_stats = sb("ln_stats", [P, 4, GROUP_TILES, 6])
        ln_mv = sb("ln_mv", [P, 4, GROUP_TILES, 2])
        ln_std = sb("ln_std", [P, 4, GROUP_TILES])
        ln_rstd = sb("ln_rstd", [P, 4, GROUP_TILES])

        eps_s, warm_up = sb("eps_s", [P, 1]), sb("warm_up", [P, 1])
        wait_word = sb("wait_word", [P, 2])
        parity = sb("parity", [P, 2])

        x_in3, attn_in = ring(0, 4, GTOK), ring(2048, 4, GTOK)
        xn3_t = ring(4096, 2, GTOK)
        logits = work[:, 5120:5120 + 512].rearrange("p (t e) -> p t e", e=EXPERTS)
        hit = work[:, 5632:6144].rearrange("p (t e) -> p t e", e=EXPERTS)
        chosen = work[:, 6144:6656].rearrange("p (e t) -> p e t", e=EXPERTS)
        seen = work[:, 6656:7168].rearrange("p (e t) -> p e t", e=EXPERTS)
        place = work[:, 7168:7680].rearrange("p (e t) -> p e t", e=EXPERTS)
        starts_hit = work[:, 7680:7936].rearrange("p (e k) -> p e k", e=EXPERTS)
        tiles_hit = work[:, 7936:7936 + ROUTED_TILES * EXPERTS].rearrange("p (k e) -> p k e", e=EXPERTS)
        best = sb("best", [P, TILES])
        rank = sb("rank", [P, TILES])
        count = sb("count", [P, EXPERTS])
        n_tiles = sb("n_tiles", [P, EXPERTS])
        tiles_end = sb("tiles_end", [P, EXPERTS])
        base = sb("base", [P, EXPERTS])
        row_f = sb("row_f", [P, TILES])
        row_i = sb("row_i", [P, TILES], I32)
        expert_f = sb("expert_f", [P, ROUTED_TILES])
        expert_i = sb("expert_i", [P, ROUTED_TILES], I32)
        gate = ring(0, 2, GTOK)
        hidden_t = ring(1024, 2, IC * GTOK)
        rhidden_t = ring(5120, 2, IC * RTILE)
        with ExitStack() as attention:
            q_stack_0 = attention.enter_context(nc.sbuf_tensor("q_stack_0", [P, TOKENS], BF16))
        rx = sb("rx", [P, 2, RTILE])
        ry = sb("ry", [P, 2, RTILE])
        rw1, rw2, rw3 = (sb(n, [P, 2, INTER]) for n in ("rw1", "rw2", "rw3"))
        xb, xn3 = rw2, rw1
        y_in = ring(7168, 4, GTOK)

        with ExitStack() as attention:
            def of_attention(name, shape, dt=F32, scope=attention):
                return scope.enter_context(nc.sbuf_tensor(name, shape, dt))

            q_stack_1 = of_attention("q_stack_1", [P, TOKENS], BF16)
            q_stacks = [q_stack_0, q_stack_1]
            rel_wins = [of_attention(f"rel_win_{a}", [P, 2, NREL, 2], BF16) for a in range(2)]
            with ExitStack() as projection:
                q_parts = of_attention("q_parts", [P, 4, 3, GTOK], BF16, projection)
                q_rest = of_attention("q_rest", [P, 2, GTOK], F32, projection)
            pos_g = of_attention("pos_g", [P, 2, 2, GTOK])
            q_g = of_attention("q_g", [P, 2, GTOK])
            k_g = of_attention("k_g", [P, 2, GTOK])
            row_max = of_attention("row_max", [P, 2, GROUP_TILES * 2, 2])

        r_up_parts = sb("r_up_parts", [P, 2, 2, 2, INTER], F32R)
        up_parts = sb("up_parts", [P, 2, 2, INTER], F32R)
        x_hi, x_lo = sb("x_hi", [P, 2, GTOK], F32R), sb("x_lo", [P, 2, GTOK], F32R)
        rx_hi, rx_lo = sb("rx_hi", [P, 2, RTILE], F32R), sb("rx_lo", [P, 2, RTILE], F32R)

        ps = ctx.enter_context(nc.psum_tensor("ps", [P, 8, 512], F32))

        eps_made, sums_made = sem("eps_made"), sem("sums_made")
        consts_made, idents_made = sem("consts_made"), sem("idents_made")
        weights_loaded, wg_loaded, zeros_stored = sem("weights_loaded"), sem("wg_loaded"), sem("zeros_stored")
        rel_transposed, rel_copied = sem("rel_transposed"), sem("rel_copied")
        qkv_weights_loaded = sem("qkv_weights_loaded")
        ctx_loaded = [sem(f"ctx_loaded{s}") for s in range(4)]
        in_loaded = [sem(f"in_loaded{s}") for s in range(4)]
        stats_done, mv_done, std_done, rstd_done, ln_done = (sem(n) for n in (
            "stats_done", "mv_done", "std_done", "rstd_done", "ln_done"))
        in_transposed, xn_t_copied, ctx_t_copied = sem("in_transposed"), sem("xn_t_copied"), sem("ctx_t_copied")
        q_projected, k_projected, v_projected = sem("q_projected"), sem("k_projected"), sem("v_projected")
        q_copied, k_copied, v_copied, q_kept = sem("q_copied"), sem("k_copied"), sem("v_copied"), sem("q_kept")
        part1_made, rest_made, part2_made, part3_made = (sem(n) for n in ("part1_made", "rest_made", "part2_made", "part3_made"))
        parts_stored = [sem(f"parts_stored{s}") for s in range(4)]
        stacks_loaded, rel_step, windows_made = sem("stacks_loaded"), sem("rel_step"), sem("windows_made")
        kv_stored = [sem(f"kv_stored{s}") for s in range(2)]

        mask_made, pos_made = sem("mask_made"), sem("pos_made")
        pos_copied_act, pos_copied_dve = sem("pos_copied_act"), sem("pos_copied_dve")
        pos_loaded = [sem(f"pos_loaded{s}") for s in range(2)]
        q_picked = sem("q_picked")
        k_loaded = [sem(f"k_loaded{s}") for s in range(2)]
        v_loaded = [sem(f"v_loaded{s}") for s in range(2)]
        k_expanded, k_expanded_act, v_expanded = sem("k_expanded"), sem("k_expanded_act"), sem("v_expanded")
        scored, maxed, shifted, exped = sem("scored"), sem("maxed"), sem("shifted"), sem("exped")
        prob_turned, prob_t_copied = sem("prob_turned"), sem("prob_t_copied")
        attended, den_inverted, normed = sem("attended"), sem("den_inverted"), sem("normed")
        attn_stored = [sem(f"attn_stored{s}") for s in range(2)]

        res_loaded = [sem(f"res_loaded{s}") for s in range(2)]
        biased, o_projected, x2_done = sem("biased"), sem("o_projected"), sem("x2_done")
        stats2, mv2, std2, rstd2, ln2 = (sem(n) for n in ("stats2", "mv2", "std2", "rstd2", "ln2"))
        xn3_kept, xn3_turned, xn3_t_copied = sem("xn3_kept"), sem("xn3_turned"), sem("xn3_t_copied")
        logit_made, logit_copied = sem("logit_made"), sem("logit_copied")
        route_step, ranked, routed, scattered = sem("route_step"), sem("ranked"), sem("routed"), sem("scattered")
        rows_made = sem("rows_made")

        gate_made, up_made, gated, hidden_made = sem("gate_made"), sem("up_made"), sem("gated"), sem("hidden_made")
        down_made, added = sem("down_made"), sem("added")
        w_hi_made, w_lo_made, x_hi_made, x_lo_made = (sem(n) for n in ("w_hi_made", "w_lo_made", "x_hi_made", "x_lo_made"))
        rw_hi_made, rw_lo_made, rx_hi_made, rx_lo_made = (sem(n) for n in (
            "rw_hi_made", "rw_lo_made", "rx_hi_made", "rx_lo_made"))
        rx_loaded, up_loaded, down_loaded = ([sem(f"{n}{s}") for s in range(2)] for n in (
            "rx_loaded", "up_loaded", "down_loaded"))
        rx_turned = sem("rx_turned")
        r_gate_made = sem("r_gate_made")
        r_up_made, r_gated, r_hidden_made = sem("r_up_made"), sem("r_gated"), sem("r_hidden_made")
        r_down_made, ry_copied = sem("r_down_made"), sem("ry_copied")
        ry_stored = [sem(f"ry_stored{s}") for s in range(2)]
        y_gathered = [sem(f"y_gathered{s}") for s in range(4)]
        summed, out_stored = sem("summed"), sem("out_stored")

        N_QKV_WEIGHTS, N_WEIGHTS = 6, 9
        block = ctx.enter_context(nc.Block())

        def pairs(eng, step, first, last):
            with eng.Fori(0, (last - first) // 2) as m:
                for par in range(2):
                    step(m * 2 + (first + par), (first + par) % 2)

        def fours(eng, step, first, last):
            with eng.Fori(0, (last - first) // 4) as m:
                for par in range(4):
                    step(m * 4 + (first + par), (first + par) % 4)

        def early(n, depth=2):
            return isinstance(n, int) and n < depth

        def first_use(quad, n):
            return isinstance(quad, int) and early(n)

        def quads(eng, body):
            body(0)
            with eng.Fori(0, QUADS - 1) as m:
                body(m + 1)

        def round_of(n, slot, depth=2):
            return (n - slot) // depth + 1

        @block.sync
        def _(sp):
            def load_in(n, s):
                if not early(n, 4):
                    sp.wait_ge(ln_done, n - 3)
                sp.dma_start(x_in[:, s, :].rearrange("p (t d) -> p t d", d=DIM), x_rows[n]).then_inc(in_loaded[s], 16)
                if not early(n, 4):
                    sp.wait_ge(in_transposed, n - 3)
                sp.dma_start(ctx_in[:, s, :].rearrange("p (t d) -> p t d", d=DIM), ctx_rows[n]).then_inc(ctx_loaded[s], 16)

            load_in(0, 0)
            load_in(1, 1)
            for dst, src in ((wq_s[:, :], wq), (wk_s[:, :], wk), (wv_s[:, :], wv),
                             (bq_s[:, :], bq.rearrange("(c a) -> c a", a=1)),
                             (bk_s[:, :], bk.rearrange("(c a) -> c a", a=1)),
                             (bv_s[:, :], bv.rearrange("(a c) -> a c", a=1).to_broadcast([P, DIM])),
                             ):
                sp.dma_start(dst, src).then_inc(qkv_weights_loaded, 16)
            load_in(2, 2)
            load_in(3, 3)
            for dst, src in ((wo_s[:, :], wo),
                             (bo_s[:, :], bo.rearrange("(a c) -> a c", a=1).to_broadcast([P, DIM])),
                             (w1s_s[:, :], w1s), (w2s_s[:, :], w2s),
                             (w3s_s[:, :, :], w3s.rearrange("(c p) d -> p c d", p=P)),
                             ):
                sp.dma_start(dst, src).then_inc(weights_loaded, 16)
            for h in range(0, HEADS, 4):
                sp.dma_start(rel_rows[:, h:h + 4, :],
                             rel_emb[1:NREL + 1, :].rearrange("r (a d) -> r a d", a=1).to_broadcast([NREL, 4, HEAD]),
                             ).then_inc(weights_loaded, 16)

            def load_stack(quad, a, block, at, size):
                sp.dma_start(q_stacks[a][QF * block:QF * block + QF, at:at + size],
                             q_parts_d[bass.ds(quad * QF, QF), Q_PARTS[a][block], at:at + size]).then_inc(stacks_loaded, 16)

            def load_chunk(chunk):
                for s in range(4):
                    sp.wait_ge(parts_stored[s], 16 * (chunk + 1))
                for a in range(2):
                    for block in range(4):
                        load_stack(0, a, block, chunk * (TOKENS // CHUNKS), TOKENS // CHUNKS)
            fours(sp, load_in, 4, GROUPS - 4)
            load_chunk(0)
            fours(sp, load_in, GROUPS - 4, GROUPS)
            sp.wait_ge(consts_made, 1)
            sp.dma_start(wg_s[:, 0:EXPERTS], Wg).then_inc(wg_loaded, 16)
            for chunk in range(1, CHUNKS - 1):
                load_chunk(chunk)
            for part, made in enumerate((part1_made, part2_made, part3_made)):
                sp.wait_ge(made, GROUPS)
                for a in range(2):
                    for block in range(4):
                        if Q_PARTS[a][block] == part:
                            sp.dma_start(q_stacks[a][QF * block:QF * block + QF, TOKENS - 4 * GTOK:TOKENS].rearrange(
                                "c (g t) -> c g t", g=4), q_parts[0:QF, :, part, :]).then_inc(stacks_loaded, 16)
            sp.wait_ge(stacks_loaded, 16 * 8 * CHUNKS)
            for s in range(4):
                sp.wait_ge(parts_stored[s], 16 * (GROUPS // 4))
            for s in range(2):
                sp.wait_ge(kv_stored[s], 32 * GROUPS // 2)

            def load_k(quad, n, s):
                if not first_use(quad, n):
                    sp.wait_ge(k_expanded, quad * GROUPS + n - 1)
                    sp.wait_ge(k_expanded_act, quad * GROUPS + n - 1)
                sp.dma_start(k_g[:, s, :], k_d[:, bass.ds(n * GTOK, GTOK)]).then_inc(k_loaded[s], 16)

            def load_pos(n, s):
                sp.dma_start(pos_g[:, s, :, :], pos_t[:, :, bass.ds(n * GTOK, GTOK)]).then_inc(pos_loaded[s], 16)

            def load_v(n, s, first_feature):
                for hp in range(2):
                    sp.dma_start(v_g[hp:P:2, s, :, :],
                                 v_keys[n][:, :, bass.ds(first_feature, QF)]).then_inc(v_loaded[s], 16)

            def store_attn(quad, n, s):
                sp.wait_ge(normed, quad * GROUPS + n + 1)
                sp.dma_start(attn_d[quad, n], attn_o[:, s, :]).then_inc(attn_stored[s], 16)

            def first_groups(quad):
                follows = not isinstance(quad, int)
                for n in range(2):
                    if follows:
                        sp.wait_ge(v_expanded, quad * GROUPS + n - 1)
                    load_k(quad, n, n)
                    load_v(n, n, quad * QF)
                    if follows:
                        store_attn(quad - 1, GROUPS - 4 + n, n)
                sp.wait_ge(pos_copied_act, quad * (POS_BANKS // 2) + POS_BANKS // 2)
                sp.wait_ge(pos_copied_dve, quad * (POS_BANKS // 2) + POS_BANKS // 2)
                for n in range(2):
                    load_pos(n, n)
                for n in range(2):
                    if follows:
                        store_attn(quad - 1, GROUPS - 2 + n, n)

            def other_groups(quad, next_stacks):
                def step(n, s):
                    sp.wait_ge(scored, quad * GROUPS + n - 1)
                    load_k(quad, n, s)
                    load_pos(n, s)
                    sp.wait_ge(v_expanded, quad * GROUPS + n - 1)
                    load_v(n, s, quad * QF)
                    if not early(n, 4):
                        store_attn(quad, n - 4, s)
                    if next_stacks and not early(n, 3):
                        sp.dma_start(sorted_x_tiles[quad * (GROUPS - 3) + n - 3],
                                     zero_row[:, :].rearrange("p (a d) -> p a d", a=1).to_broadcast([P, 2, P]),
                                     ).then_inc(zeros_stored, 16)
                for n in range(2, 10):
                    step(n, n % 2)
                    if next_stacks:
                        load_stack(quad + 1, (n - 2) // 4, (n - 2) % 4, 0, TOKENS)
                pairs(sp, step, 10, GROUPS)
            first_groups(0)
            with sp.Fori(0, QUADS - 1) as m:
                other_groups(m, True)
                first_groups(m + 1)
            other_groups(QUADS - 1, False)
            def load_res(m, half):
                if not early(m):
                    sp.wait_ge(x2_done, m * 2 - 2)
                sp.dma_start(x_in3[:, 2 * half:2 * half + 2, :].rearrange("p g (t d) -> p (g t) d", d=DIM),
                             x_pairs[m]).then_inc(res_loaded[half], 16)
                for quad in range(QUADS):
                    sp.dma_start(attn_in[32 * quad:32 * quad + 32, 2 * half:2 * half + 2, :].rearrange(
                        "c g (b t) -> c (g b) t", b=4), attn_pairs[quad, m]).then_inc(res_loaded[half], 16)
            store_attn(QUADS - 1, GROUPS - 4, 0)
            sp.wait_ge(scored, QUADS * GROUPS)
            for s in range(2):
                sp.wait_ge(attn_stored[s], (QUADS - 1) * (16 * GROUPS // 2) + 2 * 16)
            load_res(0, 0)
            store_attn(QUADS - 1, GROUPS - 3, 1)
            load_res(1, 1)
            store_attn(QUADS - 1, GROUPS - 2, 0)
            store_attn(QUADS - 1, GROUPS - 1, 1)
            for s in range(2):
                sp.wait_ge(attn_stored[s], QUADS * (16 * GROUPS // 2))
            pairs(sp, load_res, 2, GROUPS // 2)

            sp.wait_ge(routed, 1)

            def expert_of(k):
                return sp.value_load(expert_i[0:1, bass.ds(k, 1)], min_val=0, max_val=EXPERTS - 1)

            def load_rows(k, s):
                sp.dma_start(rx[:, s, :].rearrange("p (t d) -> p t d", d=DIM), sorted_x_tiles[k]).then_inc(rx_loaded[s], 16)

            def load_up(e, s):
                sp.dma_start(rw1[:, s, :], W1[e]).then_inc(up_loaded[s], 16)
                sp.dma_start(rw2[:, s, :], W2[e]).then_inc(up_loaded[s], 16)

            def load_down(e, s):
                sp.dma_start(rw3[:, s, :].rearrange("p (c d) -> p c d", d=DIM),
                             W3[e].rearrange("(c p) d -> p c d", p=P)).then_inc(down_loaded[s], 16)

            def store_tile(k, s):
                sp.wait_ge(ry_copied, k + 1)
                sp.dma_start(sorted_y_tiles[k], ry[:, s, :].rearrange("p (t d) -> p t d", d=DIM)).then_inc(ry_stored[s], 16)

            def step(k, s):
                if isinstance(k, int) and k >= ROUTED_TILES - 2:
                    down_expert = expert_of(k)
                else:
                    sp.wait_ge(rx_turned, k + 1)
                    load_rows(k + 2, s)
                    up_expert, down_expert = expert_of(k + 2), expert_of(k)
                    sp.wait_ge(rw_lo_made, k * 2 + 2)
                    load_up(up_expert, s)
                if not early(k):
                    sp.wait_ge(r_down_made, k - 1)
                load_down(down_expert, s)
                if not early(k):
                    store_tile(k - 2, s)
            for k in range(2):
                load_up(expert_of(k), k)
            sp.wait_ge(scattered, 16 * TILES)
            for k in range(2):
                load_rows(k, k)
            step(0, 0)
            step(1, 1)
            pairs(sp, step, 2, ROUTED_TILES - 3)
            for k in range(ROUTED_TILES - 3, ROUTED_TILES):
                step(k, k % 2)
            for k in range(ROUTED_TILES - 2, ROUTED_TILES):
                store_tile(k, k % 2)

            with sp.Fori(0, GROUPS) as n:
                sp.wait_ge(summed, n + 1)
                sp.dma_start(out_rows[n], acc[:, bass.ds(n * GTOK, GTOK)].rearrange("p (t d) -> p t d", d=DIM),
                             ).then_inc(out_stored, 16)
            sp.wait_ge(out_stored, 16 * GROUPS)

        @block.gpsimd
        def _(pool):
            pool.memset(wg_s[:, :], 0.0)
            pool.memset(zero_row[:, :], 0.0).then_inc(consts_made, 1)
            pool.memset(ident[:, :], 0.0).then_inc(idents_made, 1)
            pool.memset(ones[:, :], 1.0).then_inc(idents_made, 1)
            pool.memset(sum_heads[:, :, :], 0.0).then_inc(idents_made, 1)
            pool.wait_ge(idents_made, 3)
            pool.affine_select(out=ident[:, :], in_=ident[:, :], compare_op=ALU.not_equal, fill=1.0,
                               base=0, pattern=[[-1, P]], channel_multiplier=1).then_inc(idents_made, 1)
            pool.affine_select(out=lower[:, :], in_=ones[:, 0:P], compare_op=ALU.is_gt, fill=0.0,
                               base=0, pattern=[[1, P]], channel_multiplier=-1).then_inc(idents_made, 1)
            pool.affine_select(out=head_mask[:, :], in_=ones[:, 0:HEADS], compare_op=ALU.is_ge, fill=0.0,
                               base=0, pattern=[[-HEAD, HEADS]], channel_multiplier=1).then_inc(idents_made, 1)
            pool.wait_ge(idents_made, 6)
            pool.affine_select(out=head_mask[:, :], in_=head_mask[:, :], compare_op=ALU.is_ge, fill=0.0,
                               base=HEAD - 1, pattern=[[HEAD, HEADS]], channel_multiplier=-1).then_inc(idents_made, 1)
            pool.iota(expert_down[:, :], pattern=[[-1, EXPERTS]], base=EXPERTS, channel_multiplier=0,
                      allow_small_or_imprecise_dtypes=True).then_inc(idents_made, 1)
            pool.iota(tile_starts[:, :], pattern=[[RTILE, TOKENS // RTILE]], base=0, channel_multiplier=0,
                      allow_small_or_imprecise_dtypes=True).then_inc(idents_made, 1)
            pool.iota(tile_numbers[:, :], pattern=[[1, ROUTED_TILES]], base=0, channel_multiplier=0,
                      allow_small_or_imprecise_dtypes=True).then_inc(idents_made, 1)

            def part(n, s, j):
                pool.wait_ge(part1_made, n + 1)
                if not early(n):
                    pool.wait_ge(part3_made, n - 1)
                pool.tensor_tensor(q_rest[:, s, :], q_out[:, s, :], q_parts[:, j, 0, :], ALU.subtract).then_inc(rest_made, 1)

            def third_part(n, s, j):
                pool.wait_ge(part2_made, n + 1)
                pool.tensor_tensor(q_parts[:, j, 2, :], q_rest[:, s, :], q_parts[:, j, 1, :], ALU.subtract).then_inc(part3_made, 1)

            def step(n, j):
                part(n, j % 2, j)
                if not early(n, 1):
                    third_part(n - 1, (j + 1) % 2, (j + 3) % 4)
            for n in range(4):
                step(n, n)
            fours(pool, step, 4, GROUPS)
            third_part(GROUPS - 1, 1, 3)

            def pick_q(g, n, s):
                if not early(g):
                    pool.wait_ge(scored, g - 1)
                pool.tensor_tensor(q_g[:, s, :], q_all[:, bass.ds(n * GTOK, GTOK)], ones[:, :], ALU.mult).then_inc(q_picked, 1)
            pool.wait_ge(q_kept, GROUPS)
            pool.wait_ge(stacks_loaded, 16 * 8 * CHUNKS)
            for s in range(4):
                pool.wait_ge(parts_stored[s], 16 * (GROUPS // 4))

            pool.wait_ge(sums_made, 5)
            def expand_v(g, s):
                pool.wait_ge(v_loaded[s], (g - s) * 16 + 32)
                if not early(g):
                    pool.wait_ge(attended, g - 1)
                for pair in range(2):
                    last = pool.tensor_tensor(v_exp[:, s, :, pair, :], v_g[:, s, :, :],
                                              sum_heads[:, pair:pair + 1, :].to_broadcast([P, GB, 32]), ALU.mult)
                last.then_inc(v_expanded, 1)
            def attend_quad(quad):
                def step(n, s):
                    pick_q(quad * GROUPS + n + 1, n + 1, 1 - s)
                    expand_v(quad * GROUPS + n, s)
                pick_q(quad * GROUPS, 0, 0)
                step(0, 0)
                step(1, 1)
                pairs(pool, step, 2, GROUPS - 2)
                step(GROUPS - 2, 0)
                expand_v(quad * GROUPS + GROUPS - 1, 1)
            quads(pool, attend_quad)

            def stage3(n, j):
                s = j % 2
                pool.wait_ge(res_loaded[j // 2], round_of(n, j, 4) * (16 + 16 * QUADS))
                if not early(n):
                    pool.wait_ge(x2_done, n - 1)
                for t in range(GROUP_TILES):
                    last = pool.tensor_tensor(xb[:, s, t * DIM:(t + 1) * DIM], x_in3[:, j, t * DIM:(t + 1) * DIM],
                                              bo_s[:, :], ALU.add)
                last.then_inc(biased, 1)
            for n in range(4):
                stage3(n, n)
            fours(pool, stage3, 4, GROUPS)

            pool.wait_ge(rows_made, 1)
            pool.wait_ge(zeros_stored, 16 * ROUTED_TILES)
            pool.wait_ge(xn3_kept, GROUPS)
            for t in range(TILES):
                pool.indirect_dma_start(
                    out=sorted_x, out_offset=bass.IndirectOffsetOnAxis(ap=row_i[:, t:t + 1], axis=0),
                    in_=xn2[:, t * P:(t + 1) * P], in_offset=None).then_inc(scattered, 16)

            for s in range(2):
                pool.wait_ge(ry_stored[s], 16 * ((ROUTED_TILES + 1 - s) // 2))
            for n in range(GROUPS):
                s = n % 4
                if n >= 4:
                    pool.wait_ge(summed, n - 3)
                for t in range(GROUP_TILES):
                    tt = n * GROUP_TILES + t
                    pool.indirect_dma_start(
                        out=y_in[:, s, t * DIM:(t + 1) * DIM], out_offset=None, in_=sorted_y,
                        in_offset=bass.IndirectOffsetOnAxis(ap=row_i[:, tt:tt + 1], axis=0)).then_inc(y_gathered[s], 16)

        @block.scalar
        def _(act):
            act.wait_ge(eps_made, 1)
            act.activation(warm_up[:, :], eps_s[:, :], ACT.Sqrt)

            def deviation(n, j, var_done, done):
                act.wait_ge(var_done, n + 1)
                act.activation(ln_std[:, j, :], ln_mv[:, j, :, 1], ACT.Sqrt, bias=eps_s[:, 0:1]).then_inc(done, 1)

            def copy_in(n, s):
                act.wait_ge(in_transposed, n + 1)
                if not early(n):
                    act.wait_ge(v_projected, n - 1)
                act.activation(xn_t[:, s, :], ps[:, 0, :], ACT.Identity).then_inc(xn_t_copied, 1)
                act.activation(ctx_t[:, s, :], ps[:, 1, :], ACT.Identity).then_inc(ctx_t_copied, 1)

            def project(n, s, j):
                if early(n, 1):
                    act.wait_ge(qkv_weights_loaded, 16 * N_QKV_WEIGHTS)
                if not early(n):
                    act.wait_ge(kv_stored[s], round_of(n, s) * 32 - 32)
                    act.wait_ge(q_kept, n - 1)
                    act.wait_ge(rest_made, n - 1)
                act.wait_ge(q_projected, n + 1)
                act.activation(q_out[:, s, :], ps[:, 2, :], ACT.Identity, bias=bq_s[:, 0:1]).then_inc(q_copied, 1)
                act.wait_ge(k_projected, n + 1)
                act.activation(k_out[:, s, :], ps[:, 3, :], ACT.Identity, bias=bk_s[:, 0:1]).then_inc(k_copied, 1)
                act.wait_ge(q_copied, n + 1)
                if not early(n, 4):
                    act.wait_ge(parts_stored[j], round_of(n, j, 4) * 16 - 16)
                act.activation(q_parts[:, j, 0, :], q_out[:, s, :], ACT.Identity).then_inc(part1_made, 1)

            def second_part(n, s, j):
                act.wait_ge(rest_made, n + 1)
                act.activation(q_parts[:, j, 1, :], q_rest[:, s, :], ACT.Identity).then_inc(part2_made, 1)

            def store_parts(n, j):
                act.wait_ge(part3_made, n + 1)
                act.dma_start(q_parts_d[:, :, bass.ds(n * GTOK, GTOK)], q_parts[:, j, :, :]).then_inc(parts_stored[j], 16)

            def store_kv(n, s):
                act.wait_ge(k_copied, n + 1)
                act.dma_start(k_d[:, bass.ds(n * GTOK, GTOK)], k_out[:, s, :]).then_inc(kv_stored[s], 16)
                act.wait_ge(v_copied, n + 1)
                act.dma_start(v_groups[n], v_out[:, s, :].rearrange("p (t d) -> p t d", d=DIM)).then_inc(kv_stored[s], 16)

            def step(n, j, last=False):
                if not last:
                    deviation(n + 1, (j + 1) % 4, mv_done, std_done)
                copy_in(n, j % 2)
                if not early(n, 1):
                    project(n - 1, (j + 1) % 2, (j + 3) % 4)
                if not early(n, 2):
                    second_part(n - 2, j % 2, (j + 2) % 4)
                    store_kv(n - 2, j % 2)
                if not early(n, 3):
                    store_parts(n - 3, (j + 1) % 4)
            deviation(0, 0, mv_done, std_done)
            for n in range(4):
                step(n, n)
            fours(act, step, 4, GROUPS - 4)
            for n in range(GROUPS - 4, GROUPS):
                step(n, n % 4, last=n == GROUPS - 1)
            project(GROUPS - 1, 1, 3)
            second_part(GROUPS - 2, 0, 2)
            store_kv(GROUPS - 2, 0)
            store_parts(GROUPS - 3, 1)
            second_part(GROUPS - 1, 1, 3)
            act.wait_ge(stacks_loaded, 16 * 8 * CHUNKS)
            store_kv(GROUPS - 1, 1)
            store_parts(GROUPS - 2, 2)
            store_parts(GROUPS - 1, 3)

            def exp(quad, n, s):
                act.wait_ge(shifted, quad * GROUPS + n + 1)
                act.activation(prob[:, s, :], prob[:, s, :], ACT.Exp, scale=SCALE).then_inc(exped, 1)

            def copy_prob_t(quad, n, s):
                act.wait_ge(prob_turned, quad * GROUPS + n + 1)
                if not first_use(quad, n):
                    act.wait_ge(attended, quad * GROUPS + n - 1)
                act.activation(prob_t[:, s, :].rearrange("p (r t) -> p r t", r=2), ps[:, 4:6, :],
                               ACT.Identity).then_inc(prob_t_copied, 1)

            def expand_k(quad, n, s):
                act.wait_ge(k_loaded[s], (quad * (GROUPS // 2) + round_of(n, s)) * 16)
                if not first_use(quad, n):
                    act.wait_ge(scored, quad * GROUPS + n - 1)
                out = k_exp[:, s, :].rearrange("p (b r j h) -> p b r j h", r=2, j=SEQ, h=2)
                for h in range(2, QH):
                    last = act.activation(out[:, :, h // 2, :, h % 2],
                                          k_g[:, s, :].rearrange("p (b j) -> p b j", j=SEQ), ACT.Identity,
                                          scale=quad_mask[:, h:h + 1])
                last.then_inc(k_expanded_act, 1)

            def attend_quad(quad):
                follows = not isinstance(quad, int)
                if follows:
                    copy_prob_t(quad - 1, GROUPS - 2, 0)
                act.wait_ge(mask_made, quad + 1)
                for k in range(0, POS_BANKS, 2):
                    act.wait_ge(pos_made, quad * POS_BANKS + (k + 1))
                    i = 4 * (k % (SEQ // 4))
                    act.activation(
                        pos_t[:, k // (SEQ // 4), :].rearrange("p (b i) -> p i b", i=SEQ)[:, i:i + 4, :],
                        ps[:, k % 4, :].rearrange("p (i b) -> p i b", i=4), ACT.Identity).then_inc(pos_copied_act, 1)
                    if k == 0 and follows:
                        exp(quad - 1, GROUPS - 1, 1)
                    if k == 10 and follows:
                        copy_prob_t(quad - 1, GROUPS - 1, 1)
                    if k == 16:
                        expand_k(quad, 0, 0)
                    if k == 22:
                        expand_k(quad, 1, 1)
                exp(quad, 0, 0)
                expand_k(quad, 2, 0)

                def step(n, s):
                    copy_prob_t(quad, n - 2, s)
                    exp(quad, n - 1, 1 - s)
                    expand_k(quad, n + 1, 1 - s)
                step(2, 0)
                step(3, 1)
                pairs(act, step, 4, GROUPS - 2)
                step(GROUPS - 2, 0)
                copy_prob_t(quad, GROUPS - 3, 1)
                exp(quad, GROUPS - 2, 0)
            quads(act, attend_quad)
            copy_prob_t(QUADS - 1, GROUPS - 2, 0)
            exp(QUADS - 1, GROUPS - 1, 1)
            copy_prob_t(QUADS - 1, GROUPS - 1, 1)

            act.wait_ge(weights_loaded, 16 * N_WEIGHTS)
            for s in range(2):
                act.wait_ge(attn_stored[s], QUADS * (16 * GROUPS // 2))
            for m, w in enumerate((w1s_s, w2s_s)):
                act.activation(up_parts[:, m, 0, :], w[:, :], ACT.Identity).then_inc(w_hi_made, 1)

            def turned(n, s):
                act.wait_ge(xn3_turned, n + 1)
                act.activation(xn2_t[:, bass.ds(n * GTOK, GTOK)], ps[:, 2 + s, :], ACT.Identity)
                if not early(n):
                    act.wait_ge(logit_made, n - 1)
                act.activation(xn3_t[:, s, :], ps[:, 2 + s, :], ACT.Identity).then_inc(xn3_t_copied, 1)

            def keep_xn(n, s):
                act.wait_ge(ln2, n + 1)
                act.activation(xn2[:, bass.ds(n * GTOK, GTOK)], xn3[:, s, :], ACT.Identity).then_inc(xn3_kept, 1)

            def step(n, j, last=False):
                if not last:
                    deviation(n + 1, (j + 1) % 4, mv2, std2)
                keep_xn(n, j % 2)
                turned(n, j % 2)
            deviation(0, 0, mv2, std2)
            for n in range(4):
                step(n, n)
            fours(act, step, 4, GROUPS - 4)
            for n in range(GROUPS - 4, GROUPS):
                step(n, n % 4, last=n == GROUPS - 1)

            def gelu(n, s):
                for c in range(IC):
                    act.wait_ge(gate_made, n * IC + (c + 1))
                    if not (isinstance(n, int) and n == 0 and c < 2):
                        act.wait_ge(hidden_made, n * IC + (c - 1))
                    act.activation(gate[:, c % 2, :], ps[:, c % 2, :], ACT.Gelu).then_inc(gated, 1)
            gelu(0, 0)
            gelu(1, 1)
            def high_w(k, s, m):
                act.wait_ge(up_loaded[s], round_of(k, s) * 32)
                if not early(k):
                    act.wait_ge(r_up_made, (k - 1) * IC)
                act.activation(r_up_parts[:, s, m, 0, :], (rw1, rw2)[m][:, s, :], ACT.Identity).then_inc(rw_hi_made, 1)

            high_w(0, 0, 0)
            high_w(0, 0, 1)
            high_w(1, 1, 0)
            pairs(act, gelu, 2, FRONT)

            def high_rx(k, s):
                act.wait_ge(rx_turned, k + 1)
                if not early(k):
                    act.wait_ge(r_up_made, (k - 1) * IC)
                act.activation(rx_hi[:, s, :], ps[:, 6, 0:RTILE], ACT.Identity).then_inc(rx_hi_made, 1)

            def expert(k, s):
                for c in range(IC):
                    act.wait_ge(r_gate_made, k * IC + (c + 1))
                    if not (isinstance(k, int) and k == 0 and c < 2):
                        act.wait_ge(r_hidden_made, k * IC + (c - 1))
                    act.activation(gate[:, c % 2, 0:RTILE], ps[:, c % 2, 0:RTILE], ACT.Gelu).then_inc(r_gated, 1)
                    if c == 1 and not (isinstance(k, int) and k == ROUTED_TILES - 1):
                        high_w(k + 1, 1 - s, 1)
                        high_rx(k + 1, 1 - s)
                if not (isinstance(k, int) and k >= ROUTED_TILES - 2):
                    high_w(k + 2, s, 0)
            high_rx(0, 0)
            expert(0, 0)
            pairs(act, expert, 1, ROUTED_TILES - 2)
            expert(ROUTED_TILES - 2, 1)
            expert(ROUTED_TILES - 1, 0)
            pairs(act, gelu, FRONT, GROUPS)

        @block.tensor
        def _(pe):
            pe.wait_ge(idents_made, 7)

            def turn_in(n, j):
                s = j % 2
                pe.wait_ge(ctx_loaded[j], round_of(n, j, 4) * 16)
                pe.wait_ge(ln_done, n + 1)
                if not early(n, 1):
                    pe.wait_ge(xn_t_copied, n)
                    pe.wait_ge(ctx_t_copied, n)
                for t in range(GROUP_TILES):
                    pe.transpose(ps[:, 0, t * P:(t + 1) * P], xn[:, s, t * DIM:(t + 1) * DIM], ident[:, :])
                    last = pe.transpose(ps[:, 1, t * P:(t + 1) * P], ctx_in[:, j, t * DIM:(t + 1) * DIM], ident[:, :])
                last.then_inc(in_transposed, 1)

            def project(n, s):
                if early(n, 1):
                    pe.wait_ge(qkv_weights_loaded, 16 * N_QKV_WEIGHTS)
                pe.wait_ge(xn_t_copied, n + 1)
                pe.wait_ge(ctx_t_copied, n + 1)
                if not early(n, 1):
                    pe.wait_ge(q_copied, n)
                    pe.wait_ge(k_copied, n)
                    pe.wait_ge(v_copied, n)
                pe.matmul(ps[:, 2, :], wq_s[:, :], xn_t[:, s, :], start=True, stop=True).then_inc(q_projected, 1)
                pe.matmul(ps[:, 3, :], wk_s[:, :], ctx_t[:, s, :], start=True, stop=True).then_inc(k_projected, 1)
                for t in range(GROUP_TILES):
                    last = pe.matmul(ps[:, 4, t * P:(t + 1) * P], ctx_t[:, s, t * P:(t + 1) * P], wv_s[:, :],
                                     start=True, stop=True)
                last.then_inc(v_projected, 1)

            turn_in(0, 0)

            def step(n, j):
                turn_in(n + 1, (j + 1) % 4)
                project(n, j % 2)
            for n in range(4):
                step(n, n)
            fours(pe, step, 4, GROUPS - 4)
            for n in range(GROUPS - 4, GROUPS - 1):
                step(n, n % 4)
            project(GROUPS - 1, 1)
            pe.wait_ge(weights_loaded, 16 * N_WEIGHTS)
            pe.transpose(ps[:, 7, 0:P], rel_rows[:, :, :].rearrange("p h d -> p (h d)"), ident[:, :]).then_inc(rel_transposed, 1)
            pe.wait_ge(sums_made, 5)
            pe.wait_ge(v_copied, GROUPS)
            pe.wait_ge(k_copied, GROUPS)

            def score(quad, n, s):
                g = quad * GROUPS + n
                pe.wait_ge(pos_loaded[s], (quad * (GROUPS // 2) + round_of(n, s)) * 16)
                pe.wait_ge(q_picked, g + 1)
                pe.wait_ge(k_expanded, g + 1)
                pe.wait_ge(k_expanded_act, g + 1)
                if not early(n):
                    pe.wait_ge(shifted, g - 1)
                for t in range(GROUP_TILES):
                    bank, c = 2 * s + t // 2, 256 * (t % 2)
                    for pair in range(2):
                        pe.matmul(ps[:, bank, c + P * pair:c + P * pair + P], pos_g[:, s, pair, t * P:(t + 1) * P],
                                  ident[:, :], start=(t % 2 == 0 and pair == 0), stop=False, is_transpose=True,
                                  skip_group_check=True)
                    for b in range(2):
                        last = pe.matmul(ps[64 * b:64 * b + 64, bank, c:c + 256],
                                         q_g[:, s, t * P + 64 * b:t * P + 64 * b + 64],
                                         k_exp[:, s, (2 * t + b) * 256:(2 * t + b + 1) * 256],
                                         start=False, stop=True, skip_group_check=True)
                last.then_inc(scored, 1)

            def turn_prob(quad, n, s):
                g = quad * GROUPS + n
                pe.wait_ge(exped, g + 1)
                if not (first_use(quad, n) and n == 0):
                    pe.wait_ge(prob_t_copied, g)
                for pair in range(2):
                    for t in range(GROUP_TILES):
                        last = pe.transpose(ps[:, 4 + pair, t * P:(t + 1) * P],
                                            prob[:, s, t * 256 + pair * P:t * 256 + pair * P + P], ident[:, :])
                last.then_inc(prob_turned, 1)

            def attend(quad, n, s):
                g = quad * GROUPS + n
                pe.wait_ge(prob_t_copied, g + 1)
                pe.wait_ge(v_expanded, g + 1)
                if not first_use(quad, n):
                    pe.wait_ge(normed, g - 1)
                for b2 in range(2):
                    for pair in range(2):
                        for b4 in range(4):
                            b = 2 * b4 + b2
                            pe.matmul(ps[32 * b4:32 * b4 + 32, 6 + s, 64 * b2:64 * b2 + 64], v_exp[:, s, b, pair, :],
                                      prob_t[:, s, pair * GTOK + b * SEQ:pair * GTOK + (b + 1) * SEQ],
                                      start=(pair == 0), stop=(pair == 1), tile_position=(0, 32 * b4))
                for pair in range(2):
                    for b4 in range(4):
                        at = pair * GTOK + b4 * 2 * SEQ
                        last = pe.matmul(ps[32 * b4:32 * b4 + 32, 6 + s, P:2 * P], sum_heads[:, pair, :],
                                         prob_t[:, s, at:at + 2 * SEQ], start=(pair == 0), stop=(pair == 1),
                                         tile_position=(0, 32 * b4))
                last.then_inc(attended, 1)

            def attend_quad(quad):
                follows = not isinstance(quad, int)
                pe.wait_ge(windows_made, 1)
                pe.wait_ge(stacks_loaded, quad * (16 * 8) + 16 * 8 * CHUNKS)
                for k in range(POS_BANKS):
                    if k >= 4:
                        copied = pos_copied_act if k % 2 == 0 else pos_copied_dve
                        pe.wait_ge(copied, quad * (POS_BANKS // 2) + ((k - 4) // 2 + 1))
                    elif follows and k % 2 == 0:
                        pe.wait_ge(shifted, quad * GROUPS - 1 + k // 2)
                    pair, i0 = k // (SEQ // 4), 4 * (k % (SEQ // 4))
                    for i in range(i0, i0 + 4):
                        lo = MAX_REL - 1 - i
                        for a in range(2):
                            last = pe.matmul(ps[:, k % 4, (i - i0) * P:(i - i0 + 1) * P],
                                             rel_wins[a][:, pair, lo:lo + SEQ, :].rearrange("p j h -> p (j h)"),
                                             q_stacks[a][:, :].rearrange("p (b i) -> p i b", i=SEQ)[:, i, :],
                                             start=(a == 0), stop=(a == 1))
                    last.then_inc(pos_made, 1)
                    if k == 7 and follows:
                        turn_prob(quad - 1, GROUPS - 1, 1)
                if follows:
                    attend(quad - 1, GROUPS - 2, 0)
                    attend(quad - 1, GROUPS - 1, 1)
                pe.wait_ge(pos_copied_act, quad * (POS_BANKS // 2) + POS_BANKS // 2)
                pe.wait_ge(pos_copied_dve, quad * (POS_BANKS // 2) + POS_BANKS // 2)
                score(quad, 0, 0)
                score(quad, 1, 1)
                turn_prob(quad, 0, 0)

                def step(n, s):
                    score(quad, n, s)
                    turn_prob(quad, n - 1, 1 - s)
                    attend(quad, n - 2, s)
                step(2, 0)
                step(3, 1)
                pairs(pe, step, 4, GROUPS)
            quads(pe, attend_quad)
            turn_prob(QUADS - 1, GROUPS - 1, 1)
            attend(QUADS - 1, GROUPS - 2, 0)
            attend(QUADS - 1, GROUPS - 1, 1)

            pe.wait_ge(normed, QUADS * GROUPS)
            pe.wait_ge(wg_loaded, 16)

            def project_out(n, j):
                s = j % 2
                pe.wait_ge(res_loaded[j // 2], round_of(n, j, 4) * (16 + 16 * QUADS))
                if not early(n):
                    pe.wait_ge(x2_done, n - 1)
                for t in range(GROUP_TILES):
                    last = pe.matmul(ps[:, s, t * DIM:(t + 1) * DIM], attn_in[:, j, t * P:(t + 1) * P], wo_s[:, :],
                                     start=True, stop=True)
                last.then_inc(o_projected, 1)

            def turn_xn(n, s):
                pe.wait_ge(ln2, n + 1)
                if not early(n):
                    pe.wait_ge(xn3_t_copied, n - 1)
                for t in range(GROUP_TILES):
                    last = pe.transpose(ps[:, 2 + s, t * P:(t + 1) * P], xn3[:, s, t * DIM:(t + 1) * DIM], ident[:, :])
                last.then_inc(xn3_turned, 1)

            def make_logits(n, s):
                pe.wait_ge(xn3_t_copied, n + 1)
                if not early(n):
                    pe.wait_ge(logit_copied, n - 1)
                for t in range(GROUP_TILES):
                    last = pe.matmul(ps[:, 4 + s, t * P:(t + 1) * P], xn3_t[:, s, t * P:(t + 1) * P], wg_s[:, :],
                                     start=True, stop=True)
                last.then_inc(logit_made, 1)
            def step(n, j):
                project_out(n, j)
                if not early(n, 2):
                    turn_xn(n - 2, j % 2)
                if not early(n, 3):
                    make_logits(n - 3, (j + 1) % 2)
            for n in range(4):
                step(n, n)
            fours(pe, step, 4, GROUPS)
            turn_xn(GROUPS - 2, 0)
            make_logits(GROUPS - 3, 1)
            turn_xn(GROUPS - 1, 1)
            make_logits(GROUPS - 2, 0)
            make_logits(GROUPS - 1, 1)

            def rank_tokens():
                pe.wait_ge(ranked, 1)
                pe.matmul(ps[:, 6, 0:EXPERTS], lower[:, :], count[:, :], start=True, stop=True)
                pe.matmul(ps[:, 7, 0:EXPERTS], ones[:, 0:P], count[:, :], start=True, stop=True).then_inc(ranked, 1)

            pe.wait_ge(logit_copied, GROUPS)
            pe.wait_ge(w_lo_made, 2)

            def up(n, s, cs=range(IC)):
                pe.wait_ge(x_lo_made, n + 1)
                for c in cs:
                    if not (isinstance(n, int) and n == 0 and c < 2):
                        pe.wait_ge(hidden_made, n * IC + (c - 1))
                    for m in range(2):
                        for i, (w_part, x_part) in enumerate(((0, x_hi), (1, x_hi), (0, x_lo))):
                            last = pe.matmul(ps[:, 2 * m + c % 2, :], up_parts[:, m, w_part, c * P:(c + 1) * P],
                                             x_part[:, s, :], start=(i == 0), stop=(i == 2))
                        last.then_inc((gate_made, up_made)[m], 1)

            def down(n, s):
                pe.wait_ge(hidden_made, n * IC + IC)
                if not early(n):
                    pe.wait_ge(added, n - 1)
                for t in range(GROUP_TILES):
                    for c in range(IC):
                        last = pe.matmul(ps[:, 4 + s, t * DIM:(t + 1) * DIM],
                                         hidden_t[:, s, c * GTOK + t * P:c * GTOK + (t + 1) * P], w3s_s[:, c, :],
                                         start=(c == 0), stop=(c == IC - 1))
                last.then_inc(down_made, 1)
            up(0, 0, (0, 1))
            rank_tokens()
            up(0, 0, (2, 3))

            def shared(n, s):
                up(n, s)
                down(n - 1, 1 - s)
            shared(1, 1)
            pairs(pe, shared, 2, FRONT)
            down(FRONT - 1, 1)

            def turn_tile(k, s):
                pe.wait_ge(rx_loaded[s], round_of(k, s) * 16)
                if not early(k, 1):
                    pe.wait_ge(rx_lo_made, k)
                for t in range(2):
                    last = pe.transpose(ps[:, 6, t * P:(t + 1) * P], rx[:, s, t * DIM:(t + 1) * DIM], ident[:, :])
                last.then_inc(rx_turned, 1)

            def r_up(k, s, cs):
                for c in cs:
                    if c == 0:
                        pe.wait_ge(rx_lo_made, k + 1)
                        pe.wait_ge(rw_lo_made, k * 2 + 2)
                    if not (isinstance(k, int) and k == 0 and c < 2):
                        pe.wait_ge(r_hidden_made, k * IC + (c - 1))
                    for m in range(2):
                        for i, (w_part, x_part) in enumerate(((0, rx_hi), (1, rx_hi), (0, rx_lo))):
                            last = pe.matmul(ps[:, 2 * m + c % 2, 0:RTILE], r_up_parts[:, s, m, w_part, c * P:(c + 1) * P],
                                             x_part[:, s, :], start=(i == 0), stop=(i == 2))
                        last.then_inc((r_gate_made, r_up_made)[m], 1)

            def r_down(k, s, ts=(0, 1)):
                if ts[0] == 0:
                    pe.wait_ge(down_loaded[s], round_of(k, s) * 16)
                    pe.wait_ge(r_hidden_made, k * IC + IC)
                    if not early(k, 1):
                        pe.wait_ge(ry_copied, k)
                for t in ts:
                    for c in range(IC):
                        last = pe.matmul(ps[:, 4, t * DIM:(t + 1) * DIM],
                                         rhidden_t[:, s, c * RTILE + t * P:c * RTILE + (t + 1) * P],
                                         rw3[:, s, c * DIM:(c + 1) * DIM], start=(c == 0), stop=(c == IC - 1))
                if ts[-1] == 1:
                    last.then_inc(r_down_made, 1)

            pe.wait_ge(added, FRONT)
            turn_tile(0, 0)
            r_up(0, 0, range(IC))
            turn_tile(1, 1)

            def step(k, s, last=False):
                r_up(k, s, (0, 1))
                r_down(k - 1, 1 - s, (0,))
                if not last:
                    turn_tile(k + 1, 1 - s)
                r_up(k, s, (2, 3))
                r_down(k - 1, 1 - s, (1,))
            pairs(pe, step, 1, ROUTED_TILES - 2)
            step(ROUTED_TILES - 2, 1)
            step(ROUTED_TILES - 1, 0, last=True)
            r_down(ROUTED_TILES - 1, 0)

            pe.wait_ge(ry_copied, ROUTED_TILES)
            up(FRONT, 0)
            shared(FRONT + 1, 1)
            pairs(pe, shared, FRONT + 2, GROUPS)
            down(GROUPS - 1, 1)

        @block.vector
        def _(dve):
            dve.memset(eps_s[:, :], EPS).then_inc(eps_made, 1)
            dve.wait_ge(idents_made, 4)
            for hp in range(2):
                last = dve.tensor_reduce(parity[:, hp:hp + 1], ident[:, hp:P:2], AX, ALU.add)
            last.then_inc(sums_made, 1)
            dve.wait_ge(sums_made, 1)
            for h in range(QH):
                dve.tensor_scalar(sum_heads[:, h // 2, HEAD * h:HEAD * h + HEAD], ones[:, 0:HEAD], parity[:, h % 2:h % 2 + 1],
                                  None, ALU.mult).then_inc(sums_made, 1)

            def statistics(n, j, x_of, stats, mv):
                dve.memset(wait_word[:, 0:1], 0.0)
                for t in range(GROUP_TILES):
                    last = dve.bn_stats(ln_stats[:, j, t, :], x_of(t))
                last.then_inc(stats, 1)
                dve.wait_ge(stats, n + 1)
                dve.memset(wait_word[:, 1:2], 0.0)
                for t in range(GROUP_TILES):
                    last = dve.bn_aggr(ln_mv[:, j, t, :], ln_stats[:, j, t, :])
                last.then_inc(mv, 1)

            def inverse(n, j, std, rstd):
                dve.wait_ge(std, n + 1)
                dve.reciprocal(ln_rstd[:, j, :], ln_std[:, j, :]).then_inc(rstd, 1)

            def normalize(n, j, x_of, out_of, rstd, done):
                dve.wait_ge(rstd, n + 1)
                for t in range(GROUP_TILES):
                    last = dve.tensor_scalar(out_of(t), x_of(t), ln_mv[:, j, t, 0:1], ln_rstd[:, j, t:t + 1],
                                             ALU.subtract, ALU.mult)
                last.then_inc(done, 1)

            def stats_in(n, j):
                dve.wait_ge(in_loaded[j], round_of(n, j, 4) * 16)
                statistics(n, j, lambda t: x_in[:, j, t * DIM:(t + 1) * DIM], stats_done, mv_done)

            def norm_in(n, j):
                if not early(n):
                    dve.wait_ge(in_transposed, n - 1)
                normalize(n, j, lambda t: x_in[:, j, t * DIM:(t + 1) * DIM],
                          lambda t: xn[:, j % 2, t * DIM:(t + 1) * DIM], rstd_done, ln_done)

            def keep_q(n, s):
                dve.wait_ge(q_copied, n + 1)
                dve.tensor_copy(q_all[:, bass.ds(n * GTOK, GTOK)], q_out[:, s, :]).then_inc(q_kept, 1)

            def copy_v(n, s):
                if early(n, 1):
                    dve.wait_ge(qkv_weights_loaded, 16 * N_QKV_WEIGHTS)
                dve.wait_ge(v_projected, n + 1)
                if not early(n):
                    dve.wait_ge(kv_stored[s], round_of(n, s) * 32 - 32)
                dve.tensor_tensor(v_out[:, s, :].rearrange("p (t d) -> p t d", d=DIM),
                                  ps[:, 4, :].rearrange("p (t d) -> p t d", d=DIM),
                                  bv_s[:, :].rearrange("p (a d) -> p a d", a=1).to_broadcast([P, GROUP_TILES, DIM]),
                                  ALU.add).then_inc(v_copied, 1)

            def step(n, j, ahead=True):
                inverse(n, j, std_done, rstd_done)
                norm_in(n, j)
                if not early(n):
                    copy_v(n - 2, j % 2)
                if ahead:
                    stats_in(n + 2, (j + 2) % 4)
                if not early(n):
                    keep_q(n - 2, j % 2)
            stats_in(0, 0)
            stats_in(1, 1)
            for n in range(4):
                step(n, n)
            fours(dve, step, 4, GROUPS - 4)
            for n in range(GROUPS - 4, GROUPS):
                step(n, n % 4, ahead=n < GROUPS - 2)
            for n in range(GROUPS - 2, GROUPS):
                copy_v(n, n % 2)
                keep_q(n, n % 2)

            dve.wait_ge(rel_transposed, 1)
            dve.tensor_copy(rel_t[:, :], ps[:, 7, 0:NREL]).then_inc(rel_copied, 1)
            dve.wait_ge(rel_copied, 1)
            dve.tensor_reduce(head_of_quad[:, :], head_mask[:, :].rearrange("p (q h) -> p h q", h=QH), AX, ALU.add)
            dve.tensor_copy(rel_parts[:, 0, :], rel_t[:, :]).then_inc(rel_step, 1)
            dve.wait_ge(rel_step, 1)
            dve.tensor_tensor(rel_rest[:, :], rel_t[:, :], rel_parts[:, 0, :], ALU.subtract).then_inc(rel_step, 1)
            dve.wait_ge(rel_step, 2)
            dve.tensor_copy(rel_parts[:, 1, :], rel_rest[:, :]).then_inc(rel_step, 1)
            dve.wait_ge(rel_step, 3)
            dve.tensor_tensor(rel_parts[:, 2, :], rel_rest[:, :], rel_parts[:, 1, :], ALU.subtract).then_inc(rel_step, 1)
            dve.wait_ge(rel_step, 4)
            for a in range(2):
                for block in range(4):
                    rows = slice(QF * block, QF * block + QF)
                    last = dve.tensor_copy(rel_stacks[rows, a, :], rel_parts[rows, REL_PARTS[a][block], :])
            last.then_inc(rel_step, 1)
            dve.wait_ge(rel_step, 5)
            for a in range(2):
                for h in range(QH):
                    last = dve.tensor_scalar(rel_wins[a][:, h // 2, :, h % 2], rel_stacks[:, a, :], head_of_quad[:, h:h + 1],
                                             None, ALU.mult)
            last.then_inc(windows_made, 1)

            def expand_k(quad, n, s):
                dve.wait_ge(k_loaded[s], (quad * (GROUPS // 2) + round_of(n, s)) * 16)
                if not first_use(quad, n):
                    dve.wait_ge(scored, quad * GROUPS + n - 1)
                out = k_exp[:, s, :].rearrange("p (b r j h) -> p b r j h", r=2, j=SEQ, h=2)
                for h in range(2):
                    last = dve.tensor_scalar(out[:, :, h // 2, :, h % 2], k_g[:, s, :].rearrange("p (b j) -> p b j", j=SEQ),
                                             quad_mask[:, h:h + 1], None, ALU.mult)
                last.then_inc(k_expanded, 1)

            def shift(quad, n, s):
                g = quad * GROUPS + n
                scores = ps[:, 2 * s:2 * s + 2, :].rearrange("p k (r j h) -> p (k r) j h", j=SEQ, h=2)
                dve.wait_ge(scored, g + 1)
                dve.tensor_reduce(row_max[:, s, :, :], scores.rearrange("p r j h -> p r h j"), AX, ALU.max).then_inc(maxed, 1)
                dve.wait_ge(maxed, g + 1)
                if not first_use(quad, n):
                    dve.wait_ge(prob_turned, g - 1)
                dve.tensor_tensor(prob[:, s, :].rearrange("p (r j h) -> p r j h", j=SEQ, h=2), scores,
                                  row_max[:, s, :, :].rearrange("p r (a h) -> p r a h", a=1).to_broadcast(
                                      [P, GROUP_TILES * 2, SEQ, 2]), ALU.subtract).then_inc(shifted, 1)

            def norm(quad, n, s):
                g = quad * GROUPS + n
                dve.wait_ge(attended, g + 1)
                dve.reciprocal(den_r[:, s, :], ps[:, 6 + s, P:2 * P]).then_inc(den_inverted, 1)
                dve.wait_ge(den_inverted, g + 1)
                if not first_use(quad, n):
                    dve.wait_ge(attn_stored[s], (quad * (GROUPS // 2) + round_of(n, s)) * 16 - 16)
                dve.tensor_tensor(attn_o[:, s, :], ps[:, 6 + s, 0:P], den_r[:, s, :], ALU.mult).then_inc(normed, 1)

            def attend_quad(quad):
                follows = not isinstance(quad, int)
                if follows:
                    dve.wait_ge(k_expanded_act, quad * GROUPS)
                dve.tensor_copy(quad_mask[:, :], head_mask[:, bass.ds(quad * QH, QH)]).then_inc(mask_made, 1)
                if follows:
                    shift(quad - 1, GROUPS - 1, 1)
                else:
                    dve.wait_ge(mask_made, 1)
                for k in range(1, POS_BANKS, 2):
                    dve.wait_ge(pos_made, quad * POS_BANKS + (k + 1))
                    i = 4 * (k % (SEQ // 4))
                    dve.tensor_copy(
                        pos_t[:, k // (SEQ // 4), :].rearrange("p (b i) -> p i b", i=SEQ)[:, i:i + 4, :],
                        ps[:, k % 4, :].rearrange("p (i b) -> p i b", i=4)).then_inc(pos_copied_dve, 1)
                    if k == 3 and follows:
                        norm(quad - 1, GROUPS - 3, 1)
                    if k == 15:
                        expand_k(quad, 0, 0)
                    if k == 21:
                        expand_k(quad, 1, 1)
                if follows:
                    norm(quad - 1, GROUPS - 2, 0)
                    norm(quad - 1, GROUPS - 1, 1)
                shift(quad, 0, 0)
                expand_k(quad, 2, 0)
                shift(quad, 1, 1)

                def step(n, s):
                    expand_k(quad, n, s)
                    shift(quad, n - 1, 1 - s)
                    norm(quad, n - 3, 1 - s)
                step(3, 1)
                pairs(dve, step, 4, GROUPS)
            quads(dve, attend_quad)
            shift(QUADS - 1, GROUPS - 1, 1)
            for n in range(GROUPS - 3, GROUPS):
                norm(QUADS - 1, n, n % 2)

            for m, w in enumerate((w1s_s, w2s_s)):
                dve.wait_ge(w_hi_made, m + 1)
                dve.tensor_tensor(up_parts[:, m, 1, :], w[:, :], up_parts[:, m, 0, :].bitcast(F32),
                                  ALU.subtract).then_inc(w_lo_made, 1)

            def residual(n, j):
                s = j % 2
                dve.wait_ge(biased, n + 1)
                dve.wait_ge(o_projected, n + 1)
                dve.tensor_tensor(acc[:, bass.ds(n * GTOK, GTOK)], ps[:, s, :], xb[:, s, :], ALU.add).then_inc(x2_done, 1)
                dve.wait_ge(x2_done, n + 1)
                statistics(n, j, lambda t: acc[:, bass.ds(n * GTOK + t * DIM, DIM)], stats2, mv2)

            def norm2(n, j):
                if not early(n):
                    dve.wait_ge(xn3_turned, n - 1)
                    dve.wait_ge(xn3_kept, n - 1)
                normalize(n, j, lambda t: acc[:, bass.ds(n * GTOK + t * DIM, DIM)],
                          lambda t: xn3[:, j % 2, t * DIM:(t + 1) * DIM], rstd2, ln2)

            def keep_logits(n, s):
                dve.wait_ge(logit_made, n + 1)
                dve.tensor_copy(logits[:, bass.ds(n * GROUP_TILES, GROUP_TILES), :],
                                ps[:, 4 + s, :].rearrange("p (t e) -> p t e", t=GROUP_TILES)[:, :, 0:EXPERTS],
                                ).then_inc(logit_copied, 1)

            def step(n, j, ahead=True):
                inverse(n, j, std2, rstd2)
                norm2(n, j)
                if not early(n, 3):
                    keep_logits(n - 3, (j + 1) % 2)
                if ahead:
                    residual(n + 2, (j + 2) % 4)
            residual(0, 0)
            residual(1, 1)
            for n in range(4):
                step(n, n)
            fours(dve, step, 4, GROUPS - 4)
            for n in range(GROUPS - 4, GROUPS):
                step(n, n % 4, ahead=n < GROUPS - 2)
            for n in range(GROUPS - 3, GROUPS):
                keep_logits(n, n % 2)

            def split_x(n, s):
                rows = xn2_t[:, bass.ds(n * GTOK, GTOK)]
                if not early(n):
                    dve.wait_ge(up_made, (n - 1) * IC)
                dve.tensor_copy(x_hi[:, s, :], rows).then_inc(x_hi_made, 1)
                dve.wait_ge(x_hi_made, n + 1)
                dve.tensor_tensor(x_lo[:, s, :], rows, x_hi[:, s, :].bitcast(F32), ALU.subtract).then_inc(x_lo_made, 1)

            def hidden_chunk(n, s, c):
                dve.wait_ge(gated, n * IC + (c + 1))
                dve.wait_ge(up_made, n * IC + (c + 1))
                if c == 0 and not early(n):
                    dve.wait_ge(down_made, n - 1)
                dve.tensor_tensor(hidden_t[:, s, c * GTOK:(c + 1) * GTOK], ps[:, 2 + c % 2, :], gate[:, c % 2, :],
                                  ALU.mult).then_inc(hidden_made, 1)

            def hidden(n, s, last=False):
                for c in range(IC):
                    hidden_chunk(n, s, c)
                if not last:
                    split_x(n + 1, 1 - s)

            steps = [0]

            def then(ins):
                steps[0] += 1
                ins.then_inc(route_step, 1)
                if steps[0] in (9, 13):
                    hidden_chunk(0, 0, (steps[0] - 9) // 4)
                dve.wait_ge(route_step, steps[0])

            def over_experts(a):
                return a.rearrange("p (t e) -> p t e", e=1).to_broadcast([P, TILES, EXPERTS])

            dve.wait_ge(logit_copied, GROUPS)
            dve.wait_ge(idents_made, 10)
            split_x(0, 0)
            then(dve.tensor_reduce(best[:, :], logits, AX, ALU.max))
            then(dve.tensor_tensor(hit, logits, over_experts(best[:, :]), ALU.is_equal))
            down_b = expert_down[:, :].rearrange("p (t e) -> p t e", t=1).to_broadcast([P, TILES, EXPERTS])
            then(dve.tensor_tensor(hit, hit, down_b, ALU.mult))
            then(dve.tensor_reduce(rank[:, :], hit, AX, ALU.max))
            then(dve.tensor_tensor(chosen.rearrange("p e t -> p t e"), down_b, over_experts(rank[:, :]), ALU.is_equal))
            then(dve.tensor_reduce(count[:, :], chosen, AX, ALU.add))
            dve.sem_inc(ranked, 1)
            then(dve.tensor_tensor_scan(seen.rearrange("p e t -> p (e t)"), ones[:, :],
                                        chosen.rearrange("p e t -> p (e t)"), 0.0, ALU.mult, ALU.add))
            dve.wait_ge(ranked, 2)
            then(dve.tensor_tensor(starts_hit, ps[:, 7, 0:EXPERTS].rearrange("p (e k) -> p e k", k=1).to_broadcast(
                [P, EXPERTS, TOKENS // RTILE]), tile_starts[:, :].rearrange("p (e k) -> p e k", e=1).to_broadcast(
                [P, EXPERTS, TOKENS // RTILE]), ALU.is_gt))
            then(dve.tensor_reduce(n_tiles[:, :], starts_hit, AX, ALU.add))
            then(dve.tensor_tensor_scan(tiles_end[:, :], ones[:, 0:EXPERTS], n_tiles[:, :], 0.0, ALU.mult, ALU.add))
            then(dve.tensor_tensor(base[:, :], tiles_end[:, :], n_tiles[:, :], ALU.subtract))
            then(dve.scalar_tensor_tensor(out=base[:, :], in0=base[:, :], scalar=float(RTILE), in1=ps[:, 6, 0:EXPERTS],
                                          op0=ALU.mult, op1=ALU.add))
            then(dve.tensor_tensor(base[:, 1:EXPERTS], base[:, 1:EXPERTS], seen[:, 0:EXPERTS - 1, TILES - 1], ALU.subtract))
            then(dve.scalar_tensor_tensor(out=place, in0=seen, scalar=-1.0,
                                          in1=base[:, :].rearrange("p (e t) -> p e t", t=1).to_broadcast([P, EXPERTS, TILES]),
                                          op0=ALU.add, op1=ALU.add))
            then(dve.tensor_tensor(place, place, chosen, ALU.mult))
            then(dve.tensor_reduce(row_f[:, :], place.rearrange("p e t -> p t e"), AX, ALU.add))
            then(dve.tensor_copy(row_i[:, :], row_f[:, :]))
            dve.sem_inc(rows_made, 1)
            then(dve.tensor_tensor(tiles_hit, tiles_end[:, :].rearrange("p (k e) -> p k e", k=1).to_broadcast(
                [P, ROUTED_TILES, EXPERTS]), tile_numbers[:, :].rearrange("p (k e) -> p k e", e=1).to_broadcast(
                [P, ROUTED_TILES, EXPERTS]), ALU.is_le))
            then(dve.tensor_reduce(expert_f[:, :], tiles_hit, AX, ALU.add))
            then(dve.tensor_scalar(expert_f[:, :], expert_f[:, :], float(EXPERTS - 1), None, ALU.min))
            dve.tensor_copy(expert_i[:, :], expert_f[:, :]).then_inc(routed, 1)

            def low_w(k, s, m):
                dve.wait_ge(rw_hi_made, k * 2 + (m + 1))
                dve.tensor_tensor(r_up_parts[:, s, m, 1, :], (rw1, rw2)[m][:, s, :],
                                  r_up_parts[:, s, m, 0, :].bitcast(F32), ALU.subtract).then_inc(rw_lo_made, 1)

            def add_shared(n, s):
                dve.wait_ge(down_made, n + 1)
                rows = acc[:, bass.ds(n * GTOK, GTOK)]
                dve.tensor_tensor(rows, ps[:, 4 + s, :], rows, ALU.add).then_inc(added, 1)
            hidden_chunk(0, 0, 2)
            hidden_chunk(0, 0, 3)
            split_x(1, 1)
            hidden(1, 1)
            add_shared(0, 0)
            low_w(0, 0, 0)
            low_w(0, 0, 1)
            low_w(1, 1, 0)

            def step(n, s):
                hidden(n, s)
                add_shared(n - 1, 1 - s)
            pairs(dve, step, 2, FRONT)
            add_shared(FRONT - 1, 1)

            def low_rx(k, s):
                dve.wait_ge(rx_hi_made, k + 1)
                dve.tensor_tensor(rx_lo[:, s, :], ps[:, 6, 0:RTILE], rx_hi[:, s, :].bitcast(F32),
                                  ALU.subtract).then_inc(rx_lo_made, 1)

            def r_hidden(k, s):
                for c in range(IC):
                    dve.wait_ge(r_gated, k * IC + (c + 1))
                    dve.wait_ge(r_up_made, k * IC + (c + 1))
                    if c == 0 and not early(k):
                        dve.wait_ge(r_down_made, k - 1)
                    dve.tensor_tensor(rhidden_t[:, s, c * RTILE:(c + 1) * RTILE], ps[:, 2 + c % 2, 0:RTILE],
                                      gate[:, c % 2, 0:RTILE], ALU.mult).then_inc(r_hidden_made, 1)
                    if c == 1 and not (isinstance(k, int) and k == ROUTED_TILES - 1):
                        low_w(k + 1, 1 - s, 1)
                        low_rx(k + 1, 1 - s)
                if not (isinstance(k, int) and k >= ROUTED_TILES - 2):
                    low_w(k + 2, s, 0)

            def copy_y(k, s):
                dve.wait_ge(r_down_made, k + 1)
                if not early(k):
                    dve.wait_ge(ry_stored[s], round_of(k, s) * 16 - 16)
                dve.tensor_copy(ry[:, s, :], ps[:, 4, 0:RTILE]).then_inc(ry_copied, 1)

            def step(k, s):
                r_hidden(k, s)
                copy_y(k - 1, 1 - s)
            low_rx(0, 0)
            r_hidden(0, 0)
            step(1, 1)
            step(2, 0)
            pairs(dve, step, 3, ROUTED_TILES - 2)
            step(ROUTED_TILES - 2, 1)
            step(ROUTED_TILES - 1, 0)
            copy_y(ROUTED_TILES - 1, 0)

            def add_routed(n, s):
                dve.wait_ge(added, n + 1)
                dve.wait_ge(y_gathered[s], round_of(n, s, 4) * (16 * GROUP_TILES))
                rows = acc[:, bass.ds(n * GTOK, GTOK)]
                dve.tensor_tensor(rows, rows, y_in[:, s, :], ALU.add).then_inc(summed, 1)

            def step(n, s, last=False):
                hidden(n, s, last)
                for k in range(2):
                    if not early(n, FRONT + 2) or k == 1:
                        add_routed(n * 2 - (2 * FRONT + 3 - k), (2 * s + 1 + k) % 4)
                add_shared(n - 1, 1 - s)
            split_x(FRONT + 1, 1)
            hidden(FRONT, 0, last=True)
            step(FRONT + 1, 1)
            pairs(dve, step, FRONT + 2, GROUPS - 2)
            step(GROUPS - 2, 0)
            step(GROUPS - 1, 1, last=True)
            add_shared(GROUPS - 1, 1)
            for n in range(GROUPS - 3, GROUPS):
                add_routed(n, n % 4)


_INS = ['x', 'ctx_1024', 'L0_xattn_wq', 'L0_xattn_bq', 'L0_xattn_wk', 'L0_xattn_bk', 'L0_xattn_wv', 'L0_xattn_bv',
        'L0_xattn_wo', 'L0_xattn_bo', 'L0_xattn_rel_emb', 'L0_ffn_w1s', 'L0_ffn_w2s', 'L0_ffn_w3s', 'L0_ffn_W1',
        'L0_ffn_W2', 'L0_ffn_W3', 'L0_ffn_Wg']
_OUTS = [((BATCHES, SEQ, DIM), 'float32')]


def kernel(**inputs):
    import numpy as _np
    import concourse.bacc as _bacc
    from concourse import mybir as _mybir
    from concourse.bass_utils import run_bass_kernel_spmd as _run

    nc = _bacc.Bacc("TRN2", target_bir_lowering=False, num_devices=1)
    arrays, args = {}, []
    for name in _INS:
        a = _np.ascontiguousarray(inputs[name])
        arrays[f"in_{name}_dram"] = a
        args.append(nc.dram_tensor(f"in_{name}_dram", a.shape, _mybir.dt.from_np(a.dtype), kind="ExternalInput").ap())
    for i, (shape, dtype) in enumerate(_OUTS):
        dt = _mybir.dt.from_np(_np.dtype(dtype))
        args.append(nc.dram_tensor(f"out_{i}_dram", shape, dt, kind="ExternalOutput").ap())
    xattn_moe(nc, *args)
    r = _run(nc, [arrays], core_ids=[0])
    got = tuple(r.results[0][f"out_{i}_dram"] for i in range(len(_OUTS)))
    return got[0]
```
